# Optimizing a Trainium2 kernel written in Bass

```python
import numpy as np
import jax
import jax.numpy as jnp

def _softmax(x, axis=-1):
    return jax.nn.softmax(x, axis=axis)

def _gelu(x):
    return jax.nn.gelu(x, approximate=True)

def _silu(x):
    return jax.nn.silu(x)

def _sigmoid(x):
    return jax.nn.sigmoid(x)

def _layernorm(x, axis=-1, eps=1e-05):
    m = jnp.mean(x, axis=axis, keepdims=True)
    v = jnp.var(x, axis=axis, keepdims=True)
    return (x - m) / jnp.sqrt(v + eps)

def _scatter_add(tgt, idx, src, axis=0):
    return tgt.at[idx].add(src)

def _segment_sum(src, seg, n):
    return jax.ops.segment_sum(src, seg, n)
kernel_name = 'mk_flamingo_gated_d2_seqx_r8_8f09aa'

def setup_inputs(seed: int=0):
    np.random.seed(seed)
    _w = jnp.asarray

    def _rec_inputs():
        import jax
        import jax.numpy as jnp
        _rk = jax.random.key(seed)
        x = 7.22e-05 + 1 * jax.random.normal(jax.random.fold_in(_rk, 1), (1, 1024, 128), jnp.float32)
        _lenS = 1024 - jax.random.randint(jax.random.fold_in(_rk, 7), (1,), 0, max(1, 1024 // 4) + 1, jnp.int32)
        _lenS2 = 6404 - jax.random.randint(jax.random.fold_in(_rk, 8), (1,), 0, max(1, 6404 // 4) + 1, jnp.int32)
        _ctx_768P = jax.random.normal(jax.random.fold_in(_rk, 11), (1, 16, 96), jnp.float32)
        _ctx_768c = jax.random.dirichlet(jax.random.fold_in(_rk, 511), 0.3 * jnp.ones((16,), jnp.float32), (1, 6404))
        _ctx_768t = jnp.einsum('bsk,bkd->bsd', _ctx_768c, _ctx_768P)
        _ctx_768t = _ctx_768t * jax.lax.rsqrt(jnp.mean(jnp.square(_ctx_768t)) + 1e-12) * 0.953939
        ctx_768 = 3.88148e-05 + 0.999967 * (_ctx_768t + 0.3 * jax.random.normal(jax.random.fold_in(_rk, 611), (1, 6404, 96), jnp.float32))
        _validS = jnp.arange(1024)[None, :] < _lenS[:, None]
        _validS2 = jnp.arange(6404)[None, :] < _lenS2[:, None]
        _causal = jnp.tril(jnp.ones((1024, 1024), dtype=bool))
        mask_BxS_bf1 = jnp.ones((1, 1024), dtype=bool)
        mask_BxS2_bf1 = jnp.ones((1, 6404), dtype=bool)
        _g = jax.random.normal(jax.random.fold_in(_rk, 9001), (2, 2), jnp.float32)
        _g = jnp.sign(_g) * jnp.maximum(jnp.abs(_g), 1.0) + (_g == 0) * 1.0
        g_xattn = _g[0]
        g_ffn = _g[1]
        return (x, ctx_768, mask_BxS_bf1, mask_BxS2_bf1, g_xattn, g_ffn)
    x, ctx_768, mask_BxS_bf1, mask_BxS2_bf1, g_xattn, g_ffn = _rec_inputs()

    def _L0_xattn_setup():
        import jax, jax.numpy as jnp
        import numpy as np
        B, T, DT, G, DV = (16, 64, 128, 72, 96)
        H, DH = (4, 32)
        INNER = H * DH
        HID = 4 * DT
        N_STATE = 64
        K_TOP = 32

        def layernorm(x, g, b, eps=1e-05):
            m = x.mean(-1, keepdims=True)
            v = x.var(-1, keepdims=True)
            return (x - m) * jax.lax.rsqrt(v + eps) * g + b

        def s4d(x, log_dt, A_re, A_im, C_re, C_im, D_skip):
            Bb, L, D = x.shape
            dt = jnp.exp(log_dt)
            A = A_re + 1j * A_im
            C = C_re + 1j * C_im
            dtA = dt[:, None] * A
            dC = C * (jnp.exp(dtA) - 1.0) / A
            powers = jnp.exp(dtA[:, :, None] * jnp.arange(L))
            K = 2.0 * jnp.einsum('dn,dnl->dl', dC, powers).real
            n = 2 * L
            Kf = jnp.fft.rfft(K, n=n, axis=-1)
            xf = jnp.fft.rfft(x, n=n, axis=1)
            y = jnp.fft.irfft(xf * Kf.T[None], n=n, axis=1)[:, :L]
            return y + x * D_skip
        key = jax.random.key(seed)
        ks = jax.random.split(key, 16)
        s = 0.02
        inp = {'x_text': jax.random.normal(ks[0], (B, T, DT), jnp.float32), 'x_vision': jax.random.normal(ks[1], (B, G, DV), jnp.float32), 'text_mask': jnp.ones((B, T), bool), 'vision_mask': jnp.ones((B, G), bool), 'Wq': jax.random.normal(ks[2], (DT, INNER), jnp.float32) * s, 'Wk': jax.random.normal(ks[3], (DV, INNER), jnp.float32) * s, 'Wv': jax.random.normal(ks[4], (DV, DT), jnp.float32) * s, 'W_film_in': jax.random.normal(ks[5], (DT, 2 * DT), jnp.float32) * s, 'b_film_in': jnp.zeros((2 * DT,), jnp.float32), 'W_film_out': jax.random.normal(ks[6], (DT, 2 * DT), jnp.float32) * s, 'b_film_out': jnp.zeros((2 * DT,), jnp.float32), 'g_norm_in': jnp.ones((DT,), jnp.float32), 'b_norm_in': jnp.zeros((DT,), jnp.float32), 'g_norm_out': jnp.ones((DT,), jnp.float32), 'b_norm_out': jnp.zeros((DT,), jnp.float32), 'g_ffn': jnp.ones((DT,), jnp.float32), 'b_ffn': jnp.zeros((DT,), jnp.float32), 'W1': jax.random.normal(ks[7], (DT, HID), jnp.float32) * s, 'b1': jnp.zeros((HID,), jnp.float32), 'W2': jax.random.normal(ks[8], (HID, DT), jnp.float32) * s, 'b2': jnp.zeros((DT,), jnp.float32), 'log_dt': jnp.log(0.001) + jax.random.uniform(ks[9], (DT,), jnp.float32) * (jnp.log(0.1) - jnp.log(0.001)), 'A_re': -0.5 * jnp.ones((DT, N_STATE), jnp.float32), 'A_im': jnp.tile(jnp.pi * jnp.arange(N_STATE, dtype=jnp.float32), (DT, 1)), 'C_re': jax.random.normal(ks[10], (DT, N_STATE), jnp.float32) * 0.5 ** 0.5, 'C_im': jax.random.normal(ks[11], (DT, N_STATE), jnp.float32) * 0.5 ** 0.5, 'D_skip': jax.random.normal(ks[12], (DT,), jnp.float32), 'mod_gate': jnp.array(0.5, jnp.float32)}
        return inp
    _L0_xattn_all = _L0_xattn_setup()
    _L0_xattn_in = {k: v for k, v in _L0_xattn_all.items() if k in ('Wq', 'Wk', 'Wv', 'W_film_in', 'b_film_in', 'W_film_out', 'b_film_out', 'g_norm_in', 'b_norm_in', 'g_norm_out', 'b_norm_out', 'g_ffn', 'b_ffn', 'W1', 'b1', 'W2', 'b2', 'log_dt', 'A_re', 'A_im', 'C_re', 'C_im', 'D_skip', 'mod_gate')}
    del _L0_xattn_all

    def _L0_ffn_setup():
        import jax, jax.numpy as jnp
        import numpy as np
        D_MODEL, D_FF, RANK = (128, 512, 32)
        B, S = (4, 512)
        key = jax.random.key(seed)
        ks = jax.random.split(key, 7)
        return {'x': jax.random.normal(ks[0], (B, S, D_MODEL), dtype=jnp.float32), 'U1': jax.random.normal(ks[1], (D_MODEL, RANK), dtype=jnp.float32) * 0.02, 'V1': jax.random.normal(ks[2], (RANK, D_FF), dtype=jnp.float32) * 0.02, 'b1': jnp.zeros((D_FF,), dtype=jnp.float32), 'U2': jax.random.normal(ks[3], (D_FF, RANK), dtype=jnp.float32) * 0.02, 'V2': jax.random.normal(ks[4], (RANK, D_MODEL), dtype=jnp.float32) * 0.02, 'b2': jnp.zeros((D_MODEL,), dtype=jnp.float32)}
    _L0_ffn_all = _L0_ffn_setup()
    _L0_ffn_in = {k: v for k, v in _L0_ffn_all.items() if k in ('U1', 'V1', 'b1', 'U2', 'V2', 'b2')}
    del _L0_ffn_all

    def _L1_xattn_setup():
        import jax, jax.numpy as jnp
        import numpy as np
        N_HEADS = 16
        DIM_EMBED = 128
        DIM_CROSS = 96
        DIM_HEAD = DIM_EMBED // N_HEADS
        key = jax.random.key(seed)
        ks = jax.random.split(key, 10)
        B, Sq, Sk = (8, 512, 77)
        s_e = 1.0 / np.sqrt(DIM_EMBED)
        s_c = 1.0 / np.sqrt(DIM_CROSS)
        return {'x': jax.random.normal(ks[0], (B, Sq, DIM_EMBED), jnp.float32), 'y': jax.random.normal(ks[1], (B, Sk, DIM_CROSS), jnp.float32), 'wq': jax.random.normal(ks[2], (DIM_EMBED, DIM_EMBED), jnp.float32) * s_e, 'bq': jax.random.normal(ks[3], (DIM_EMBED,), jnp.float32) * 0.01, 'wk': jax.random.normal(ks[4], (DIM_CROSS, DIM_EMBED), jnp.float32) * s_c, 'bk': jax.random.normal(ks[5], (DIM_EMBED,), jnp.float32) * 0.01, 'wv': jax.random.normal(ks[6], (DIM_CROSS, DIM_EMBED), jnp.float32) * s_c, 'bv': jax.random.normal(ks[7], (DIM_EMBED,), jnp.float32) * 0.01, 'wo': jax.random.normal(ks[8], (DIM_EMBED, DIM_EMBED), jnp.float32) * s_e, 'bo': jax.random.normal(ks[9], (DIM_EMBED,), jnp.float32) * 0.01}
    _L1_xattn_all = _L1_xattn_setup()
    _L1_xattn_in = {k: v for k, v in _L1_xattn_all.items() if k in ('wq', 'bq', 'wk', 'bk', 'wv', 'bv', 'wo', 'bo')}
    del _L1_xattn_all

    def _L1_ffn_setup():
        import jax, jax.numpy as jnp
        import numpy as np
        TOP_K = 2
        TEMP = 0.9
        EPS = 1e-05
        B, S, D, F, E = (2, 256, 128, 512, 8)

        def _moe_forward(x, gate_w, gate_b, w1, b1, w2, b2, ln_g, ln_b):
            logits = (x @ gate_w + gate_b) / TEMP
            topk_vals, topk_idx = jax.lax.top_k(logits, TOP_K)
            keep = jax.nn.one_hot(topk_idx, E, dtype=jnp.bool_).any(-2)
            masked = jnp.where(keep, logits, -jnp.inf)
            gate_probs = jax.nn.softmax(masked, axis=-1)
            h = jnp.einsum('bsd,edf->bsef', x, w1) + b1
            h = jax.nn.gelu(h, approximate=False)
            expert_out = jnp.einsum('bsef,efd->bsed', h, w2) + b2
            out = jnp.einsum('bse,bsed->bsd', gate_probs, expert_out)
            mu = out.mean(-1, keepdims=True)
            var = out.var(-1, keepdims=True)
            out = (out - mu) / jnp.sqrt(var + EPS) * ln_g + ln_b
            return out
        key = jax.random.key(seed)
        ks = jax.random.split(key, 4)
        scale_in = 1.0 / np.sqrt(D)
        scale_ff = 1.0 / np.sqrt(F)
        return {'x': jax.random.normal(ks[0], (B, S, D), jnp.float32), 'gate_w': jax.random.normal(ks[1], (D, E), jnp.float32) * scale_in, 'gate_b': jnp.zeros((E,), jnp.float32), 'w1': jax.random.normal(ks[2], (E, D, F), jnp.float32) * scale_in, 'b1': jnp.zeros((E, F), jnp.float32), 'w2': jax.random.normal(ks[3], (E, F, D), jnp.float32) * scale_ff, 'b2': jnp.zeros((E, D), jnp.float32), 'ln_g': jnp.ones((D,), jnp.float32), 'ln_b': jnp.zeros((D,), jnp.float32)}
    _L1_ffn_all = _L1_ffn_setup()
    _L1_ffn_in = {k: v for k, v in _L1_ffn_all.items() if k in ('gate_w', 'gate_b', 'w1', 'b1', 'w2', 'b2', 'ln_g', 'ln_b')}
    del _L1_ffn_all
    return {'x': x, 'ctx_768': ctx_768, 'mask_BxS_bf1': mask_BxS_bf1, 'mask_BxS2_bf1': mask_BxS2_bf1, 'g_xattn': g_xattn, 'g_ffn': g_ffn, 'L0_xattn_Wq': _L0_xattn_in['Wq'], 'L0_xattn_Wk': _L0_xattn_in['Wk'], 'L0_xattn_Wv': _L0_xattn_in['Wv'], 'L0_xattn_W_film_in': _L0_xattn_in['W_film_in'], 'L0_xattn_b_film_in': _L0_xattn_in['b_film_in'], 'L0_xattn_W_film_out': _L0_xattn_in['W_film_out'], 'L0_xattn_b_film_out': _L0_xattn_in['b_film_out'], 'L0_xattn_g_norm_in': _L0_xattn_in['g_norm_in'], 'L0_xattn_b_norm_in': _L0_xattn_in['b_norm_in'], 'L0_xattn_g_norm_out': _L0_xattn_in['g_norm_out'], 'L0_xattn_b_norm_out': _L0_xattn_in['b_norm_out'], 'L0_xattn_g_ffn': _L0_xattn_in['g_ffn'], 'L0_xattn_b_ffn': _L0_xattn_in['b_ffn'], 'L0_xattn_W1': _L0_xattn_in['W1'], 'L0_xattn_b1': _L0_xattn_in['b1'], 'L0_xattn_W2': _L0_xattn_in['W2'], 'L0_xattn_b2': _L0_xattn_in['b2'], 'L0_xattn_log_dt': _L0_xattn_in['log_dt'], 'L0_xattn_A_re': _L0_xattn_in['A_re'], 'L0_xattn_A_im': _L0_xattn_in['A_im'], 'L0_xattn_C_re': _L0_xattn_in['C_re'], 'L0_xattn_C_im': _L0_xattn_in['C_im'], 'L0_xattn_D_skip': _L0_xattn_in['D_skip'], 'L0_xattn_mod_gate': _L0_xattn_in['mod_gate'], 'L0_ffn_U1': _L0_ffn_in['U1'], 'L0_ffn_V1': _L0_ffn_in['V1'], 'L0_ffn_b1': _L0_ffn_in['b1'], 'L0_ffn_U2': _L0_ffn_in['U2'], 'L0_ffn_V2': _L0_ffn_in['V2'], 'L0_ffn_b2': _L0_ffn_in['b2'], 'L1_xattn_wq': _L1_xattn_in['wq'], 'L1_xattn_bq': _L1_xattn_in['bq'], 'L1_xattn_wk': _L1_xattn_in['wk'], 'L1_xattn_bk': _L1_xattn_in['bk'], 'L1_xattn_wv': _L1_xattn_in['wv'], 'L1_xattn_bv': _L1_xattn_in['bv'], 'L1_xattn_wo': _L1_xattn_in['wo'], 'L1_xattn_bo': _L1_xattn_in['bo'], 'L1_ffn_gate_w': _L1_ffn_in['gate_w'], 'L1_ffn_gate_b': _L1_ffn_in['gate_b'], 'L1_ffn_w1': _L1_ffn_in['w1'], 'L1_ffn_b1': _L1_ffn_in['b1'], 'L1_ffn_w2': _L1_ffn_in['w2'], 'L1_ffn_b2': _L1_ffn_in['b2'], 'L1_ffn_ln_g': _L1_ffn_in['ln_g'], 'L1_ffn_ln_b': _L1_ffn_in['ln_b']}

def reference(x, ctx_768, mask_BxS_bf1, mask_BxS2_bf1, g_xattn, g_ffn, L0_xattn_Wq, L0_xattn_Wk, L0_xattn_Wv, L0_xattn_W_film_in, L0_xattn_b_film_in, L0_xattn_W_film_out, L0_xattn_b_film_out, L0_xattn_g_norm_in, L0_xattn_b_norm_in, L0_xattn_g_norm_out, L0_xattn_b_norm_out, L0_xattn_g_ffn, L0_xattn_b_ffn, L0_xattn_W1, L0_xattn_b1, L0_xattn_W2, L0_xattn_b2, L0_xattn_log_dt, L0_xattn_A_re, L0_xattn_A_im, L0_xattn_C_re, L0_xattn_C_im, L0_xattn_D_skip, L0_xattn_mod_gate, L0_ffn_U1, L0_ffn_V1, L0_ffn_b1, L0_ffn_U2, L0_ffn_V2, L0_ffn_b2, L1_xattn_wq, L1_xattn_bq, L1_xattn_wk, L1_xattn_bk, L1_xattn_wv, L1_xattn_bv, L1_xattn_wo, L1_xattn_bo, L1_ffn_gate_w, L1_ffn_gate_b, L1_ffn_w1, L1_ffn_b1, L1_ffn_w2, L1_ffn_b2, L1_ffn_ln_g, L1_ffn_ln_b):
    import jax
    import jax.numpy as jnp

    def _L0_xattn_ref(x_text, x_vision, text_mask, vision_mask, Wq, Wk, Wv, W_film_in, b_film_in, W_film_out, b_film_out, g_norm_in, b_norm_in, g_norm_out, b_norm_out, g_ffn, b_ffn, W1, b1, W2, b2, log_dt, A_re, A_im, C_re, C_im, D_skip, mod_gate):
        import jax, jax.numpy as jnp
        import numpy as np
        B, T, DT, G, DV = (16, 64, 128, 72, 96)
        H, DH = (4, 32)
        INNER = H * DH
        HID = 4 * DT
        N_STATE = 64
        K_TOP = 32

        def layernorm(x, g, b, eps=1e-05):
            m = x.mean(-1, keepdims=True)
            v = x.var(-1, keepdims=True)
            return (x - m) * jax.lax.rsqrt(v + eps) * g + b

        def s4d(x, log_dt, A_re, A_im, C_re, C_im, D_skip):
            Bb, L, D = x.shape
            dt = jnp.exp(log_dt)
            A = A_re + 1j * A_im
            C = C_re + 1j * C_im
            dtA = dt[:, None] * A
            dC = C * (jnp.exp(dtA) - 1.0) / A
            powers = jnp.exp(dtA[:, :, None] * jnp.arange(L))
            K = 2.0 * jnp.einsum('dn,dnl->dl', dC, powers).real
            n = 2 * L
            Kf = jnp.fft.rfft(K, n=n, axis=-1)
            xf = jnp.fft.rfft(x, n=n, axis=1)
            y = jnp.fft.irfft(xf * Kf.T[None], n=n, axis=1)[:, :L]
            return y + x * D_skip
        Bb, Tt, D = x_text.shape
        Gg = x_vision.shape[1]
        Q = (x_text @ Wq).reshape(Bb, Tt, H, DH)
        K = (x_vision @ Wk).reshape(Bb, Gg, H, DH)
        scores = jnp.einsum('bthd,bghd->bhtg', Q, K) / np.sqrt(DH).astype(np.float32)
        scores = jnp.where(vision_mask[:, None, None, :], scores, -jnp.inf)
        topv, topi = jax.lax.top_k(scores, K_TOP)
        probs = jax.nn.softmax(topv, axis=-1)
        bi = jnp.arange(Bb)[:, None, None, None]
        hi = jnp.arange(H)[None, :, None, None]
        ti = jnp.arange(Tt)[None, None, :, None]
        attn = jnp.zeros_like(scores).at[bi, hi, ti, topi].set(probs)
        attn_mean = attn.mean(axis=1)
        V = x_vision @ Wv
        c_t = jnp.einsum('btg,bgd->btd', attn_mean, V)
        c_t = c_t * text_mask[..., None]
        x = layernorm(x_text, g_norm_in, b_norm_in)
        scale_in, shift_in = jnp.split(c_t @ W_film_in + b_film_in, 2, axis=-1)
        x = x * (1.0 + mod_gate * scale_in) + mod_gate * shift_in
        y = s4d(x, log_dt, A_re, A_im, C_re, C_im, D_skip)
        scale_out, shift_out = jnp.split(c_t @ W_film_out + b_film_out, 2, axis=-1)
        y = y * (1.0 + mod_gate * scale_out) + mod_gate * shift_out
        xt = x_text + y
        h = layernorm(xt, g_ffn, b_ffn)
        h = jax.nn.gelu(h @ W1 + b1, approximate=False) @ W2 + b2
        xt = xt + h
        return layernorm(xt, g_norm_out, b_norm_out)

    def _L0_ffn_ref(x, U1, V1, b1, U2, V2, b2):
        import jax, jax.numpy as jnp
        import numpy as np
        D_MODEL, D_FF, RANK = (128, 512, 32)
        B, S = (4, 512)
        P = jnp.einsum('bsd,dr->bsr', x, U1)
        H = jax.nn.gelu(jnp.einsum('bsr,rf->bsf', P, V1) + b1)
        Q = jnp.einsum('bsf,fr->bsr', H, U2)
        return jnp.einsum('bsr,rd->bsd', Q, V2) + b2

    def _L1_xattn_ref(x, y, wq, bq, wk, bk, wv, bv, wo, bo):
        import jax, jax.numpy as jnp
        import numpy as np
        N_HEADS = 16
        DIM_EMBED = 128
        DIM_CROSS = 96
        DIM_HEAD = DIM_EMBED // N_HEADS
        B, Sq, E = x.shape
        H, D = (N_HEADS, DIM_HEAD)
        q = (x @ wq + bq).reshape(B, Sq, H, D).transpose(0, 2, 1, 3)
        k = (y @ wk + bk).reshape(B, -1, H, D).transpose(0, 2, 1, 3)
        v = (y @ wv + bv).reshape(B, -1, H, D).transpose(0, 2, 1, 3)
        scores = jnp.einsum('bhqd,bhkd->bhqk', q, k) / jnp.sqrt(jnp.asarray(D, x.dtype))
        attn = jax.nn.softmax(scores, axis=-1)
        out = jnp.einsum('bhqk,bhkd->bhqd', attn, v)
        out = out.transpose(0, 2, 1, 3).reshape(B, Sq, E)
        return out @ wo + bo

    def _L1_ffn_ref(x, gate_w, gate_b, w1, b1, w2, b2, ln_g, ln_b):
        import jax, jax.numpy as jnp
        import numpy as np
        TOP_K = 2
        TEMP = 0.9
        EPS = 1e-05
        B, S, D, F, E = (2, 256, 128, 512, 8)

        def _moe_forward(x, gate_w, gate_b, w1, b1, w2, b2, ln_g, ln_b):
            logits = (x @ gate_w + gate_b) / TEMP
            topk_vals, topk_idx = jax.lax.top_k(logits, TOP_K)
            keep = jax.nn.one_hot(topk_idx, E, dtype=jnp.bool_).any(-2)
            masked = jnp.where(keep, logits, -jnp.inf)
            gate_probs = jax.nn.softmax(masked, axis=-1)
            h = jnp.einsum('bsd,edf->bsef', x, w1) + b1
            h = jax.nn.gelu(h, approximate=False)
            expert_out = jnp.einsum('bsef,efd->bsed', h, w2) + b2
            out = jnp.einsum('bse,bsed->bsd', gate_probs, expert_out)
            mu = out.mean(-1, keepdims=True)
            var = out.var(-1, keepdims=True)
            out = (out - mu) / jnp.sqrt(var + EPS) * ln_g + ln_b
            return out
        return _moe_forward(x, gate_w, gate_b, w1, b1, w2, b2, ln_g, ln_b)
    x = x + jnp.tanh(g_xattn[0]) * _L0_xattn_ref(_layernorm(x, axis=-1), ctx_768, mask_BxS_bf1, mask_BxS2_bf1, L0_xattn_Wq, L0_xattn_Wk, L0_xattn_Wv, L0_xattn_W_film_in, L0_xattn_b_film_in, L0_xattn_W_film_out, L0_xattn_b_film_out, L0_xattn_g_norm_in, L0_xattn_b_norm_in, L0_xattn_g_norm_out, L0_xattn_b_norm_out, L0_xattn_g_ffn, L0_xattn_b_ffn, L0_xattn_W1, L0_xattn_b1, L0_xattn_W2, L0_xattn_b2, L0_xattn_log_dt, L0_xattn_A_re, L0_xattn_A_im, L0_xattn_C_re, L0_xattn_C_im, L0_xattn_D_skip, L0_xattn_mod_gate)
    x = x + jnp.tanh(g_ffn[0]) * _L0_ffn_ref(_layernorm(x, axis=-1), L0_ffn_U1, L0_ffn_V1, L0_ffn_b1, L0_ffn_U2, L0_ffn_V2, L0_ffn_b2)
    x = x + jnp.tanh(g_xattn[1]) * _L1_xattn_ref(_layernorm(x, axis=-1), ctx_768, L1_xattn_wq, L1_xattn_bq, L1_xattn_wk, L1_xattn_bk, L1_xattn_wv, L1_xattn_bv, L1_xattn_wo, L1_xattn_bo)
    x = x + jnp.tanh(g_ffn[1]) * _L1_ffn_ref(_layernorm(x, axis=-1), L1_ffn_gate_w, L1_ffn_gate_b, L1_ffn_w1, L1_ffn_b1, L1_ffn_w2, L1_ffn_b2, L1_ffn_ln_g, L1_ffn_ln_b)
    return x

_drawn_inputs = setup_inputs


def setup_inputs(seed=0):
    import zlib

    import numpy as np

    out = dict(_drawn_inputs(seed))
    spreads = {'g_ffn': (-1.0, 0.2),
     'L0_xattn_b_film_in': (0.0, 0.1),
     'L0_xattn_b_film_out': (0.0, 0.1),
     'L0_xattn_g_norm_in': (1.0, 0.2),
     'L0_xattn_b_norm_in': (0.0, 0.1),
     'L0_xattn_g_norm_out': (1.0, 0.2),
     'L0_xattn_b_norm_out': (0.0, 0.1),
     'L0_xattn_g_ffn': (1.0, 0.6),
     'L0_xattn_b_ffn': (0.0, 2.0),
     'L0_xattn_b1': (0.0, 0.341),
     'L0_xattn_b2': (0.0, 0.1),
     'L0_xattn_A_re': (-0.5, 0.2),
     'L0_ffn_b1': (0.0, 0.636),
     'L0_ffn_b2': (0.0, 0.1),
     'L1_ffn_gate_b': (0.0, 0.1),
     'L1_ffn_b1': (0.0, 0.1),
     'L1_ffn_b2': (0.0, 0.1),
     'L1_ffn_ln_g': (1.0, 0.2),
     'L1_ffn_ln_b': (0.0, 0.1)}
    factors = {'L0_xattn_Wq': 8.887,
     'L0_xattn_Wk': 2.945,
     'L0_ffn_U1': 8.0,
     'L0_ffn_V1': 5.469,
     'L0_ffn_U2': 4.447,
     'L0_ffn_V2': 4.661,
     'L1_xattn_bq': 8.0,
     'L1_xattn_bk': 64.0,
     'L1_xattn_bv': 2.891}
    for name, (base, spread) in spreads.items():
        noise = np.random.default_rng([zlib.crc32(name.encode()), seed]).standard_normal(out[name].shape)
        drawn = base * np.exp(spread * noise) if base else spread * noise
        out[name] = jnp.asarray(drawn.astype(out[name].dtype))
    for name, factor in factors.items():
        out[name] = (out[name] * factor).astype(out[name].dtype)
    return out
```

```python
import numpy as np
import concourse.bass as bass
from concourse import mybir
from contextlib import ExitStack

F32 = mybir.dt.float32
BF16 = mybir.dt.bfloat16
U8 = mybir.dt.uint8
U32 = mybir.dt.uint32
I32 = mybir.dt.int32
ALU = mybir.AluOpType
ACT = mybir.ActivationFunctionType
AX = mybir.AxisListType

P = 128
T = 1024
NT = T // P
TB = 512
NB = T // TB
D = 128
DC = 96
G = 6404
NG = -(-G // P)
GP = NG * P
GROUP = 512
NGROUP = -(-GP // GROUP)
H0, DH0, TOPK = 4, 32, 32
H1, DH1 = 16, 8
VW = DH1 + 1
NS = 64
KTAP = 32
HID = 512
RANK = 32
E = 8
LEVELS = 3
PIECE = 128
NPIECE = GP // PIECE
NCAND = NPIECE * 8
UNROLL = 3
TURNS = NG // UNROLL
MASKED = -1.0e30
LOWEST = -3.0e38
EXP_RANGE = 60.0
LN_EPS = 1e-5
ROUND = 12582912.0
assert GP == NG * P and NG % UNROLL == 0


SPARE = []


def take_wait(eng, spare=SPARE):
    eng.sem_inc(spare[0], 1)


def take_part(eng, spare=SPARE):
    eng.sem_inc(spare[0], 1)


class Chain:

    def __init__(self, eng, sem):
        self.eng, self.sem, self.n, self.turn = eng, sem, 0, 0

    def __call__(self, ins, before_max=False):
        ins.then_inc(self.sem, 1)
        self.n += 1
        self.eng.wait_ge(self.sem, self.turn + self.n)
        if before_max:
            take_wait(self.eng)

    def loop(self, i, steps):
        self.turn = i * steps

    def looped(self, steps, turns):
        self.turn = 0
        self.n += steps * (turns - 1)


def build(nc, A):
    with ExitStack() as whole:
        program(nc, A, whole)


def program(nc, A, whole):
    stage_sems = {}
    stage = [0]

    def S(name):
        if name not in stage_sems:
            stage_sems[name] = nc.alloc_semaphore(name=f"{name}_{stage[0]}")
        return stage_sems[name]

    def next_stage():
        nc.clear_and_free_semaphores(list(stage_sems.values()))
        nc.all_engine_barrier()
        stage_sems.clear()
        stage[0] += 1
        for chain, name in chains:
            chain.sem, chain.n = S(name), 0
        ln_stats.n = 0


    def sb(ctx, name, shape, dt=F32):
        return ctx.enter_context(nc.sbuf_tensor(name, shape, dt))

    SPARE[:] = [whole.enter_context(nc.semaphore("spare"))]
    V, C, M, PL = nc.vector, nc.scalar, nc.tensor, nc.gpsimd
    dchain = Chain(V, S("dve_chain"))
    achain = Chain(C, S("act_chain"))
    pchain = Chain(PL, S("pool_chain"))
    chains = ((dchain, "dve_chain"), (achain, "act_chain"), (pchain, "pool_chain"))

    ps = whole.enter_context(nc.psum_tensor("ps", [P, 8, 512], F32))

    k0_parts = nc.dram_tensor("k0_parts", [LEVELS, P, GP], BF16).ap()
    k1_parts = nc.dram_tensor("k1_parts", [LEVELS, P, GP], BF16).ap()
    v1_rows = nc.dram_tensor("v1_rows", [P, NG, H1 * VW], F32).ap()
    nmid_lines = nc.dram_tensor("nmid_lines", [LEVELS, H0 * T], BF16).ap()
    ns_lines = nc.dram_tensor("ns_lines", [LEVELS, H1 * T], BF16).ap()
    mask_line = nc.dram_tensor("mask_line", [3, GP], BF16).ap()

    ident = sb(whole, "ident", [P, P])
    x_sb = sb(whole, "x_sb", [P, NT, D])
    xn = sb(whole, "xn", [P, NT, D])
    xnT = sb(whole, "xnT", [P, T])
    gates = sb(whole, "gates", [P, 4])
    ones = sb(whole, "ones", [P, 1])
    general = sb(whole, "general", [1, 2], I32)
    kabs = sb(whole, "kabs", [P, NGROUP])
    kabs1 = sb(whole, "kabs1", [P, 1])
    quarter = sb(whole, "quarter", [P, 1])
    gt = sb(whole, "gt", [P, 4])
    stats = sb(whole, "stats", [P, NT, 6])
    mv = sb(whole, "mv", [P, NT, 2])
    vare = sb(whole, "vare", [P, NT])
    sdev = sb(whole, "sdev", [P, NT])
    rstd = sb(whole, "rstd", [P, NT])
    c_t = sb(whole, "c_t", [P, NT, D])
    q1_parts = nc.dram_tensor("q1_parts", [LEVELS, P, T], BF16).ap()

    def every_tile(row):
        return row[:, :].unsqueeze(1).to_broadcast([P, NT, D])

    def flat(tile):
        return tile[:, :, :].rearrange("p a b -> p (a b)")

    def ln_stats(src, ready, wait=True):
        for t in range(NT):
            V.bn_stats(stats[:, t, :], src[:, t, :]).then_inc(S("ln_stats"), 1)
        ln_stats.n += NT
        V.wait_ge(S("ln_stats"), ln_stats.n)
        for t in range(NT):
            last = V.bn_aggr(mv[:, t, :], stats[:, t, :])
            last.then_inc(S("ln_stats"), 1)
        ln_stats.n += NT
        V.wait_ge(S("ln_stats"), ln_stats.n)
        V.tensor_scalar(vare[:, :], mv[:, :, 1], LN_EPS, None, ALU.add).then_inc(ready, 1)

    ln_stats.n = 0

    def ln_sqrt(count, ready, done):
        C.wait_ge(ready, count)
        C.activation(sdev[:, :], vare[:, :], ACT.Sqrt).then_inc(done, 1)

    def ln_apply(dst, src, done, count, out_sem):
        V.wait_ge(done, count)
        dchain(V.reciprocal(rstd[:, :], sdev[:, :]))
        for t in range(NT):
            V.tensor_scalar(dst[:, t, :], src[:, t, :], mv[:, t, 0:1], rstd[:, t:t + 1],
                            ALU.subtract, ALU.mult).then_inc(out_sem, 1)

    def transpose_tiles(src, bank, done):
        for t in range(NT):
            last = M.transpose(ps[:, bank + t // 4, (t % 4) * P:(t % 4 + 1) * P], src[:, t, :], ident[:, :])
        last.then_inc(done, 1)

    l0 = ExitStack()
    KA = sb(l0, "KA", [P, H0, GP], BF16)
    KB = sb(l0, "KB", [P, H0, GP], BF16)
    V0 = sb(l0, "V0", [P, NG, D])
    QA = sb(l0, "QA", [P, H0, T], BF16)
    QB = sb(l0, "QB", [P, H0, T], BF16)
    NROW, NAUX = 2 * DH0 + 1, 2 * DH0 + 4

    with ExitStack() as b1:
        wq0 = sb(b1, "wq0", [P, P])
        wk0 = sb(b1, "wk0", [DC, P])
        wk1 = sb(b1, "wk1", [DC, P])
        wv = sb(b1, "wv", [DC, 2 * P])
        bk1 = sb(b1, "bk1", [P, 1])
        bv1 = sb(b1, "bv1", [P, P])
        NR = 3
        ctx_in = sb(b1, "ctx_in", [P, NR, 4, DC])
        ctxT = sb(b1, "ctxT", [DC, 2, GROUP])
        res0 = sb(b1, "res0", [P, GROUP])
        res1 = sb(b1, "res1", [P, GROUP])
        k1f = sb(b1, "k1f", [P, GROUP])
        kl0 = sb(b1, "kl0", [P, 2, LEVELS, GROUP], BF16)
        kl1 = sb(b1, "kl1", [P, 2, LEVELS, GROUP], BF16)
        v1g = sb(b1, "v1g", [P, 2, 4, H1, VW])
        qs = sb(b1, "qs", [P, T])
        ql = sb(b1, "ql", [P, LEVELS, T], BF16)
        mask8 = sb(b1, "mask8", [P, NG], U8)
        maskf = sb(b1, "maskf", [P, 3, NG], BF16)
        lastv = G - (NG - 1) * P

        def width(i):
            return min(GROUP, GP - i * GROUP)

        def stores(n, r):
            return (n + 1 - r) // 2

        SECTIONS = [(0, 4), (4, 8), (8, NGROUP)]

        with nc.Block() as block:
            @block.sync
            def _(sp):
                sp.dma_start(x_sb[:, :, :], A["x"][0].rearrange("(n p) d -> p n d", p=P)).then_inc(S("x_in"), 16)
                sp.dma_start(ident[:, :], A["ident"]).then_inc(S("w_in"), 16)
                sp.dma_start(wk0[:, :], A["L0_xattn_Wk"]).then_inc(S("w_in"), 16)
                sp.dma_start(wk1[:, :], A["L1_xattn_wk"]).then_inc(S("w_in"), 16)
                sp.dma_start(wv[:, 0:P], A["L0_xattn_Wv"]).then_inc(S("w_in"), 16)
                sp.dma_start(wv[:, P:2 * P], A["L1_xattn_wv"]).then_inc(S("w_in"), 16)
                sp.dma_start(wq0[:, :], A["L0_xattn_Wq"]).then_inc(S("w_in"), 16)
                for i in range(NGROUP):
                    if i >= NR:
                        sp.wait_ge(S("ctxT_ps"), i - NR + 1)
                    if i == NGROUP - 1:
                        sp.wait_ge(S("ctx_pad"), 1)
                        full = (G - i * GROUP) // P
                        sp.dma_start(ctx_in[:, i % NR, 0:full, :],
                                     A["ctx_768"][0, i * GROUP:i * GROUP + full * P, :]
                                     .rearrange("(c p) d -> p c d", p=P)).then_inc(S(f"ctx_in{i % NR}"), 16)
                        sp.dma_start(ctx_in[0:lastv, i % NR, full, :],
                                     A["ctx_768"][0, G - lastv:G, :]).then_inc(S(f"ctx_in{i % NR}"), 16)
                    else:
                        sp.dma_start(ctx_in[:, i % NR, :, :],
                                     A["ctx_768"][0, i * GROUP:(i + 1) * GROUP, :]
                                     .rearrange("(c p) d -> p c d", p=P)).then_inc(S(f"ctx_in{i % NR}"), 16)
                sp.wait_ge(S("mask_out"), 48)
                for h in range(H0):
                    sp.dma_start(KB[2 * DH0:NROW, h, :], mask_line[0:1, :]).then_inc(S("k0_gathered"), 16)
                    sp.dma_start(KB[NROW:NAUX, h, :], mask_line[2, :].partition_broadcast(LEVELS))\
                        .then_inc(S("k0_gathered"), 16)
                for s0, s1 in SECTIONS:
                    for r in range(2):
                        sp.wait_ge(S(f"k0_out{r}"), 16 * stores(s1, r))
                    c0, c1 = s0 * GROUP, min(s1 * GROUP, GP)
                    for r, lv in enumerate((0, 1, 0, 1)):
                        sp.dma_start(KA[DH0 * r:DH0 * (r + 1), :, c0:c1],
                                     k0_parts[lv, :, c0:c1].rearrange("(h d) g -> d h g", h=H0))\
                          .then_inc(S("k0_gathered"), 16)
                    for r, lv in enumerate((2, 0)):
                        sp.dma_start(KB[DH0 * r:DH0 * (r + 1), :, c0:c1],
                                     k0_parts[lv, :, c0:c1].rearrange("(h d) g -> d h g", h=H0))\
                          .then_inc(S("k0_gathered"), 16)
                sp.wait_ge(S("k0_gathered"), 16 * (2 * H0 + 6 * len(SECTIONS)))
                for r in range(2):
                    sp.wait_ge(S(f"k1_out{r}"), 16 * stores(NGROUP, r))
                    sp.wait_ge(S(f"v1_out{r}"), 16 * stores(NGROUP, r))

            @block.gpsimd
            def _(pool):
                PL.memset(mask8[:, :], 0).then_inc(S("mask8_zero"), 1)
                pool.wait_ge(S("mask8_zero"), 1)
                PL.memset(v1g[:, :, :, :, DH1:VW], 1.0).then_inc(S("v1_ones"), 1)
                pool.wait_ge(S("v1_ones"), 1)
                PL.dma_start(bv1[:, :], A["L1_xattn_bv"].partition_broadcast(P)).then_inc(S("bv_in"), 16)
                PL.dma_start(bk1[:, :], A["L1_xattn_bk"].rearrange("(p a) -> p a", a=1)).then_inc(S("bk_in"), 16)
                pool.wait_ge(S("mask8_zero"), 1)
                full = G // NG
                PL.dma_start(mask8[0:full, :], A["mask_BxS2_bf1"][0, 0:full * NG].rearrange("(p c) -> p c", c=NG))\
                    .then_inc(S("mask_in"), 16)
                PL.dma_start(mask8[full:full + 1, 0:G - full * NG],
                             A["mask_BxS2_bf1"][0:1, full * NG:G]).then_inc(S("mask_in"), 16)
                pchain(PL.memset(maskf[:, 2, :], 1.0))
                pchain(PL.memset(maskf[:, 1, :], 0.0))
                pchain(PL.affine_select(out=maskf[:, 1, :], in_=maskf[:, 1, :], pattern=[[-1, NG]],
                                        compare_op=ALU.is_gt, fill=MASKED, base=G, channel_multiplier=-NG))
                pool.wait_ge(S("mask_in"), 32)
                pchain(PL.tensor_scalar(maskf[:, 0, :], mask8[:, :], -1.0, -MASKED, ALU.add, ALU.mult))
                for j in range(3):
                    PL.dma_start(mask_line[j, :].rearrange("(p c) -> p c", c=NG), maskf[:, j, :])\
                        .then_inc(S("mask_out"), 16)
                pchain(PL.memset(QB[2 * DH0:P, :, :], 1.0))
                for i in range(NGROUP):
                    w, r = width(i), i % 2
                    pool.wait_ge(S("k1_evac"), i + 1)
                    if i >= 2:
                        pool.wait_ge(S(f"k1_out{r}"), 16 * (i // 2))
                    pchain(PL.tensor_copy(kl1[:, r, 0, 0:w], k1f[:, 0:w]))
                    pchain(PL.tensor_tensor(res1[:, 0:w], k1f[:, 0:w], kl1[:, r, 0, 0:w], ALU.subtract))
                    pchain(PL.tensor_copy(kl1[:, r, 1, 0:w], res1[:, 0:w]))
                    PL.tensor_tensor(kl1[:, r, 2, 0:w], res1[:, 0:w], kl1[:, r, 1, 0:w], ALU.subtract)\
                        .then_inc(S("k1_split"), 1)
                    pool.wait_ge(S("k1_split"), i + 1)

            @block.scalar
            def _(act):
                ln_sqrt(1, S("ln_var"), S("ln_sd"))
                act.wait_ge(S("xnT_ps"), 1)
                C.copy(xnT[:, :], ps[:, 0:2, :].rearrange("p a b -> p (a b)")).then_inc(S("xnT_sb"), 1)
                act.wait_ge(S("q_ps"), 1)
                achain(C.mul(qs[:, :], ps[:, 2:4, :].rearrange("p a b -> p (a b)"), float(DH0) ** -0.5))
                C.copy(ql[:, 0, :], qs[:, :]).then_inc(S("q_h"), 1)
                act.wait_ge(S("bk_in"), 16)
                for i in range(NGROUP):
                    w, r = width(i), i % 2
                    act.wait_ge(S("ctxT_ps"), i + 1)
                    if i >= 2:
                        act.wait_ge(S("v_ps"), i - 1)
                    C.copy(ctxT[:, r, 0:w], ps[0:DC, 4, 0:w]).then_inc(S("ctxT_sb"), 1)
                    act.wait_ge(S("k_ps"), i + 1)
                    if i >= 1:
                        act.wait_ge(S("k1_split"), i)
                        act.wait_ge(S("k1_seen"), i)
                    C.activation(k1f[:, 0:w], ps[:, 6, 0:w], ACT.Identity, bias=bk1[:, 0:1]).then_inc(S("k1_evac"), 1)
                    if i >= 2:
                        act.wait_ge(S(f"k0_out{r}"), 16 * (i // 2))
                    C.copy(kl0[:, r, 0, 0:w], ps[:, 5, 0:w]).then_inc(S("k0_h"), 1)
                    act.wait_ge(S("v_ps"), i + 1)
                    C.copy(V0[:, 4 * i:4 * i + w // P, :],
                           ps[:, 7, 0:w].rearrange("p (c k) -> p c k", k=P)).then_inc(S("v0_evac"), 1)
                    for j in ([i - 1] if i else []) + ([i] if i == NGROUP - 1 else []):
                        wj = width(j)
                        act.wait_ge(S("k0_split"), j + 1)
                        C.dma_start(k0_parts[:, :, j * GROUP:j * GROUP + wj].rearrange("l p g -> p l g"),
                                    kl0[:, j % 2, :, 0:wj]).then_inc(S(f"k0_out{j % 2}"), 16)
                        act.wait_ge(S("k1_split"), j + 1)
                        C.dma_start(k1_parts[:, :, j * GROUP:j * GROUP + wj].rearrange("l p g -> p l g"),
                                    kl1[:, j % 2, :, 0:wj]).then_inc(S(f"k1_out{j % 2}"), 16)
                        act.wait_ge(S("v1_evac"), j + 1)
                        C.dma_start(v1_rows[:, 4 * j:4 * j + wj // P, :],
                                    v1g[:, j % 2, 0:wj // P, :, :].rearrange("p c h v -> p c (h v)"))\
                            .then_inc(S(f"v1_out{j % 2}"), 16)

            @block.vector
            def _(dve):
                dchain(V.memset(ones[:, :], 1.0))
                dve.wait_ge(S("x_in"), 16)
                ln_stats(x_sb, S("ln_var"))
                ln_apply(xn, x_sb, S("ln_sd"), 1, S("xn_ready"))
                dve.wait_ge(S("q_h"), 1)
                dchain(V.tensor_tensor(qs[:, :], qs[:, :], ql[:, 0, :], ALU.subtract))
                dchain(V.tensor_copy(ql[:, 1, :], qs[:, :]))
                V.tensor_tensor(ql[:, 2, :], qs[:, :], ql[:, 1, :], ALU.subtract).then_inc(S("q_split"), 1)
                dve.wait_ge(S("bv_in"), 16)
                dve.wait_ge(S("v1_ones"), 1)
                for i in range(NGROUP):
                    w, r = width(i), i % 2
                    if i == NGROUP - 4:
                        dve.wait_ge(S("ctxT_ps"), NGROUP - NR)
                        V.memset(ctx_in[:, (NGROUP - 1) % NR, :, :], 0.0).then_inc(S("ctx_pad"), 1)
                    dve.wait_ge(S("k1_evac"), i + 1)
                    dchain(V.tensor_reduce(kabs[:, i:i + 1], k1f[:, 0:w], AX.X, ALU.max, apply_absolute_value=True))
                    V.sem_inc(S("k1_seen"), 1)
                    dve.wait_ge(S("k0_h"), i + 1)
                    dchain(V.tensor_tensor(res0[:, 0:w], ps[:, 5, 0:w], kl0[:, r, 0, 0:w], ALU.subtract))
                    dchain(V.tensor_copy(kl0[:, r, 1, 0:w], res0[:, 0:w]))
                    V.tensor_tensor(kl0[:, r, 2, 0:w], res0[:, 0:w], kl0[:, r, 1, 0:w], ALU.subtract)\
                        .then_inc(S("k0_split"), 1)
                    dve.wait_ge(S("k0_split"), i + 1)
                    dve.wait_ge(S("v_ps"), i + 1)
                    if i >= 2:
                        dve.wait_ge(S(f"v1_out{r}"), 16 * (i // 2))
                    n = w // P
                    V.tensor_tensor(v1g[:, r, 0:n, :, 0:DH1],
                                    ps[:, 0, 0:w].rearrange("p (c h v) -> p c h v", h=H1, v=DH1),
                                    bv1[:, :].rearrange("p (h v) -> p h v", v=DH1).unsqueeze(1)
                                    .to_broadcast([P, n, H1, DH1]), ALU.add).then_inc(S("v1_evac"), 1)

            @block.tensor
            def _(pe):
                pe.wait_ge(S("w_in"), 16 * 6)
                pe.wait_ge(S("xn_ready"), NT)
                transpose_tiles(xn, 0, S("xnT_ps"))
                pe.wait_ge(S("xnT_sb"), 1)
                for b in range(NB):
                    last = M.matmul(ps[:, 2 + b, :], wq0[:, :], xnT[:, b * TB:(b + 1) * TB], start=True, stop=True)
                last.then_inc(S("q_ps"), 1)

                def turn(i):
                    pe.wait_ge(S(f"ctx_in{i % NR}"), 16 * (i // NR + 1) + (16 if i == NGROUP - 1 else 0))
                    if i >= 1:
                        pe.wait_ge(S("ctxT_sb"), i)
                    for c in range(width(i) // P):
                        last = M.transpose(ps[0:DC, 4, c * P:(c + 1) * P], ctx_in[:, i % NR, c, :], ident[:, :])
                    last.then_inc(S("ctxT_ps"), 1)
                    last2 = last
                turn(0)
                for i in range(NGROUP):
                    w, r = width(i), i % 2
                    pe.wait_ge(S("ctxT_sb"), i + 1)
                    if i + 1 < NGROUP:
                        turn(i + 1)
                    if i >= 1:
                        pe.wait_ge(S("k0_split"), i)
                        pe.wait_ge(S("k1_evac"), i)
                    M.matmul(ps[:, 5, 0:w], wk0[:, :], ctxT[:, r, 0:w], start=True, stop=True)
                    M.matmul(ps[:, 6, 0:w], wk1[:, :], ctxT[:, r, 0:w], start=True, stop=True).then_inc(S("k_ps"), 1)
                    if i >= 1:
                        pe.wait_ge(S("v0_evac"), i)
                        pe.wait_ge(S("v1_evac"), i)
                    for c in range(w // P):
                        for bank, cols in ((7, slice(0, P)), (0, slice(P, 2 * P))):
                            last = M.matmul(ps[:, bank, c * P:(c + 1) * P], ctxT[:, r, c * P:(c + 1) * P],
                                            wv[:, cols], start=True, stop=True)
                    last.then_inc(S("v_ps"), 1)

        with nc.Block() as block:
            @block.sync
            def _(sp):
                for h in range(H0):
                    rows = slice(DH0 * h, DH0 * (h + 1))
                    for r, lv in enumerate((0, 0, 1, 1)):
                        sp.dma_start(QA[DH0 * r:DH0 * (r + 1), h, :], ql[rows, lv, :]).then_inc(S("q_gathered"), 16)
                    for r, lv in enumerate((0, 2)):
                        sp.dma_start(QB[DH0 * r:DH0 * (r + 1), h, :], ql[rows, lv, :]).then_inc(S("q_gathered"), 16)
                sp.wait_ge(S("q_gathered"), 16 * 6 * H0)

    NI = H0 * NT
    tops = sb(l0, "tops", [P, NI, 40])
    weight = sb(l0, "weight", [P, NI])
    with ExitStack() as b2:
        cand = sb(b2, "cand", [P, NPIECE, 8])
        cand2 = sb(b2, "cand2", [P, NCAND])
        odd = sb(b2, "odd", [P, 2, NI])
        odd1 = sb(b2, "odd1", [P, 1])
        top40 = sb(b2, "top40", [P, 40])
        hidden = sb(b2, "hidden", [P, NI])
        mid = sb(b2, "mid", [P, NI])
        nmid = sb(b2, "nmid", [P, NI])
        tshift = sb(b2, "tshift", [P, NI, TOPK])
        tsum = sb(b2, "tsum", [P, NI])
        nmT = sb(b2, "nmT", [NI, P])
        nmR = sb(b2, "nmR", [NI, P])
        nml = sb(b2, "nml", [NI, LEVELS, P], BF16)
        BANKS = 7
        NBK = -(-GP // 512)
        SELECT = 11

        with nc.Block() as block:
            @block.tensor
            def _(pe):
                with pe.Fori(0, NI) as i:
                    for j in range(NBK):
                        w = min(512, GP - j * 512)
                        used = j - BANKS if j >= BANKS else (j + BANKS - NBK if j + BANKS < NBK else j - NBK)
                        pe.wait_ge(S("bank_read"), i * NBK + NBK + used + 1)
                        M.matmul(ps[:, j % BANKS, 0:w], QA[:, :, :].rearrange("p h t -> p (h t)")[:, bass.ds(i * P, P)],
                                 KA[:, :, :].rearrange("p h g -> p (h g)")[:, bass.ds((i // NT) * GP + j * 512, w)],
                                 start=True, stop=False)
                        M.matmul(ps[:, j % BANKS, 0:w], QB[0:NROW, :, :].rearrange("p h t -> p (h t)")[:, bass.ds(i * P, P)],
                                 KB[0:NROW, :, :].rearrange("p h g -> p (h g)")[:, bass.ds((i // NT) * GP + j * 512, w)],
                                 start=False, stop=True).then_inc(S("bank_full"), 1)
                pe.wait_ge(S("nmid_ready"), 1)
                M.transpose(ps[0:NI, 7, 0:P], nmid[:, :], ident[:, :]).then_inc(S("nmT_ps"), 1)
                pe.wait_ge(S("odd_ready"), 1)
                M.matmul(ps[0:1, 6, 0:1], odd1[:, :], ones[:, :], start=True, stop=True).then_inc(S("odd_ps"), 1)

            @block.vector
            def _(dve):
                dve.sem_inc(S("bank_read"), NBK)
                with dve.Fori(0, NI) as i:
                    dchain.loop(i, SELECT)
                    n0 = dchain.n
                    for j in range(NBK):
                        w = min(512, GP - j * 512)
                        dve.wait_ge(S("bank_full"), i * NBK + j + 1)
                        take_wait(dve)
                        for q in range(w // PIECE):
                            last = V.max(cand[:, 4 * j + q, :], ps[:, j % BANKS, q * PIECE:(q + 1) * PIECE])
                        last.then_inc(S("bank_read"), 1)
                    dve.wait_ge(S("bank_read"), i * NBK + 2 * NBK)
                    flat = cand[:, :, :].rearrange("p a b -> p (a b)")
                    dchain(V.reduce_max(hidden[:, bass.ds(i, 1)], cand[:, :, 7], AX.X), before_max=True)
                    for r in range(5):
                        top = top40[:, 8 * r:8 * r + 8]
                        src = flat if r == 0 else cand2[:, :]
                        dchain(V.max(top, src), before_max=r < 4)
                        if r < 4:
                            dchain(V.match_replace(cand2[:, :], top, src, LOWEST), before_max=True)
                    dchain(V.tensor_copy(tops[:, bass.ds(i, 1), :], top40[:, :].unsqueeze(1)))
                    assert dchain.n - n0 == SELECT
                dchain.looped(SELECT, NI)
                dchain(V.tensor_tensor(mid[:, :], tops[:, :, TOPK - 1], tops[:, :, TOPK], ALU.add))
                V.tensor_scalar(nmid[:, :], mid[:, :], -0.5, None, ALU.mult).then_inc(S("nmid_ready"), 1)
                dve.wait_ge(S("nmid_ready"), 1)
                V.tensor_tensor(tshift[:, :, :], tops[:, :, 0:TOPK],
                                nmid[:, :].unsqueeze(2).to_broadcast([P, NI, TOPK]), ALU.add).then_inc(S("tshift_ready"), 1)
                dchain(V.tensor_tensor(odd[:, 0, :], hidden[:, :], tops[:, :, TOPK], ALU.is_gt))
                dchain(V.tensor_tensor(odd[:, 1, :], tops[:, :, TOPK - 1], tops[:, :, TOPK], ALU.is_equal))
                dchain(V.tensor_tensor(odd[:, 0, :], odd[:, 0, :], odd[:, 1, :], ALU.add))
                dchain(V.tensor_tensor(odd[:, 1, :], tops[:, :, 0], nmid[:, :], ALU.add))
                dchain(V.tensor_scalar(odd[:, 1, :], odd[:, 1, :], EXP_RANGE, None, ALU.is_gt))
                dchain(V.tensor_tensor(odd[:, 0, :], odd[:, 0, :], odd[:, 1, :], ALU.add))
                V.reduce_max(odd1[:, :], odd[:, 0, :], AX.X).then_inc(S("odd_ready"), 1)
                dve.wait_ge(S("odd_ps"), 1)
                dchain(V.tensor_copy(general[0:1, 0:1], ps[0:1, 6, 0:1]))
                dve.wait_ge(S("texp_ready"), 1)
                dchain(V.reduce_sum(tsum[:, :], tshift[:, :, :], AX.X))
                dchain(V.tensor_scalar(tsum[:, :], tsum[:, :], float(H0), None, ALU.mult))
                dchain(V.reciprocal(weight[:, :], tsum[:, :]))
                dve.wait_ge(S("nmT_ps"), 1)
                dchain(V.tensor_copy(nmT[:, :], ps[0:NI, 7, 0:P]))
                dchain(V.tensor_copy(nml[:, 0, :], nmT[:, :]))
                dchain(V.tensor_tensor(nmR[:, :], nmT[:, :], nml[:, 0, :], ALU.subtract))
                dchain(V.tensor_copy(nml[:, 1, :], nmR[:, :]))
                V.tensor_tensor(nml[:, 2, :], nmR[:, :], nml[:, 1, :], ALU.subtract).then_inc(S("nml_ready"), 1)

            @block.scalar
            def _(act):
                act.wait_ge(S("tshift_ready"), 1)
                C.activation(tshift[:, :, :], tshift[:, :, :], ACT.Exp).then_inc(S("texp_ready"), 1)

            @block.sync
            def _(sp):
                sp.wait_ge(S("nml_ready"), 1)
                sp.dma_start(nmid_lines.rearrange("l (i p) -> i l p", p=P), nml[:, :, :]).then_inc(S("nmid_out"), 16)
                sp.wait_ge(S("nmid_out"), 16)
                sp.dma_start(QB[NROW:NAUX, :, :].rearrange("l h t -> l (h t)"), nmid_lines).then_inc(S("nmid_rows"), 16)
                sp.wait_ge(S("nmid_rows"), 16)

    next_stage()
    l0_general = nc.values_load(general[0:1, 0:1], min_val=0, max_val=P * 3)
    with nc.If(l0_general > 0):
        with ExitStack() as b3:
            row = sb(b3, "row", [P, GP])
            t40 = sb(b3, "t40", [P, TOPK])
            nmax = sb(b3, "nmax", [P, 1])
            zsum, zinv = sb(b3, "zsum", [P, 1]), sb(b3, "zinv", [P, 1])
            junk = sb(b3, "junk", [P, TOPK])
            junk2 = sb(b3, "junk2", [P, D])
            exg, pg, pgT = (sb(b3, n, [P, 2, 512]) for n in ("exg", "pg", "pgT"))
            flatA = lambda t, rows: t[rows, :, :].rearrange("p h t -> p (h t)")

            def bank_width(j):
                return min(512, GP - j * 512)

            with nc.Block() as block:
                @block.gpsimd
                def _(pool):
                    PL.memset(c_t[:, :, :], 0.0).then_inc(S("c_zero"), 1)

                @block.sync
                def _(sp):
                    take_part(sp)

                @block.tensor
                def _(pe):
                    def scores(h, i, e):
                        j, w = e % NBK, bank_width(e % NBK)
                        pe.wait_ge(S("g_read"), i * 2 * NBK + e + 1)
                        M.matmul(ps[:, e % 2, 0:w], flatA(QA, slice(0, P))[:, bass.ds(i * P, P)],
                                 flatA(KA, slice(0, P))[:, bass.ds(h * GP + j * 512, w)], start=True, stop=False)
                        M.matmul(ps[:, e % 2, 0:w], flatA(QB, slice(0, NROW))[:, bass.ds(i * P, P)],
                                 flatA(KB, slice(0, NROW))[:, bass.ds(h * GP + j * 512, w)], start=False, stop=True)\
                            .then_inc(S("g_scored"), 1)

                    with pe.Fori(0, H0) as h:
                        with pe.Fori(0, NT) as t:
                            i = h * NT + t
                            for e in range(NBK):
                                scores(h, i, e)
                            for j in range(NBK):
                                scores(h, i, NBK + j)
                                pe.wait_ge(S("g_kept"), i * NBK + j + 2)
                                for c in range(bank_width(j) // P):
                                    last = M.transpose(ps[:, 2 + j % 2, c * P:(c + 1) * P], pg[:, j % 2, c * P:(c + 1) * P],
                                                       ident[:, :])
                                last.then_inc(S("g_turned"), 1)
                                pe.wait_ge(S("g_placed"), i * NBK + j + 1)
                                if j == 0:
                                    pe.wait_ge(S("g_added"), i + 1)
                                n = bank_width(j) // P
                                for c in range(n):
                                    last = M.matmul(ps[:, 4, 0:D], pgT[:, j % 2, c * P:(c + 1) * P], V0[:, 4 * j + c, :],
                                                    start=j == 0 and c == 0, stop=j == NBK - 1 and c == n - 1)
                                last.then_inc(S("g_summed"), 1)

                @block.scalar
                def _(act):
                    act.sem_inc(S("g_read"), 2)
                    with act.Fori(0, NI) as i:
                        for j in range(NBK):
                            w = bank_width(j)
                            act.wait_ge(S("g_scored"), i * 2 * NBK + j + 1)
                            if j == 0:
                                act.wait_ge(S("g_kept"), i * NBK + 1)
                            C.copy(row[:, j * 512:j * 512 + w], ps[:, j % 2, 0:w]).then_inc(S("g_read"), 1)
                        act.wait_ge(S("g_max"), i + 1)
                        C.activation(junk[:, :], t40[:, :], ACT.Exp, bias=nmax[:, 0:1], accum_out=zsum[:, :]).then_inc(S("g_z"), 1)
                        for j in range(NBK):
                            w, e = bank_width(j), NBK + j
                            act.wait_ge(S("g_scored"), i * 2 * NBK + e + 1)
                            if j >= 2:
                                act.wait_ge(S("g_kept"), i * NBK + j)
                            C.activation(exg[:, j % 2, 0:w], ps[:, e % 2, 0:w], ACT.Exp, bias=nmax[:, 0:1])\
                                .then_inc(S("g_read"), 1)

                @block.vector
                def _(dve):
                    steps_ = 2 * (TOPK // 8) + 4
                    dve.wait_ge(S("c_zero"), 1)
                    dve.sem_inc(S("g_added"), 1)
                    dve.sem_inc(S("g_kept"), 1)
                    with dve.Fori(0, H0) as h:
                        with dve.Fori(0, NT) as t:
                            i = h * NT + t
                            dchain.loop(i, steps_)
                            n0 = dchain.n
                            dve.wait_ge(S("g_read"), i * 2 * NBK + NBK + 2)
                            take_wait(dve)
                            for r in range(TOPK // 8):
                                top = t40[:, 8 * r:8 * r + 8]
                                dchain(V.max(top, row[:, :]), before_max=True)
                                dchain(V.match_replace(row[:, :], top, row[:, :], LOWEST), before_max=True)
                            V.tensor_scalar(nmax[:, :], t40[:, 0:1], -1.0, None, ALU.mult).then_inc(S("g_max"), 1)
                            for j in range(NBK):
                                w = bank_width(j)
                                dve.wait_ge(S("g_read"), i * 2 * NBK + NBK + j + 3)
                                V.scalar_tensor_tensor(pg[:, j % 2, 0:w], row[:, j * 512:j * 512 + w], LOWEST,
                                                       exg[:, j % 2, 0:w], ALU.is_equal, ALU.mult).then_inc(S("g_kept"), 1)
                                dve.wait_ge(S("g_turned"), i * NBK + j + 1)
                                if j >= 2:
                                    dve.wait_ge(S("g_summed"), i * NBK + j - 1)
                                V.tensor_copy(pgT[:, j % 2, 0:w], ps[:, 2 + j % 2, 0:w]).then_inc(S("g_placed"), 1)
                            dve.wait_ge(S("g_z"), i + 1)
                            dchain(V.tensor_scalar(zinv[:, :], zsum[:, :], float(H0), None, ALU.mult))
                            dchain(V.reciprocal(zinv[:, :], zinv[:, :]))
                            dve.wait_ge(S("g_summed"), i * NBK + NBK)
                            dchain(V.tensor_scalar(junk2[:, :], ps[:, 4, 0:D], zinv[:, 0:1], None, ALU.mult))
                            tile = c_t[:, bass.ds(t, 1), :]
                            dchain(V.tensor_tensor(tile, tile, junk2[:, :].unsqueeze(1), ALU.add))
                            dve.sem_inc(S("g_added"), 1)
                            assert dchain.n - n0 == steps_
                    dchain.looped(steps_, NI)
        next_stage()
    with nc.Else():
        with ExitStack() as b3:
            ex = sb(b3, "ex", [P, 2, 2, TB])
            pm = sb(b3, "pm", [P, 2, 2, TB])
            vst = sb(b3, "vst", [P, UNROLL, D])
            cT = sb(b3, "cT", [P, H0, TB])
            UNITS = 2 * UNROLL
            for tb in range(NB):
                U0, G0 = tb * 2 * NG, tb * NG
                with nc.Block() as block:
                    @block.sync
                    def _(sp):
                        take_part(sp)

                    @block.tensor
                    def _(pe):
                        def scores(k, g, unit):
                            slot = k % 2
                            if unit is not None:
                                pe.wait_ge(S("kept"), unit - 1)
                            for hh in range(2):
                                h = 2 * (k % 2) + hh
                                M.matmul(ps[:, 2 * slot + hh, :], KA[:, h, bass.ds(g * P, P)],
                                         QA[:, h, tb * TB:(tb + 1) * TB], start=True, stop=False)
                                last = M.matmul(ps[:, 2 * slot + hh, :], KB[0:NAUX, h, bass.ds(g * P, P)],
                                                QB[0:NAUX, h, tb * TB:(tb + 1) * TB], start=False, stop=True)
                            last.then_inc(S("scored"), 1)

                        def values(k, gk, unit, start, stop):
                            slot = k % 2
                            pe.wait_ge(S("kept"), unit + 1)
                            pe.wait_ge(S("v_placed"), gk + 1)
                            for hh in range(2):
                                h = 2 * (k % 2) + hh
                                last = M.matmul(ps[:, 4 + h, :], vst[:, (k // 2) % UNROLL, :], pm[:, slot, hh, :],
                                                start=start, stop=stop, skip_group_check=True)
                            last.then_inc(S("summed"), 1)

                        def turn(i, first=False, last=False):
                            for k in range(UNITS):
                                u, g = U0 + i * UNITS + k, i * UNROLL + k // 2
                                if not (last and k == UNITS - 1):
                                    nxt = k + 1
                                    free = None if first and tb == 0 and k == 0 else u + 1
                                    scores(nxt, i * UNROLL + nxt // 2, free)
                                values(k, G0 + g, u, first and k < 2, last and k >= UNITS - 2)

                        scores(0, 0, U0 if tb else None)
                        turn(0, first=True)
                        with pe.Fori(1, TURNS - 1) as i:
                            turn(i)
                        turn(TURNS - 1, last=True)
                        pe.wait_ge(S("cT_ready"), tb + 1)
                        for h in range(H0):
                            for c in range(TB // P):
                                last = M.transpose(ps[:, h, c * P:(c + 1) * P], cT[:, h, c * P:(c + 1) * P], ident[:, :])
                        last.then_inc(S("c_turned"), 1)

                    @block.scalar
                    def _(act):
                        def unit(k, u, first):
                            slot = k % 2
                            act.wait_ge(S("scored"), u + 1)
                            if not first:
                                act.wait_ge(S("kept"), u - 1)
                            C.activation(ex[:, slot, :, :], ps[:, 2 * slot:2 * slot + 2, :], ACT.Exp).then_inc(S("exped"), 1)

                        for k in range(UNITS):
                            unit(k, U0 + k, tb == 0 and k < 2)
                        with act.Fori(1, TURNS) as i:
                            for k in range(UNITS):
                                unit(k, U0 + i * UNITS + k, False)
                        act.wait_ge(S("summed"), 2 * NG * (tb + 1))
                        C.copy(cT[:, :, :], ps[:, 4:8, :]).then_inc(S("cT_ready"), 1)

                    @block.vector
                    def _(dve):
                        def unit(k, u, first):
                            slot = k % 2
                            dve.wait_ge(S("exped"), u + 1)
                            if not first:
                                dve.wait_ge(S("summed"), u - 1)
                            V.scalar_tensor_tensor(pm[:, slot, :, :], ps[:, 2 * slot:2 * slot + 2, :], 0.0,
                                                   ex[:, slot, :, :], ALU.is_ge, ALU.mult).then_inc(S("kept"), 1)

                        for k in range(UNITS):
                            unit(k, U0 + k, tb == 0 and k < 2)
                        with dve.Fori(1, TURNS) as i:
                            for k in range(UNITS):
                                unit(k, U0 + i * UNITS + k, False)
                        dve.wait_ge(S("c_turned"), tb + 1)
                        for c in range(TB // P):
                            t = tb * (TB // P) + c
                            dchain(V.tensor_scalar(c_t[:, t, :], ps[:, 0, c * P:(c + 1) * P],
                                                   weight[:, t:t + 1], None, ALU.mult))
                            for h in range(1, H0):
                                dchain(V.scalar_tensor_tensor(c_t[:, t, :], ps[:, h, c * P:(c + 1) * P],
                                                              weight[:, h * NT + t:h * NT + t + 1], c_t[:, t, :],
                                                              ALU.mult, ALU.add))

                    @block.gpsimd
                    def _(pool):
                        def place(k, g, first):
                            if not first:
                                pool.wait_ge(S("summed"), 2 * (G0 + g) - 2 * UNROLL + 2)
                            PL.tensor_copy(vst[:, k, :].unsqueeze(1), V0[:, bass.ds(g, 1), :]).then_inc(S("v_placed"), 1)

                        for k in range(UNROLL):
                            place(k, k, tb == 0)
                        with pool.Fori(1, TURNS) as i:
                            for k in range(UNROLL):
                                place(k, i * UNROLL + k, False)
        next_stage()
    l0.close()



    taps = sb(whole, "taps", [P, NT, D])
    with ExitStack() as b4:
        small = lambda name, n=NS: sb(b4, name, [P, n])
        a_re, a_im, c_re, c_im = (small(n) for n in ("a_re", "a_im", "c_re", "c_im"))
        ldt, dt = small("ldt", 1), small("dt", 1)
        rr, tau, z, q, e1 = (small(n) for n in ("rr", "tau", "z", "q", "e1"))
        sh, sn, cs = (small(n) for n in ("sh", "sn", "cs"))
        er, ei, nr, ni, den, t1, t2 = (small(n) for n in ("er", "ei", "nr", "ni", "den", "t1", "t2"))
        rows = sb(b4, "rows", [P, 4, 2 * NS])
        rowsT = sb(b4, "rowsT", [P, 4, D])
        turnsA = sb(b4, "turnsA", [P, D])
        rateA = sb(b4, "rateA", [P, D])
        steps = sb(b4, "steps", [P, KTAP])
        dskip = sb(b4, "dskip", [1, D])
        table = lambda name: sb(b4, name, [P, KTAP, D])
        phase, mag, work = table("phase"), table("mag"), table("work")
        zb, ua, ub = table("zb"), table("ua"), table("ub")
        QUARTER = float(np.pi / 2)
        TURN = float(2 * np.pi * (1 - 1e-7))

        with nc.Block() as block:
            @block.sync
            def _(sp):
                for dst, name in ((a_re, "A_re"), (a_im, "A_im"), (c_re, "C_re"), (c_im, "C_im")):
                    sp.dma_start(dst[:, :], A["L0_xattn_" + name]).then_inc(S("s4_in"), 16)
                sp.dma_start(ldt[:, :], A["L0_xattn_log_dt"].rearrange("(p a) -> p a", a=1)).then_inc(S("s4_in"), 16)
                sp.dma_start(steps[:, :], A["steps"].partition_broadcast(P)).then_inc(S("s4_in"), 16)
                sp.dma_start(dskip[:, :], A["L0_xattn_D_skip"].unsqueeze(0)).then_inc(S("s4_in"), 16)

            @block.vector
            def _(dve):
                tt = lambda o, a, b, op: dchain(V.tensor_tensor(o, a, b, op))
                ts = lambda o, a, s1, s2, o1, o2=ALU.bypass: dchain(V.tensor_scalar(o, a, s1, s2, o1, o2))
                a = lambda t: t[:, :]
                dve.wait_ge(S("dt_ready"), 1)
                dve.wait_ge(S("s4_in"), 16 * 7)
                ts(a(rr), a(a_re), dt[:, 0:1], None, ALU.mult)
                ts(a(t1), a(a_im), dt[:, 0:1], float(0.5 / np.pi), ALU.mult, ALU.mult)
                ts(a(t2), a(t1), ROUND, ROUND, ALU.add, ALU.subtract)
                V.tensor_tensor(a(tau), a(t1), a(t2), ALU.subtract).then_inc(S("tau_ready"), 1)
                ts(a(z), a(rr), -18.0, 1.0 / 16, ALU.max, ALU.mult)
                ts(a(q), a(z), 1.0 / 9, 1.0, ALU.mult, ALU.add)
                for k in range(8, 1, -1):
                    dchain(V.scalar_tensor_tensor(a(q), a(z), 1.0 / k, a(q), ALU.mult, ALU.mult))
                    ts(a(q), a(q), 1.0, None, ALU.add)
                tt(a(e1), a(z), a(q), ALU.mult)
                for _ in range(4):
                    dchain(V.scalar_tensor_tensor(a(e1), a(e1), 2.0, a(e1), ALU.add, ALU.mult))
                dve.wait_ge(S("trig_ready"), 2)
                tt(a(t1), a(sh), a(sh), ALU.mult)
                ts(a(cs), a(t1), -2.0, 1.0, ALU.mult, ALU.add)
                tt(a(er), a(e1), a(cs), ALU.mult)
                dchain(V.scalar_tensor_tensor(a(er), a(t1), -2.0, a(er), ALU.mult, ALU.add))
                dchain(V.scalar_tensor_tensor(a(ei), a(e1), 1.0, a(sn), ALU.add, ALU.mult))
                tt(a(nr), a(c_re), a(er), ALU.mult)
                tt(a(t1), a(c_im), a(ei), ALU.mult)
                tt(a(nr), a(nr), a(t1), ALU.subtract)
                tt(a(ni), a(c_re), a(ei), ALU.mult)
                tt(a(t1), a(c_im), a(er), ALU.mult)
                tt(a(ni), a(ni), a(t1), ALU.add)
                tt(a(den), a(a_re), a(a_re), ALU.mult)
                tt(a(t1), a(a_im), a(a_im), ALU.mult)
                tt(a(den), a(den), a(t1), ALU.add)
                dchain(V.reciprocal(a(den), a(den)))
                tt(a(t1), a(nr), a(a_re), ALU.mult)
                tt(a(t2), a(ni), a(a_im), ALU.mult)
                tt(a(t1), a(t1), a(t2), ALU.add)
                tt(a(t1), a(t1), a(den), ALU.mult)
                tt(a(t2), a(ni), a(a_re), ALU.mult)
                tt(a(z), a(nr), a(a_im), ALU.mult)
                tt(a(t2), a(t2), a(z), ALU.subtract)
                tt(a(t2), a(t2), a(den), ALU.mult)
                for half, sign in ((slice(0, NS), 2.0), (slice(NS, 2 * NS), -2.0)):
                    dchain(V.tensor_copy(rows[:, 0, half], a(rr)))
                    dchain(V.tensor_copy(rows[:, 1, half], a(tau)))
                    ts(rows[:, 2, half], a(t1), sign, None, ALU.mult)
                    ts(rows[:, 3, half], a(t2), -2.0, None, ALU.mult)
                V.tensor_copy(dt[:, :], dt[:, :]).then_inc(S("rows_ready"), 1)
                dve.wait_ge(S("rowsT_ps"), 1)
                dchain(V.tensor_copy(rowsT[:, :, :], ps[:, 0, :].rearrange("p (a d) -> p a d", d=D)))
                ts(a(rateA), rowsT[:, 0, :], float(KTAP), None, ALU.mult)
                ts(a(turnsA), rowsT[:, 1, :], float(KTAP), None, ALU.mult)
                ts(work[:, 0, :], a(turnsA), ROUND, ROUND, ALU.add, ALU.subtract)
                tt(a(turnsA), a(turnsA), work[:, 0, :], ALU.subtract)
                V.tensor_copy(dt[:, :], dt[:, :]).then_inc(S("rates_ready"), 1)

                over_d = lambda t: t.unsqueeze(1).to_broadcast([P, KTAP, D])
                over_steps = steps[:, :].unsqueeze(2).to_broadcast([P, KTAP, D])
                w = lambda t: t[:, :, :]

                def phases(turns):
                    tt(w(phase), over_d(turns), over_steps, ALU.mult)
                    ts(w(work), w(phase), ROUND, ROUND, ALU.add, ALU.subtract)
                    V.tensor_tensor(w(phase), w(phase), w(work), ALU.subtract).then_inc(S("phase_ready"), 1)

                phases(rowsT[:, 1, :])
                dve.wait_ge(S("zb_trig"), 1)
                dve.wait_ge(S("mag_exp"), 1)
                dchain(V.tensor_tensor(w(zb), w(zb), w(mag), ALU.mult))
                V.tensor_copy(dt[:, :], dt[:, :]).then_inc(S("zb_ready"), 1)
                phases(a(turnsA))
                dve.wait_ge(S("mag_exp"), 2)
                dve.wait_ge(S("ua_trig"), 1)
                tt(w(ua), w(ua), over_d(rowsT[:, 2, :]), ALU.mult)
                tt(w(ub), w(ub), over_d(rowsT[:, 3, :]), ALU.mult)
                tt(w(ua), w(ua), w(ub), ALU.add)
                V.tensor_tensor(w(ua), w(ua), w(mag), ALU.mult).then_inc(S("ua_ready"), 1)
                for h in range(2):
                    dve.wait_ge(S("taps_ps"), h + 1)
                    for r in range(4):
                        src = ps[0:KTAP, 4 * h:4 * h + 4, :].rearrange("p k (d m r) -> p m k d r", m=NT, r=4)
                        for kk in range(4):
                            d0 = 64 * h + 16 * kk
                            V.tensor_copy(taps[KTAP * r:KTAP * (r + 1), :, d0:d0 + 16], src[:, :, kk, :, r])\
                                .then_inc(S("taps_ready"), 1)
                dve.wait_ge(S("taps_ready"), 32)
                V.tensor_tensor(taps[0:1, 0, :], taps[0:1, 0, :], dskip[0:1, :], ALU.add).then_inc(S("taps_ready"), 1)

            @block.scalar
            def _(act):
                act.wait_ge(S("s4_in"), 16 * 7)
                C.activation(dt[:, :], ldt[:, :], ACT.Exp).then_inc(S("dt_ready"), 1)
                act.wait_ge(S("tau_ready"), 1)
                C.activation(sn[:, :], tau[:, :], ACT.Sin, scale=TURN).then_inc(S("trig_ready"), 1)
                C.activation(sh[:, :], tau[:, :], ACT.Sin, scale=TURN / 2).then_inc(S("trig_ready"), 1)
                w = lambda t: t[:, :, :]

                def trig(dst, rows_, sine):
                    if sine:
                        C.activation(dst[rows_, :, :], phase[rows_, :, :], ACT.Sin, scale=TURN)\
                            .then_inc(S("trig_done"), 1)
                    else:
                        C.activation(dst[rows_, :, :], work[rows_, :, :], ACT.Sin, scale=-TURN, bias=quarter[rows_, 0:1])\
                            .then_inc(S("trig_done"), 1)

                lo, hi = slice(0, NS), slice(NS, P)
                act.wait_ge(S("mag_ready"), 1)
                C.activation(w(mag), w(mag), ACT.Exp).then_inc(S("mag_exp"), 1)
                act.wait_ge(S("phase_ready"), 1)
                achain(C.activation(w(work), w(phase), ACT.Abs))
                act.wait_ge(S("quarter_ready"), 1)
                trig(zb, lo, False)
                trig(zb, hi, True)
                act.wait_ge(S("trig_done"), 2)
                act.sem_inc(S("zb_trig"), 1)
                act.wait_ge(S("phase_ready"), 2)
                achain(C.activation(w(work), w(phase), ACT.Abs))
                for dst, cos_rows, sin_rows in ((ua, lo, hi), (ub, hi, lo)):
                    trig(dst, cos_rows, False)
                    trig(dst, sin_rows, True)
                act.wait_ge(S("trig_done"), 6)
                act.sem_inc(S("ua_trig"), 1)
                act.wait_ge(S("mag_ready"), 2)
                C.activation(w(mag), w(mag), ACT.Exp).then_inc(S("mag_exp"), 1)

            @block.gpsimd
            def _(pool):
                PL.memset(quarter[:, :], QUARTER).then_inc(S("quarter_ready"), 1)
                over_steps = steps[:, :].unsqueeze(2).to_broadcast([P, KTAP, D])
                for n, rate in ((0, rowsT[:, 0, :]), (1, rateA[:, :])):
                    pool.wait_ge(S("rates_ready"), 1)
                    if n:
                        pool.wait_ge(S("zb_ready"), 1)
                    PL.tensor_tensor(mag[:, :, :], rate.unsqueeze(1).to_broadcast([P, KTAP, D]), over_steps,
                                     ALU.mult).then_inc(S("mag_ready"), 1)

            @block.tensor
            def _(pe):
                pe.wait_ge(S("rows_ready"), 1)
                for k in range(4):
                    last = M.transpose(ps[:, 0, k * D:(k + 1) * D], rows[:, k, :], ident[:, :])
                last.then_inc(S("rowsT_ps"), 1)
                pe.wait_ge(S("zb_ready"), 1)
                pe.wait_ge(S("ua_ready"), 1)
                for d in range(D):
                    last = M.matmul(ps[0:KTAP, d // 16, (d % 16) * KTAP:(d % 16 + 1) * KTAP],
                                    zb[:, :, d], ua[:, :, d], start=True, stop=True)
                    if d % 64 == 63:
                        last.then_inc(S("taps_ps"), 1)

    xt = sb(whole, "xt", [P, NT, D])
    wT = sb(whole, "wT", [P, T])
    with ExitStack() as b5:
        mask_t8 = sb(b5, "mask_t8", [P, NT], U8)
        mask_t = sb(b5, "mask_t", [P, NT])
        mg = sb(b5, "mg", [P, 1])
        wf = sb(b5, "wf", [P, HID])
        bf = sb(b5, "bf", [P, HID])
        rowsb = {n: sb(b5, "row_" + n, [P, D]) for n in ("g_norm_in", "b_norm_in", "g_ffn", "b_ffn")}
        dft = sb(b5, "dft", [P, 9, P])
        cT5 = sb(b5, "cT5", [P, T])
        film = sb(b5, "film", [P, NT, 4, D])
        xf = sb(b5, "xf", [P, NT, D])
        spec_x = sb(b5, "spec_x", [P, 2, NT, D])
        spec_k = sb(b5, "spec_k", [P, 2, NT, D])
        prod = sb(b5, "prod", [P, 2, 4, NT, D])
        FX, FK0, FK1, IFR, IFN, IFI = 0, 2, 4, 6, 7, 8
        with nc.Block() as block:
            @block.sync
            def _(sp):
                sp.dma_start(wf[:, 0:2 * D], A["L0_xattn_W_film_in"]).then_inc(S("b5_in"), 16)
                sp.dma_start(wf[:, 2 * D:], A["L0_xattn_W_film_out"]).then_inc(S("b5_in"), 16)
                sp.dma_start(bf[:, 0:2 * D], A["L0_xattn_b_film_in"].partition_broadcast(P)).then_inc(S("b5_in"), 16)
                sp.dma_start(bf[:, 2 * D:], A["L0_xattn_b_film_out"].partition_broadcast(P)).then_inc(S("b5_in"), 16)
                sp.dma_start(dft[:, :, :], A["dft"]).then_inc(S("b5_in"), 16)
                sp.dma_start(mg[:, :], A["L0_xattn_mod_gate"].partition_broadcast(P)).then_inc(S("b5_in"), 16)
                sp.dma_start(mask_t8[:, :], A["mask_BxS_bf1"].rearrange("o (n p) -> p (o n)", p=P),
                             allow_slow_non_contiguous=True).then_inc(S("b5_in"), 16)
                for n, tile in rowsb.items():
                    sp.dma_start(tile[:, :], A["L0_xattn_" + n].partition_broadcast(P)).then_inc(S("b5_in"), 16)

            @block.tensor
            def _(pe):
                pe.wait_ge(S("cm_ready"), NT)
                pe.wait_ge(S("b5_in"), 16 * 11)
                transpose_tiles(c_t, 0, S("cm_turned"))
                for part in range(2):
                    for half in range(2):
                        bank = ps[:, 2 + 2 * part + half, :]
                        if half == 0:
                            M.matmul(bank[:, D:4 * D], dft[:, FK0 + part, :], taps[:, 0:3, :], start=True, stop=False,
                                     skip_group_check=True)
                        else:
                            M.matmul(bank, dft[:, FK0 + part, :], taps[:, 3:7, :], start=True, stop=False,
                                     skip_group_check=True)
                        last = M.matmul(bank, dft[:, FK1 + part, :], taps[:, 4 * half:4 * half + 4, :],
                                        start=False, stop=True, skip_group_check=True)
                last.then_inc(S("spec_k_ps"), 1)
                pe.wait_ge(S("cT5_ready"), 1)
                pe.wait_ge(S("spec_k_ready"), 1)
                for t in range(NT):
                    if t >= 6:
                        pe.wait_ge(S("film_read"), t - 5)
                    M.matmul(ps[:, 2 + t % 6, :], cT5[:, t * P:(t + 1) * P], wf[:, :], start=True, stop=True)\
                        .then_inc(S("film_ps"), 1)
                pe.wait_ge(S("xf_ready"), 1)
                for part in range(2):
                    for half in range(2):
                        last = M.matmul(ps[:, 2 + 2 * part + half, :], dft[:, FX + part, :],
                                        xf[:, 4 * half:4 * half + 4, :], start=True, stop=True)
                last.then_inc(S("spec_x_ps"), 1)
                started = [False, False]
                for n, m in enumerate(reversed(range(NT))):
                    pe.wait_ge(S("prod_ready"), 4 * (n + 1))
                    for k, table in enumerate((IFR, IFN, IFI, IFI)):
                        for half in range(2):
                            lo_, hi_ = max(m, 4 * half), 4 * half + 4
                            if hi_ <= lo_:
                                continue
                            end = m == 0 and k == 3
                            last = M.matmul(ps[:, half, (lo_ - 4 * half) * D:(hi_ - 4 * half) * D],
                                            dft[:, table, :], prod[:, n % 2, k, lo_ - m:hi_ - m, :],
                                            start=not started[half], stop=end, skip_group_check=True)
                            started[half] = True
                    last.then_inc(S("prod_used"), 1)

            @block.scalar
            def _(act):
                act.wait_ge(S("cm_turned"), 1)
                C.copy(cT5[:, :], flat(ps[:, 0:2, :])).then_inc(S("cT5_ready"), 1)
                act.wait_ge(S("spec_k_ps"), 1)
                C.copy(spec_k[:, :, :, :].rearrange("p a b c -> p (a b c)"), flat(ps[:, 2:6, :])).then_inc(S("spec_k_ready"), 1)
                ln_sqrt(1, S("ln_in_var"), S("ln_in_sd"))
                act.wait_ge(S("spec_x_ps"), 1)
                C.copy(spec_x[:, :, :, :].rearrange("p a b c -> p (a b c)"), flat(ps[:, 2:6, :])).then_inc(S("spec_x_ready"), 1)
                ln_sqrt(1, S("ln_f_var"), S("ln_f_sd"))

            @block.vector
            def _(dve):
                dve.wait_ge(S("b5_in"), 16 * 11)
                dchain(V.tensor_copy(mask_t[:, :], mask_t8[:, :]))
                for t in range(NT):
                    V.tensor_scalar(c_t[:, t, :], c_t[:, t, :], mask_t[:, t:t + 1], None, ALU.mult).then_inc(S("cm_ready"), 1)
                ln_stats(xn, S("ln_in_var"))
                ln_apply(xf, xn, S("ln_in_sd"), 1, S("xl_ready"))
                dve.wait_ge(S("xl_ready"), NT)
                w = lambda t: t[:, :, :]
                dchain(V.tensor_tensor(w(xf), w(xf), every_tile(rowsb["g_norm_in"]), ALU.mult))
                dchain(V.tensor_tensor(w(xf), w(xf), every_tile(rowsb["b_norm_in"]), ALU.add))
                for t in range(NT):
                    dve.wait_ge(S("film_ps"), t + 1)
                    V.tensor_tensor(film[:, t, :, :].rearrange("p a b -> p (a b)"), ps[:, 2 + t % 6, :], bf[:, :], ALU.add)\
                        .then_inc(S("film_read"), 1)
                dve.wait_ge(S("film_read"), NT)
                dchain(V.tensor_scalar(film[:, :, :, :], film[:, :, :, :], mg[:, 0:1], None, ALU.mult))
                for k in (0, 2):
                    dchain(V.tensor_scalar(film[:, :, k, :], film[:, :, k, :], 1.0, None, ALU.add))
                dchain(V.tensor_tensor(w(xf), w(xf), film[:, :, 0, :], ALU.mult))
                V.tensor_tensor(w(xf), w(xf), film[:, :, 1, :], ALU.add).then_inc(S("xf_ready"), 1)
                dve.wait_ge(S("spec_x_ready"), 1)
                dve.wait_ge(S("spec_k_ready"), 1)
                for r, m in enumerate(reversed(range(NT))):
                    if r >= 2:
                        dve.wait_ge(S("prod_used"), r - 1)
                    n = NT - m
                    for k, (kp, xp) in enumerate(((0, 0), (1, 1), (0, 1), (1, 0))):
                        V.tensor_tensor(prod[:, r % 2, k, 0:n, :], spec_x[:, xp, 0:n, :],
                                        spec_k[:, kp, m, :].unsqueeze(1).to_broadcast([P, n, D]), ALU.mult)\
                            .then_inc(S("prod_ready"), 1)
                dve.wait_ge(S("prod_used"), NT)
                dchain(V.tensor_tensor(w(xt), ps[:, 0:2, :].rearrange("p a (b d) -> p (a b) d", d=D), film[:, :, 2, :], ALU.mult))
                dchain(V.tensor_tensor(w(xt), w(xt), film[:, :, 3, :], ALU.add))
                dchain(V.tensor_tensor(w(xt), w(xt), w(xn), ALU.add))
                ln_stats(xt, S("ln_f_var"))
                ln_apply(xf, xt, S("ln_f_sd"), 1, S("xl_ready"))
                dve.wait_ge(S("xl_ready"), 2 * NT)
                dchain(V.tensor_tensor(w(xf), w(xf), every_tile(rowsb["g_ffn"]), ALU.mult))
                dchain(V.tensor_tensor(w(xf), w(xf), every_tile(rowsb["b_ffn"]), ALU.add))
        with nc.Block() as block:
            @block.tensor
            def _(pe):
                transpose_tiles(xf, 0, S("xfT_ps"))

            @block.scalar
            def _(act):
                act.wait_ge(S("xfT_ps"), 1)
                C.copy(wT[:, :], flat(ps[:, 0:2, :])).then_inc(S("wT_ready"), 1)

    NF = HID // P

    with ExitStack() as b6:
        w1 = sb(b6, "w1", [P, HID])
        w2 = sb(b6, "w2", [P, NF, D])
        b1c = sb(b6, "b1c", [P, NF])
        row6 = {n: sb(b6, "row6_" + n, [P, D]) for n in ("b2", "g_norm_out", "b_norm_out")}
        hid = sb(b6, "hid", [P, NB, NF, TB])
        yo = sb(b6, "yo", [P, NT, D])
        with nc.Block() as block:
            @block.sync
            def _(sp):
                sp.dma_start(w1[:, :], A["L0_xattn_W1"]).then_inc(S("b6_in"), 16)
                sp.dma_start(w2[:, :, :], A["L0_xattn_W2"].rearrange("(f p) d -> p f d", p=P)).then_inc(S("b6_in"), 16)
                sp.dma_start(b1c[:, :], A["L0_xattn_b1"].rearrange("(f p) -> p f", p=P),
                             allow_slow_non_contiguous=True).then_inc(S("b6_in"), 16)
                for n, tile in row6.items():
                    sp.dma_start(tile[:, :], A["L0_xattn_" + n].partition_broadcast(P)).then_inc(S("b6_in"), 16)
                sp.dma_start(gates[:, 0:2], A["g_xattn"].partition_broadcast(P)).then_inc(S("b6_in"), 16)
                sp.dma_start(gates[:, 2:4], A["g_ffn"].partition_broadcast(P)).then_inc(S("b6_in"), 16)

            @block.tensor
            def _(pe):
                pe.wait_ge(S("b6_in"), 16 * 8)
                for tb in range(NB):
                    for f in range(NF):
                        if tb:
                            pe.wait_ge(S("hid6"), (tb - 1) * NF + f + 1)
                        M.matmul(ps[:, f, :], w1[:, f * P:(f + 1) * P], wT[:, tb * TB:(tb + 1) * TB],
                                 start=True, stop=True).then_inc(S("hid6_ps"), 1)
                for t in range(NT):
                    pe.wait_ge(S("hid6"), (t // 4 + 1) * NF)
                    for f in range(NF):
                        last = M.matmul(ps[:, 4 + t // 4, (t % 4) * P:(t % 4 + 1) * P],
                                        hid[:, t // 4, f, (t % 4) * P:(t % 4 + 1) * P], w2[:, f, :],
                                        start=f == 0, stop=f == NF - 1)
                last.then_inc(S("out6_ps"), 1)
                pe.wait_ge(S("xn6"), NT)
                transpose_tiles(xn, 0, S("xn6T_ps"))

            @block.scalar
            def _(act):
                act.wait_ge(S("b6_in"), 16 * 8)
                C.activation(gt[:, :], gates[:, :], ACT.Tanh).then_inc(S("gt_ready"), 1)
                for u in range(NB * NF):
                    act.wait_ge(S("hid6_ps"), u + 1)
                    C.activation(hid[:, u // NF, u % NF, :], ps[:, u % NF, :], ACT.Gelu,
                                 bias=b1c[:, u % NF:u % NF + 1]).then_inc(S("hid6"), 1)
                ln_sqrt(1, S("ln_o_var"), S("ln_o_sd"))
                ln_sqrt(1, S("ln_x1_var"), S("ln_x1_sd"))
                act.wait_ge(S("xn6T_ps"), 1)
                C.copy(wT[:, :], flat(ps[:, 0:2, :])).then_inc(S("wT6"), 1)

            @block.vector
            def _(dve):
                w = lambda t: t[:, :, :]
                dve.wait_ge(S("b6_in"), 16 * 8)
                dchain(V.tensor_tensor(w(xt), w(xt), every_tile(row6["b2"]), ALU.add))
                dve.wait_ge(S("out6_ps"), 1)
                dchain(V.tensor_tensor(w(xt), ps[:, 4:6, :].rearrange("p a (b d) -> p (a b) d", d=D), w(xt), ALU.add))
                ln_stats(xt, S("ln_o_var"))
                ln_apply(yo, xt, S("ln_o_sd"), 1, S("yo_ready"))
                dve.wait_ge(S("yo_ready"), NT)
                dchain(V.tensor_tensor(w(yo), w(yo), every_tile(row6["g_norm_out"]), ALU.mult))
                dchain(V.tensor_tensor(w(yo), w(yo), every_tile(row6["b_norm_out"]), ALU.add))
                dve.wait_ge(S("gt_ready"), 1)
                dchain(V.scalar_tensor_tensor(flat(x_sb), flat(yo), gt[:, 0:1], flat(x_sb), ALU.mult, ALU.add))
                ln_stats(x_sb, S("ln_x1_var"))
                ln_apply(xn, x_sb, S("ln_x1_sd"), 1, S("xn6"))

    q1s = ExitStack()
    Q1 = sb(q1s, "Q1", [P, H1, T], BF16)
    Q1v = Q1[:, :, :].rearrange("p (j a) t -> p j a t", a=2)
    ROW1 = 6 * DH1
    with ExitStack() as b7:
        u1 = sb(b7, "u1", [P, RANK])
        v1w = sb(b7, "v1w", [RANK, HID])
        b1c = sb(b7, "b1c7", [P, NF])
        u2 = sb(b7, "u2", [P, NF, RANK])
        v2w = sb(b7, "v2w", [RANK, D])
        b2r = sb(b7, "b2r7", [P, D])
        lowT = sb(b7, "lowT", [RANK, T])
        lowT2 = sb(b7, "lowT2", [RANK, T])
        hid = sb(b7, "hid7", [P, NB, NF, TB])
        yo = sb(b7, "yo7", [P, NT, D])
        wq1 = sb(b7, "wq1", [P, P])
        bq1 = sb(b7, "bq1", [P, 1])
        bq1s = sb(b7, "bq1s", [P, 1])
        qs = sb(b7, "qs7", [P, T])
        ql = sb(b7, "ql7", [P, LEVELS, T], BF16)
        qabs, bound = sb(b7, "qabs", [P, 1]), sb(b7, "bound", [P, 1])
        boundh, bound1 = sb(b7, "boundh", [1, H1]), sb(b7, "bound1", [1, 1])
        SC1 = float(DH1) ** -0.5
        with nc.Block() as block:
            @block.sync
            def _(sp):
                for dst, name in ((u1, "L0_ffn_U1"), (v1w, "L0_ffn_V1"), (v2w, "L0_ffn_V2"), (wq1, "L1_xattn_wq")):
                    sp.dma_start(dst[:, :], A[name]).then_inc(S("b7_in"), 16)
                sp.dma_start(u2[:, :, :], A["L0_ffn_U2"].rearrange("(f p) r -> p f r", p=P)).then_inc(S("b7_in"), 16)
                sp.dma_start(b1c[:, :], A["L0_ffn_b1"].rearrange("(f p) -> p f", p=P),
                             allow_slow_non_contiguous=True).then_inc(S("b7_in"), 16)
                sp.dma_start(bq1[:, :], A["L1_xattn_bq"].rearrange("(p a) -> p a", a=1)).then_inc(S("b7_in"), 16)
                sp.dma_start(b2r[:, :], A["L0_ffn_b2"].partition_broadcast(P)).then_inc(S("b7_in"), 16)
                sp.wait_ge(S("q1_split"), 1)
                sp.dma_start(q1_parts.rearrange("l p t -> p l t"), ql[:, :, :]).then_inc(S("q1_out"), 16)
                sp.wait_ge(S("q1_out"), 16)
                sp.wait_ge(S("q1_zero"), 1)
                for par in range(2):
                    r0 = 64 * par
                    for r, lv in enumerate((0, 0, 0, 1, 1, 2)):
                        sp.dma_start(Q1v[r0 + DH1 * r:r0 + DH1 * (r + 1), :, par, :],
                                     q1_parts[lv].rearrange("(j a d) t -> d j a t", a=2, d=DH1)[:, :, par, :])\
                          .then_inc(S("q1_gathered"), 16)
                    sp.dma_start(Q1v[r0 + ROW1 + LEVELS:r0 + ROW1 + LEVELS + 1, :, par, :],
                                 mask_line[2:3, 0:T].unsqueeze(1).to_broadcast([1, H1 // 2, T]))\
                        .then_inc(S("q1_gathered"), 16)
                sp.wait_ge(S("q1_gathered"), 16 * 14)

            @block.gpsimd
            def _(pool):
                PL.memset(Q1[:, :, :], 0.0).then_inc(S("q1_zero"), 1)

            @block.tensor
            def _(pe):
                pe.wait_ge(S("b7_in"), 16 * 8)
                for tb in range(NB):
                    last = M.matmul(ps[0:RANK, 6 + tb, :], u1[:, :], wT[:, tb * TB:(tb + 1) * TB], start=True, stop=True)
                last.then_inc(S("low_ps"), 1)
                pe.wait_ge(S("low_sb"), 1)
                for tb in range(NB):
                    for f in range(NF):
                        if tb:
                            pe.wait_ge(S("hid7"), (tb - 1) * NF + f + 1)
                        M.matmul(ps[:, f, :], v1w[:, f * P:(f + 1) * P], lowT[:, tb * TB:(tb + 1) * TB],
                                 start=True, stop=True).then_inc(S("hid7_ps"), 1)
                for tb in range(NB):
                    pe.wait_ge(S("hid7"), (tb + 1) * NF)
                    for f in range(NF):
                        last = M.matmul(ps[0:RANK, 6 + tb, :], u2[:, f, :], hid[:, tb, f, :], start=f == 0, stop=f == NF - 1)
                last.then_inc(S("low_ps"), 1)
                pe.wait_ge(S("low_sb"), 2)
                for t in range(NT):
                    last = M.matmul(ps[:, 4 + t // 4, (t % 4) * P:(t % 4 + 1) * P], lowT2[:, t * P:(t + 1) * P], v2w[:, :],
                                    start=True, stop=True)
                last.then_inc(S("out7_ps"), 1)
                pe.wait_ge(S("xn7"), NT)
                transpose_tiles(xn, 0, S("xn7T_ps"))
                pe.wait_ge(S("wT7"), 1)
                for tb in range(NB):
                    last = M.matmul(ps[:, 2 + tb, :], wq1[:, :], wT[:, tb * TB:(tb + 1) * TB], start=True, stop=True)
                last.then_inc(S("q1_ps"), 1)
                pe.wait_ge(S("bound_ready"), 1)
                M.matmul(ps[0:1, 6, 0:P], bound[:, :], ident[:, :], start=True, stop=True).then_inc(S("bound_ps"), 1)

            @block.scalar
            def _(act):
                act.wait_ge(S("low_ps"), 1)
                C.copy(lowT[:, :], flat(ps[0:RANK, 6:8, :])).then_inc(S("low_sb"), 1)
                for u in range(NB * NF):
                    act.wait_ge(S("hid7_ps"), u + 1)
                    C.activation(hid[:, u // NF, u % NF, :], ps[:, u % NF, :], ACT.Gelu_apprx_tanh,
                                 bias=b1c[:, u % NF:u % NF + 1]).then_inc(S("hid7"), 1)
                act.wait_ge(S("low_ps"), 2)
                C.copy(lowT2[:, :], flat(ps[0:RANK, 6:8, :])).then_inc(S("low_sb"), 1)
                ln_sqrt(1, S("ln_x2_var"), S("ln_x2_sd"))
                act.wait_ge(S("xn7T_ps"), 1)
                C.copy(wT[:, :], flat(ps[:, 0:2, :])).then_inc(S("wT7"), 1)
                act.wait_ge(S("q1_ps"), 1)
                act.wait_ge(S("bq1s"), 1)
                C.activation(qs[:, :], flat(ps[:, 2:4, :]), ACT.Identity, bias=bq1s[:, 0:1], scale=SC1).then_inc(S("q1_sb"), 1)

            @block.vector
            def _(dve):
                w = lambda t: t[:, :, :]
                dve.wait_ge(S("b7_in"), 16 * 8)
                V.tensor_scalar(bq1s[:, :], bq1[:, :], SC1, None, ALU.mult).then_inc(S("bq1s"), 1)
                dve.wait_ge(S("out7_ps"), 1)
                dchain(V.tensor_tensor(w(yo), ps[:, 4:6, :].rearrange("p a (b d) -> p (a b) d", d=D), every_tile(b2r), ALU.add))
                dchain(V.scalar_tensor_tensor(flat(x_sb), flat(yo), gt[:, 2:3], flat(x_sb), ALU.mult, ALU.add))
                ln_stats(x_sb, S("ln_x2_var"))
                ln_apply(xn, x_sb, S("ln_x2_sd"), 1, S("xn7"))
                dve.wait_ge(S("q1_sb"), 1)
                dchain(V.tensor_reduce(qabs[:, :], qs[:, :], AX.X, ALU.max, apply_absolute_value=True))
                dchain(V.reduce_max(kabs1[:, :], kabs[:, :], AX.X))
                V.tensor_tensor(bound[:, :], qabs[:, :], kabs1[:, :], ALU.mult).then_inc(S("bound_ready"), 1)
                dchain(V.tensor_copy(ql[:, 0, :], qs[:, :]))
                dchain(V.tensor_tensor(qs[:, :], qs[:, :], ql[:, 0, :], ALU.subtract))
                dchain(V.tensor_copy(ql[:, 1, :], qs[:, :]))
                V.tensor_tensor(ql[:, 2, :], qs[:, :], ql[:, 1, :], ALU.subtract).then_inc(S("q1_split"), 1)
                dve.wait_ge(S("bound_ps"), 1)
                dchain(V.reduce_sum(boundh[:, :], ps[0:1, 6, 0:P].rearrange("p (h d) -> p h d", d=DH1), AX.X))
                dchain(V.reduce_max(bound1[:, :], boundh[:, :], AX.X))
                dchain(V.tensor_scalar(bound1[:, :], bound1[:, :], EXP_RANGE, None, ALU.is_gt))
                dchain(V.tensor_copy(general[0:1, 1:2], bound1[:, :]))

    l1_general = nc.values_load(general[0:1, 1:2], min_val=0, max_val=1)
    with nc.If(l1_general > 0):
        with ExitStack() as b7g:
            K1g = sb(b7g, "K1g", [P, H1 // 2, GP], BF16)
            gmax = sb(b7g, "gmax", [P, 16])
            nshift = sb(b7g, "nshift", [P, H1 * NT])
            nsT = sb(b7g, "nsT", [P, P])
            nsR = sb(b7g, "nsR", [P, P])
            nsl = sb(b7g, "nsl", [P, LEVELS, P], BF16)
            NBK = -(-GP // 512)
            BANKS = 7
            gchain = Chain(V, S("g1_chain"))
            with nc.Block() as block:
                @block.gpsimd
                def _(pool):
                    PL.memset(K1g[:, :, :], 0.0).then_inc(S("k1g_zero"), 1)

                @block.sync
                def _(sp):
                    sp.wait_ge(S("k1g_zero"), 1)
                    for par in range(2):
                        for r, lv in enumerate((0, 1, 2, 0, 1, 0)):
                            r0 = 64 * par + DH1 * r
                            src = k1_parts[lv].rearrange("(j a d) g -> d j a g", a=2, d=DH1)
                            sp.dma_start(K1g[r0:r0 + DH1, :, :], src[:, :, par, :]).then_inc(S("k1g_in"), 16)
                        r0 = 64 * par + ROW1 + LEVELS
                        sp.dma_start(K1g[r0:r0 + 1, :, :], mask_line[1:2, :].unsqueeze(1)
                                     .to_broadcast([1, H1 // 2, GP])).then_inc(S("k1g_in"), 16)
                    sp.wait_ge(S("nsl_ready"), 1)
                    sp.dma_start(ns_lines.rearrange("l (i p) -> i l p", p=P), nsl[:, :, :]).then_inc(S("ns_out"), 16)
                    sp.wait_ge(S("ns_out"), 16)
                    for par in range(2):
                        r0 = 64 * par + ROW1
                        sp.dma_start(Q1v[r0:r0 + LEVELS, :, par, :],
                                     ns_lines.rearrange("l (j a t) -> l j a t", a=2, t=T)[:, :, par, :])\
                            .then_inc(S("ns_in"), 16)
                    sp.wait_ge(S("ns_in"), 32)

                @block.tensor
                def _(pe):
                    pe.wait_ge(S("k1g_in"), 16 * 14)
                    with pe.Fori(0, H1 * NT) as i:
                        for j in range(NBK):
                            w = min(512, GP - j * 512)
                            used = j - BANKS if j >= BANKS else (j + BANKS - NBK if j + BANKS < NBK else j - NBK)
                            pe.wait_ge(S("g1_read"), i * NBK + NBK + used + 1)
                            M.matmul(ps[:, j % BANKS, 0:w],
                                     Q1[:, :, :].rearrange("p h t -> p (h t)")[:, bass.ds(i * P, P)],
                                     K1g[:, :, :].rearrange("p j g -> p (j g)")[:, bass.ds((i // (2 * NT)) * GP + j * 512, w)],
                                     start=True, stop=True).then_inc(S("g1_scored"), 1)
                    pe.wait_ge(S("nshift_ready"), 1)
                    M.transpose(ps[:, 7, 0:P], nshift[:, :], ident[:, :]).then_inc(S("nsT_ps"), 1)

                @block.scalar
                def _(act):
                    act.wait_ge(S("nsT_ps"), 1)
                    C.copy(nsT[:, :], ps[:, 7, 0:P]).then_inc(S("nsT_sb"), 1)

                @block.vector
                def _(dve):
                    dve.sem_inc(S("g1_read"), NBK)
                    with dve.Fori(0, H1 * NT) as i:
                        gchain.loop(i, 1)
                        for j in range(NBK):
                            w = min(512, GP - j * 512)
                            dve.wait_ge(S("g1_scored"), i * NBK + j + 1)
                            V.reduce_max(gmax[:, j:j + 1], ps[:, j % BANKS, 0:w], AX.X).then_inc(S("g1_read"), 1)
                        dve.wait_ge(S("g1_read"), i * NBK + NBK + NBK)
                        gchain(V.reduce_max(nshift[:, bass.ds(i, 1)], gmax[:, 0:NBK], AX.X))
                    gchain.looped(1, H1 * NT)
                    V.tensor_scalar(nshift[:, :], nshift[:, :], -1.0, None, ALU.mult).then_inc(S("nshift_ready"), 1)
                    dve.wait_ge(S("nsT_sb"), 1)
                    gchain(V.tensor_copy(nsl[:, 0, :], nsT[:, :]))
                    gchain(V.tensor_tensor(nsR[:, :], nsT[:, :], nsl[:, 0, :], ALU.subtract))
                    gchain(V.tensor_copy(nsl[:, 1, :], nsR[:, :]))
                    V.tensor_tensor(nsl[:, 2, :], nsR[:, :], nsl[:, 1, :], ALU.subtract).then_inc(S("nsl_ready"), 1)

    next_stage()

    NQ = H1 // 4
    oq = ExitStack()
    o1 = sb(oq, "o1", [P, NQ, T])
    with ExitStack() as b8:
        K1 = sb(b8, "K1", [P, 2, 2, GP], BF16)
        V1 = sb(b8, "V1", [P, 2, NG, 4 * VW])
        vs1 = sb(b8, "vs1", [P, UNROLL, 4, 32])
        ex1 = sb(b8, "ex1", [P, 2 * UNROLL, 2, TB])
        UNITS = 2 * UNROLL
        RING = 3
        NPASS = NQ * NB
        with nc.Block() as block:
            @block.gpsimd
            def _(pool):
                for r in range(2):
                    PL.memset(K1[:, r, :, :], 0.0).then_inc(S("k1_zero"), 1)
                    pool.wait_ge(S("k1_zero"), r + 1)
                PL.memset(vs1[:, :, :, :], 0.0).then_inc(S("vs1_zero"), 1)
                pool.wait_ge(S("vs1_zero"), 1)

                for w in range(NPASS):
                    quad, tb = divmod(w, NB)
                    pool.wait_ge(S(f"v1_in{quad % 2}"), 16 * (quad // 2 + 1))

                    def place(k, g, n, first):
                        if not first:
                            pool.wait_ge(S("summed1"), n - UNROLL + 1)
                        PL.tensor_copy(vs1[:, k, :, 0:VW].unsqueeze(1),
                                       V1[:, quad % 2, bass.ds(g, 1), :].rearrange("p c (h v) -> p c h v", v=VW))\
                            .then_inc(S("v1_placed"), 1)

                    for k in range(UNROLL):
                        place(k, k, w * NG + k, w == 0)
                    with pool.Fori(1, TURNS) as i:
                        for k in range(UNROLL):
                            place(k, i * UNROLL + k, i * UNROLL + (w * NG + k), False)

            @block.sync
            def _(sp):
                for quad in range(NQ):
                    b = quad % 2
                    if quad >= 2:
                        sp.wait_ge(S("scored1"), (quad - 1) * NB * 2 * NG)
                        sp.wait_ge(S("v1_placed"), (quad - 1) * NB * NG)
                    else:
                        sp.wait_ge(S("k1_zero"), quad + 1)
                        for par in range(2):
                            r0 = 64 * par + ROW1
                            for pr in range(2):
                                sp.dma_start(K1[r0:r0 + LEVELS, b, pr, :], mask_line[2, :].partition_broadcast(LEVELS))\
                                    .then_inc(S(f"k1_in{b}"), 16)
                                sp.dma_start(K1[r0 + LEVELS:r0 + LEVELS + 1, b, pr, :], mask_line[1:2, :])\
                                    .then_inc(S(f"k1_in{b}"), 16)
                    for par in range(2):
                        for r, lv in enumerate((0, 1, 2, 0, 1, 0)):
                            r0 = 64 * par + DH1 * r
                            src = k1_parts[lv].rearrange("(q j a d) g -> q d j a g", j=2, a=2, d=DH1)
                            sp.dma_start(K1[r0:r0 + DH1, b, :, :], src[quad, :, :, par, :]).then_inc(S(f"k1_in{b}"), 16)
                    sp.dma_start(V1[:, b, :, :], v1_rows[:, :, quad * 4 * VW:(quad + 1) * 4 * VW])\
                        .then_inc(S(f"v1_in{b}"), 16)

            KIN0, KIN = 8 + 12, 12

            @block.tensor
            def _(pe):
                pe.wait_ge(S("vs1_zero"), 1)
                for w in range(NPASS):
                    quad, tb = divmod(w, NB)
                    U0, G0 = w * 2 * NG, w * NG
                    pe.wait_ge(S(f"k1_in{quad % 2}"), 16 * (KIN0 + KIN * (quad // 2)))

                    def scores(k, g, free):
                        if free is not None:
                            pe.wait_ge(S("exped1"), free)
                        for hh in range(2):
                            last = M.matmul(ps[:, 2 * (k % RING) + hh, :], K1[:, quad % 2, k % 2, bass.ds(g * P, P)],
                                            Q1[:, 4 * quad + 2 * (k % 2) + hh, tb * TB:(tb + 1) * TB], start=True, stop=True)
                        last.then_inc(S("scored1"), 1)

                    def values(t, n, start, stop):
                        pe.wait_ge(S("exped1"), 2 * n + 2)
                        pe.wait_ge(S("v1_placed"), n + 1)
                        if start and w >= 2:
                            pe.wait_ge(S("o1_read"), w - 1)
                        for j in range(4):
                            last = M.matmul(ps[32 * j:32 * j + 32, 6 + w % 2, :], vs1[:, t, j, :],
                                            ex1[:, 2 * t + j // 2, j % 2, :], start=start, stop=stop,
                                            tile_position=(0, 32 * j))
                        last.then_inc(S("summed1"), 1)

                    def turn(i, first=False, last=False):
                        for t in range(UNROLL):
                            for q in range(2):
                                k = 2 * t + q
                                free = None if first and w == 0 and k < RING else i * UNITS + (U0 + k - RING + 1)
                                scores(k, i * UNROLL + t, free)
                            if not (first and t == 0):
                                n = i * UNROLL + (G0 + t - 1)
                                values((t - 1) % UNROLL, n, first and t == 1, False)
                        if last:
                            values(UNROLL - 1, i * UNROLL + (G0 + UNROLL - 1), False, True)

                    turn(0, first=True)
                    with pe.Fori(1, TURNS - 1) as i:
                        turn(i)
                    turn(TURNS - 1, last=True)

            @block.scalar
            def _(act):
                for w in range(NPASS):
                    U0, G0 = w * 2 * NG, w * NG

                    def unit(k, i, first):
                        act.wait_ge(S("scored1"), i * UNITS + (U0 + k + 1))
                        if not first:
                            act.wait_ge(S("summed1"), i * UNROLL + (G0 + k // 2 - UNROLL + 1))
                        C.activation(ex1[:, k, :, :], ps[:, 2 * (k % RING):2 * (k % RING) + 2, :], ACT.Exp)\
                            .then_inc(S("exped1"), 1)

                    for k in range(UNITS):
                        unit(k, 0, w == 0)
                    with act.Fori(1, TURNS) as i:
                        for k in range(UNITS):
                            unit(k, i, False)

            @block.vector
            def _(dve):
                for w in range(NPASS):
                    quad, tb = divmod(w, NB)
                    dve.wait_ge(S("summed1"), (w + 1) * NG)
                    V.tensor_copy(o1[:, quad, tb * TB:(tb + 1) * TB], ps[:, 6 + w % 2, :]).then_inc(S("o1_read"), 1)

    with ExitStack() as b9:
        wo = sb(b9, "wo", [P, D])
        bo = sb(b9, "bo", [P, D])
        rs = sb(b9, "rs", [P, NT, H1])
        on = sb(b9, "on", [P, NT, H1, DH1])
        onT = sb(b9, "onT", [P, T])
        yo = sb(b9, "yo9", [P, NT, D])
        with nc.Block() as block:
            @block.sync
            def _(sp):
                sp.dma_start(wo[:, :], A["L1_xattn_wo"]).then_inc(S("b9_in"), 16)
                sp.dma_start(bo[:, :], A["L1_xattn_bo"].partition_broadcast(P)).then_inc(S("b9_in"), 16)

            @block.tensor
            def _(pe):
                for t in range(NT):
                    for quad in range(NQ):
                        last = M.transpose(ps[:, t, quad * P:(quad + 1) * P], o1[:, quad, t * P:(t + 1) * P], ident[:, :])
                    last.then_inc(S("o1T_ps"), 1)
                pe.wait_ge(S("on_ready"), NT)
                for t in range(NT):
                    last = M.transpose(ps[:, t // 4, (t % 4) * P:(t % 4 + 1) * P],
                                       on[:, t, :, :].rearrange("p h v -> p (h v)"), ident[:, :])
                last.then_inc(S("onT_ps"), 1)
                pe.wait_ge(S("onT"), 1)
                pe.wait_ge(S("b9_in"), 32)
                for t in range(NT):
                    last = M.matmul(ps[:, 4 + t // 4, (t % 4) * P:(t % 4 + 1) * P], onT[:, t * P:(t + 1) * P], wo[:, :],
                                    start=True, stop=True)
                last.then_inc(S("out9_ps"), 1)
                pe.wait_ge(S("xn9"), NT)
                transpose_tiles(xn, 0, S("xn9T_ps"))

            @block.scalar
            def _(act):
                act.wait_ge(S("onT_ps"), 1)
                C.copy(onT[:, :], flat(ps[:, 0:2, :])).then_inc(S("onT"), 1)
                ln_sqrt(1, S("ln_x3_var"), S("ln_x3_sd"))
                act.wait_ge(S("xn9T_ps"), 1)
                C.copy(wT[:, :], flat(ps[:, 0:2, :])).then_inc(S("wT9"), 1)

            @block.vector
            def _(dve):
                for t in range(NT):
                    dve.wait_ge(S("o1T_ps"), t + 1)
                    rows_ = ps[:, t, :].rearrange("p (h v) -> p h v", v=32)
                    dchain(V.reciprocal(rs[:, t, :], rows_[:, :, DH1]))
                    V.tensor_tensor(on[:, t, :, :], rows_[:, :, 0:DH1],
                                    rs[:, t, :].unsqueeze(2).to_broadcast([P, H1, DH1]), ALU.mult).then_inc(S("on_ready"), 1)
                w = lambda t: t[:, :, :]
                dve.wait_ge(S("b9_in"), 32)
                dve.wait_ge(S("out9_ps"), 1)
                dchain(V.tensor_tensor(w(yo), ps[:, 4:6, :].rearrange("p a (b d) -> p (a b) d", d=D), every_tile(bo), ALU.add))
                dchain(V.scalar_tensor_tensor(flat(x_sb), flat(yo), gt[:, 1:2], flat(x_sb), ALU.mult, ALU.add))
                ln_stats(x_sb, S("ln_x3_var"))
                ln_apply(xn, x_sb, S("ln_x3_sd"), 1, S("xn9"))
    oq.close()
    q1s.close()

    next_stage()

    with ExitStack() as b10:
        gw = sb(b10, "gw", [P, E])
        gb = sb(b10, "gb", [P, E])
        w1 = sb(b10, "w1m", [P, E, HID])
        w2 = sb(b10, "w2m", [P, E, NF, D])
        b1c = sb(b10, "b1m", [P, E, NF])
        b2e = sb(b10, "b2m", [E, D])
        sel = sb(b10, "sel", [E, E, P])
        lg, lw = sb(b10, "lg", [P, NT, E]), sb(b10, "lw", [P, NT, E])
        t8 = sb(b10, "t8", [P, NT, 8])
        i8 = sb(b10, "i8", [P, NT, 8], U32)
        i8f = sb(b10, "i8f", [P, NT, 2])
        experts = sb(b10, "experts", [P, E])
        keep, keep2 = sb(b10, "keep", [P, NT, E]), sb(b10, "keep2", [P, NT, E])
        pr = sb(b10, "pr", [P, NT, E])
        psum_ = sb(b10, "psm", [P, NT])
        pT = sb(b10, "pT", [E, T])
        hid = sb(b10, "hidm", [P, 2, NF, TB])
        hidp = sb(b10, "hidp", [P, 2, NF, TB])
        oT = sb(b10, "oT", [P, T])
        oo = sb(b10, "oo", [P, NT, D])
        row10 = {n: sb(b10, "row10_" + n, [P, D]) for n in ("ln_g", "ln_b")}
        NJ = E * NB
        with nc.Block() as block:
            @block.sync
            def _(sp):
                sp.dma_start(gw[:, :], A["L1_ffn_gate_w"]).then_inc(S("b10_in"), 16)
                sp.dma_start(gb[:, :], A["L1_ffn_gate_b"].partition_broadcast(P)).then_inc(S("b10_in"), 16)
                sp.dma_start(experts[:, :], A["steps"][0:E].partition_broadcast(P)).then_inc(S("b10_in"), 16)
                sp.dma_start(b2e[:, :], A["L1_ffn_b2"]).then_inc(S("b10_in"), 16)
                sp.dma_start(sel[:, :, :], A["select"]).then_inc(S("b10_in"), 16)
                for e in range(E):
                    sp.dma_start(b1c[:, e, :], A["L1_ffn_b1"][e].rearrange("(f p) -> p f", p=P),
                                 allow_slow_non_contiguous=True).then_inc(S("b10_in"), 16)
                for n, tile in row10.items():
                    sp.dma_start(tile[:, :], A["L1_ffn_" + n].partition_broadcast(P)).then_inc(S("b10_in"), 16)
                sp.dma_start(w1[:, :, :], A["L1_ffn_w1"].rearrange("e d f -> d e f")).then_inc(S("b10_in"), 16)
                sp.dma_start(w2[:, :, :, :].rearrange("p e f d -> p (e f) d"),
                             A["L1_ffn_w2"].rearrange("e (f p) d -> p (e f) d", p=P)).then_inc(S("b10_in"), 16)
                sp.wait_ge(S("x4_ready"), 1)
                sp.dma_start(A["out"][0].rearrange("(n p) d -> p n d", p=P), x_sb[:, :, :]).then_inc(S("stored"), 16)
                sp.wait_ge(S("stored"), 16)

            NIN = 5 + E + 2 + 2

            @block.tensor
            def _(pe):
                pe.wait_ge(S("b10_in"), 16 * NIN)
                for t in range(NT):
                    last = M.matmul(ps[:, 0, t * E:(t + 1) * E], wT[:, t * P:(t + 1) * P], gw[:, :], start=True, stop=True)
                last.then_inc(S("logits_ps"), 1)

                def hidden(j):
                    e, tb = divmod(j, NB)
                    for f in range(NF):
                        if j:
                            pe.wait_ge(S("hidm"), (j - 1) * NF + f + 1)
                        elif f == 0:
                            pe.wait_ge(S("logits_read"), 1)
                        M.matmul(ps[:, f, :], w1[:, e, f * P:(f + 1) * P], wT[:, tb * TB:(tb + 1) * TB],
                                 start=True, stop=True).then_inc(S("hidm_ps"), 1)

                def share(j):
                    e, tb = divmod(j, NB)
                    if j >= 2:
                        pe.wait_ge(S("hidp"), j - 1)
                    M.matmul(ps[:, 4 + j % 2, :], sel[:, e, :], pT[:, tb * TB:(tb + 1) * TB], start=True, stop=True)\
                        .then_inc(S("share_ps"), 1)

                hidden(0)
                pe.wait_ge(S("pr_ready"), 1)
                for t in range(NT):
                    last = M.transpose(ps[0:E, 4 + t // 4, (t % 4) * P:(t % 4 + 1) * P], pr[:, t, :], ident[:, :])
                last.then_inc(S("pT_ps"), 1)
                pe.wait_ge(S("pT_ready"), 1)
                share(0)
                for j in range(NJ):
                    e, tb = divmod(j, NB)
                    if j + 1 < NJ:
                        hidden(j + 1)
                        share(j + 1)
                    pe.wait_ge(S("hidp"), j + 1)
                    for f in range(NF):
                        M.matmul(ps[:, 6 + tb, :], w2[:, e, f, :], hidp[:, j % 2, f, :], start=e == 0 and f == 0, stop=False)\
                            .then_inc(S("outm"), 1)
                for tb in range(NB):
                    last = M.matmul(ps[:, 6 + tb, :], b2e[:, :], pT[:, tb * TB:(tb + 1) * TB], start=False, stop=True)
                last.then_inc(S("oT_ps"), 1)
                pe.wait_ge(S("oT"), 1)
                for t in range(NT):
                    last = M.transpose(ps[:, 4 + t // 4, (t % 4) * P:(t % 4 + 1) * P], oT[:, t * P:(t + 1) * P], ident[:, :])
                last.then_inc(S("oo_ps"), 1)

            @block.scalar
            def _(act):
                act.wait_ge(S("b10_in"), 16 * NIN)
                act.wait_ge(S("lw_ready"), 1)
                C.activation(pr[:, :, :], lw[:, :, :], ACT.Exp).then_inc(S("pr_exp"), 1)
                act.wait_ge(S("pT_ps"), 1)
                C.copy(pT[:, :], flat(ps[0:E, 4:6, :])).then_inc(S("pT_ready"), 1)
                for j in range(NJ):
                    e, tb = divmod(j, NB)
                    for f in range(NF):
                        act.wait_ge(S("hidm_ps"), j * NF + f + 1)
                        if j >= 2:
                            act.wait_ge(S("hidp"), j - 1)
                        C.activation(hid[:, j % 2, f, :], ps[:, f, :], ACT.Gelu, bias=b1c[:, e, f:f + 1]).then_inc(S("hidm"), 1)
                act.wait_ge(S("oT_ps"), 1)
                C.copy(oT[:, :], flat(ps[:, 6:8, :])).then_inc(S("oT"), 1)
                ln_sqrt(1, S("ln_m_var"), S("ln_m_sd"))

            @block.vector
            def _(dve):
                w = lambda t: t[:, :, :]
                over_e = lambda t: t.unsqueeze(2).to_broadcast([P, NT, E])
                dve.wait_ge(S("b10_in"), 16 * NIN)
                dve.wait_ge(S("logits_ps"), 1)
                dchain(V.tensor_tensor(w(lg), ps[:, 0, 0:NT * E].rearrange("p (t e) -> p t e", e=E),
                                       gb[:, :].unsqueeze(1).to_broadcast([P, NT, E]), ALU.add))
                V.tensor_scalar(w(lg), w(lg), float(1 / 0.9), None, ALU.mult).then_inc(S("logits_read"), 1)
                dve.wait_ge(S("logits_read"), 1)
                for t in range(NT):
                    V.max(t8[:, t, :], lg[:, t, :]).then_inc(S("t8"), 1)
                dve.wait_ge(S("t8"), NT)
                V.tensor_tensor(w(lw), w(lg), over_e(t8[:, :, 0]), ALU.subtract).then_inc(S("lw_ready"), 1)
                for t in range(NT):
                    V.max_index(i8[:, t, :], t8[:, t, :], lg[:, t, :]).then_inc(S("i8"), 1)
                dve.wait_ge(S("i8"), NT)
                dchain(V.tensor_copy(w(i8f), i8[:, :, 0:2]))
                each = experts[:, :].unsqueeze(1).to_broadcast([P, NT, E])
                dchain(V.tensor_tensor(w(keep), each, over_e(i8f[:, :, 0]), ALU.is_equal))
                dchain(V.tensor_tensor(w(keep2), each, over_e(i8f[:, :, 1]), ALU.is_equal))
                dchain(V.tensor_tensor(w(keep), w(keep), w(keep2), ALU.add))
                dve.wait_ge(S("pr_exp"), 1)
                dchain(V.tensor_tensor(w(pr), w(pr), w(keep), ALU.mult))
                dchain(V.reduce_sum(psum_[:, :], w(pr), AX.X))
                dchain(V.reciprocal(psum_[:, :], psum_[:, :]))
                V.tensor_tensor(w(pr), w(pr), over_e(psum_[:, :]), ALU.mult).then_inc(S("pr_ready"), 1)
                for j in range(NJ):
                    dve.wait_ge(S("share_ps"), j + 1)
                    dve.wait_ge(S("hidm"), (j + 1) * NF)
                    if j >= 2:
                        dve.wait_ge(S("outm"), (j - 1) * NF)
                    V.tensor_tensor(hidp[:, j % 2, :, :], hid[:, j % 2, :, :],
                                    ps[:, 4 + j % 2, :].unsqueeze(1).to_broadcast([P, NF, TB]), ALU.mult).then_inc(S("hidp"), 1)
                dve.wait_ge(S("oo_ps"), 1)
                dchain(V.tensor_copy(w(oo), ps[:, 4:6, :].rearrange("p a (b d) -> p (a b) d", d=D)))
                ln_stats(oo, S("ln_m_var"))
                ln_apply(xn, oo, S("ln_m_sd"), 1, S("xn10"))
                dve.wait_ge(S("xn10"), NT)
                dchain(V.tensor_tensor(w(xn), w(xn), every_tile(row10["ln_g"]), ALU.mult))
                dchain(V.tensor_tensor(w(xn), w(xn), every_tile(row10["ln_b"]), ALU.add))
                V.scalar_tensor_tensor(flat(x_sb), flat(xn), gt[:, 3:4], flat(x_sb), ALU.mult, ALU.add).then_inc(S("x4_ready"), 1)

    next_stage()


def constants():
    n = 2 * P
    om = 2 * np.pi * (np.arange(P) + 0.5) / n
    j = np.arange(P)
    fx = np.exp(-1j * np.outer(j, om))
    fk1 = np.exp(-1j * np.outer(P - 1 + j, om))
    fk0 = np.exp(-1j * np.outer(j - 1, om))
    fk0[0] = 0
    inv = np.exp(1j * np.outer(om, P - 1 + j)) / P
    dft = np.stack([fx.real, fx.imag, fk0.real, fk0.imag, fk1.real, fk1.imag, inv.real, -inv.real, -inv.imag], axis=1)
    return {"ident": np.eye(P, dtype=np.float32), "steps": np.arange(KTAP, dtype=np.float32),
            "select": np.ascontiguousarray(np.repeat(np.eye(E, dtype=np.float32)[:, :, None], P, axis=2)),
            "dft": np.ascontiguousarray(dft.astype(np.float32))}


def kernel(**inputs):
    import concourse.bacc as _bacc
    from concourse.bass_utils import run_bass_kernel_spmd as _run

    nc = _bacc.Bacc("TRN2", target_bir_lowering=False, num_devices=1)
    arrays, args = {}, {}
    for name, a in list(inputs.items()) + list(constants().items()):
        a = np.ascontiguousarray(a)
        if a.dtype.kind == "b":
            a = a.view(np.uint8)
        if a.ndim == 0:
            a = a.reshape(1)
        arrays[f"in_{name}"] = a
        args[name] = nc.dram_tensor(f"in_{name}", a.shape, mybir.dt.from_np(a.dtype), kind="ExternalInput").ap()
    args["out"] = nc.dram_tensor("out", (1, T, D), F32, kind="ExternalOutput").ap()
    build(nc, args)
    r = _run(nc, [arrays], core_ids=[0])
    return r.results[0]["out"]
```

```python
import numpy as np
import concourse.bass as bass
from concourse import mybir
from contextlib import ExitStack

F32 = mybir.dt.float32
BF16 = mybir.dt.bfloat16
U8 = mybir.dt.uint8
U32 = mybir.dt.uint32
I32 = mybir.dt.int32
ALU = mybir.AluOpType
ACT = mybir.ActivationFunctionType
AX = mybir.AxisListType

P = 128
T = 1024
NT = T // P
TB = 512
NB = T // TB
D = 128
DC = 96
G = 6404
NG = -(-G // P)
GP = NG * P
GROUP = 512
NGROUP = -(-GP // GROUP)
H0, DH0, TOPK = 4, 32, 32
H1, DH1 = 16, 8
VW = DH1 + 1
NS = 64
KTAP = 32
HID = 512
RANK = 32
E = 8
LEVELS = 3
PIECE = 128
NPIECE = G // PIECE
NCAND = NPIECE * 8
UNROLL = 3
TURNS = NG // UNROLL
MASKED = -1.0e30
LOWEST = -3.0e38
EXP_RANGE = 60.0
LN_EPS = 1e-5
ROUND = 12582912.0
assert GP == NG * P and NG % UNROLL == 0


SPARE = []


def take_wait(eng, spare=SPARE):
    eng.sem_inc(spare[0], 1)


def take_part(eng, spare=SPARE):
    eng.sem_inc(spare[0], 1)


class Chain:

    def __init__(self, eng, sem):
        self.eng, self.sem, self.n, self.turn = eng, sem, 0, 0

    def __call__(self, ins, before_max=False):
        ins.then_inc(self.sem, 1)
        self.n += 1
        self.eng.wait_ge(self.sem, self.turn + self.n)
        if before_max:
            take_wait(self.eng)

    def loop(self, i, steps):
        self.turn = i * steps

    def looped(self, steps, turns):
        self.turn = 0
        self.n += steps * (turns - 1)


def build(nc, A):
    with ExitStack() as whole:
        program(nc, A, whole)


def program(nc, A, whole):
    stage_sems = {}
    stage = [0]

    def S(name):
        if name not in stage_sems:
            stage_sems[name] = nc.alloc_semaphore(name=f"{name}_{stage[0]}")
        return stage_sems[name]

    def next_stage():
        nc.clear_and_free_semaphores(list(stage_sems.values()))
        nc.all_engine_barrier()
        stage_sems.clear()
        stage[0] += 1
        for chain, name in chains:
            chain.sem, chain.n = S(name), 0
        ln_stats.n = 0


    def sb(ctx, name, shape, dt=F32):
        return ctx.enter_context(nc.sbuf_tensor(name, shape, dt))

    SPARE[:] = [whole.enter_context(nc.semaphore("spare"))]
    V, C, M, PL = nc.vector, nc.scalar, nc.tensor, nc.gpsimd
    dchain = Chain(V, S("dve_chain"))
    achain = Chain(C, S("act_chain"))
    pchain = Chain(PL, S("pool_chain"))
    chains = ((dchain, "dve_chain"), (achain, "act_chain"), (pchain, "pool_chain"))

    ps = whole.enter_context(nc.psum_tensor("ps", [P, 8, 512], F32))

    k1_parts = nc.dram_tensor("k1_parts", [LEVELS, P, GP], BF16).ap()
    v1_rows = nc.dram_tensor("v1_rows", [P, NG, H1 * VW], F32).ap()
    ns_lines = nc.dram_tensor("ns_lines", [LEVELS, H1 * T], BF16).ap()
    mask_line = nc.dram_tensor("mask_line", [3, GP], BF16).ap()

    ident = sb(whole, "ident", [P, P])
    x_sb = sb(whole, "x_sb", [P, NT, D])
    xn = sb(whole, "xn", [P, NT, D])
    xnT = sb(whole, "xnT", [P, T])
    gates = sb(whole, "gates", [P, 4])
    ones = sb(whole, "ones", [P, 1])
    general = sb(whole, "general", [1, 2], I32)
    kabs = sb(whole, "kabs", [P, NGROUP])
    kabs1 = sb(whole, "kabs1", [P, 1])
    quarter = sb(whole, "quarter", [P, 1])
    gt = sb(whole, "gt", [P, 4])
    stats = sb(whole, "stats", [P, NT, 6])
    mv = sb(whole, "mv", [P, NT, 2])
    vare = sb(whole, "vare", [P, NT])
    sdev = sb(whole, "sdev", [P, NT])
    rstd = sb(whole, "rstd", [P, NT])
    c_t = sb(whole, "c_t", [P, NT, D])
    q1_parts = nc.dram_tensor("q1_parts", [LEVELS, P, T], BF16).ap()

    def every_tile(row):
        return row[:, :].unsqueeze(1).to_broadcast([P, NT, D])

    def flat(tile):
        return tile[:, :, :].rearrange("p a b -> p (a b)")

    def ln_stats(src, ready, wait=True):
        for t in range(NT):
            V.bn_stats(stats[:, t, :], src[:, t, :]).then_inc(S("ln_stats"), 1)
        ln_stats.n += NT
        V.wait_ge(S("ln_stats"), ln_stats.n)
        for t in range(NT):
            last = V.bn_aggr(mv[:, t, :], stats[:, t, :])
            last.then_inc(S("ln_stats"), 1)
        ln_stats.n += NT
        V.wait_ge(S("ln_stats"), ln_stats.n)
        V.tensor_scalar(vare[:, :], mv[:, :, 1], LN_EPS, None, ALU.add).then_inc(ready, 1)

    ln_stats.n = 0

    def ln_sqrt(count, ready, done):
        C.wait_ge(ready, count)
        C.activation(sdev[:, :], vare[:, :], ACT.Sqrt).then_inc(done, 1)

    def ln_apply(dst, src, done, count, out_sem):
        V.wait_ge(done, count)
        dchain(V.reciprocal(rstd[:, :], sdev[:, :]))
        for t in range(NT):
            V.tensor_scalar(dst[:, t, :], src[:, t, :], mv[:, t, 0:1], rstd[:, t:t + 1],
                            ALU.subtract, ALU.mult).then_inc(out_sem, 1)

    def transpose_tiles(src, bank, done):
        for t in range(NT):
            last = M.transpose(ps[:, bank + t // 4, (t % 4) * P:(t % 4 + 1) * P], src[:, t, :], ident[:, :])
        last.then_inc(done, 1)

    l0 = ExitStack()
    K0 = sb(l0, "K0", [P, GP])
    Q0 = sb(l0, "Q0", [P, T])
    V0 = sb(l0, "V0", [P, NG, D])
    masked = sb(l0, "masked", [P, 1])

    with ExitStack() as b1:
        wq0 = sb(b1, "wq0", [P, P])
        wk0 = sb(b1, "wk0", [DC, P])
        wk1 = sb(b1, "wk1", [DC, P])
        wv = sb(b1, "wv", [DC, 2 * P])
        bk1 = sb(b1, "bk1", [P, 1])
        bv1 = sb(b1, "bv1", [P, P])
        NR = 3
        ctx_in = sb(b1, "ctx_in", [P, NR, 4, DC])
        ctxT = sb(b1, "ctxT", [DC, 2, GROUP])
        res1 = sb(b1, "res1", [P, GROUP])
        k1f = sb(b1, "k1f", [P, GROUP])
        kl1 = sb(b1, "kl1", [P, 2, LEVELS, GROUP], BF16)
        v1g = sb(b1, "v1g", [P, 2, 4, H1, VW])
        mask8 = sb(b1, "mask8", [P, NG], U8)
        maskf = sb(b1, "maskf", [P, 3, NG], BF16)
        openf = sb(b1, "openf", [P, NG])
        lastv = G - (NG - 1) * P

        def width(i):
            return min(GROUP, GP - i * GROUP)

        def stores(n, r):
            return (n + 1 - r) // 2

        with nc.Block() as block:
            @block.sync
            def _(sp):
                sp.dma_start(x_sb[:, :, :], A["x"][0].rearrange("(n p) d -> p n d", p=P)).then_inc(S("x_in"), 16)
                sp.dma_start(ident[:, :], A["ident"]).then_inc(S("w_in"), 16)
                sp.dma_start(wk0[:, :], A["L0_xattn_Wk"]).then_inc(S("w_in"), 16)
                sp.dma_start(wk1[:, :], A["L1_xattn_wk"]).then_inc(S("w_in"), 16)
                sp.dma_start(wv[:, 0:P], A["L0_xattn_Wv"]).then_inc(S("w_in"), 16)
                sp.dma_start(wv[:, P:2 * P], A["L1_xattn_wv"]).then_inc(S("w_in"), 16)
                sp.dma_start(wq0[:, :], A["L0_xattn_Wq"]).then_inc(S("w_in"), 16)
                for i in range(NGROUP):
                    if i >= NR:
                        sp.wait_ge(S("ctxT_ps"), i - NR + 1)
                    if i == NGROUP - 1:
                        sp.wait_ge(S("ctx_pad"), 1)
                        full = (G - i * GROUP) // P
                        sp.dma_start(ctx_in[:, i % NR, 0:full, :],
                                     A["ctx_768"][0, i * GROUP:i * GROUP + full * P, :]
                                     .rearrange("(c p) d -> p c d", p=P)).then_inc(S(f"ctx_in{i % NR}"), 16)
                        sp.dma_start(ctx_in[0:lastv, i % NR, full, :],
                                     A["ctx_768"][0, G - lastv:G, :]).then_inc(S(f"ctx_in{i % NR}"), 16)
                    else:
                        sp.dma_start(ctx_in[:, i % NR, :, :],
                                     A["ctx_768"][0, i * GROUP:(i + 1) * GROUP, :]
                                     .rearrange("(c p) d -> p c d", p=P)).then_inc(S(f"ctx_in{i % NR}"), 16)
                sp.wait_ge(S("mask_out"), 48)
                for r in range(2):
                    sp.wait_ge(S(f"k1_out{r}"), 16 * stores(NGROUP, r))
                    sp.wait_ge(S(f"v1_out{r}"), 16 * stores(NGROUP, r))

            @block.gpsimd
            def _(pool):
                PL.memset(mask8[:, :], 0).then_inc(S("mask8_zero"), 1)
                pool.wait_ge(S("mask8_zero"), 1)
                PL.memset(v1g[:, :, :, :, DH1:VW], 1.0).then_inc(S("v1_ones"), 1)
                pool.wait_ge(S("v1_ones"), 1)
                PL.dma_start(bv1[:, :], A["L1_xattn_bv"].partition_broadcast(P)).then_inc(S("bv_in"), 16)
                PL.dma_start(bk1[:, :], A["L1_xattn_bk"].rearrange("(p a) -> p a", a=1)).then_inc(S("bk_in"), 16)
                pool.wait_ge(S("mask8_zero"), 1)
                full = G // NG
                PL.dma_start(mask8[0:full, :], A["mask_BxS2_bf1"][0, 0:full * NG].rearrange("(p c) -> p c", c=NG))\
                    .then_inc(S("mask_in"), 16)
                PL.dma_start(mask8[full:full + 1, 0:G - full * NG],
                             A["mask_BxS2_bf1"][0:1, full * NG:G]).then_inc(S("mask_in"), 16)
                pchain(PL.memset(maskf[:, 2, :], 1.0))
                pchain(PL.memset(maskf[:, 1, :], 0.0))
                pchain(PL.affine_select(out=maskf[:, 1, :], in_=maskf[:, 1, :], pattern=[[-1, NG]],
                                        compare_op=ALU.is_gt, fill=MASKED, base=G, channel_multiplier=-NG))
                pool.wait_ge(S("mask_in"), 32)
                pchain(PL.tensor_scalar(maskf[:, 0, :], mask8[:, :], -1.0, -MASKED, ALU.add, ALU.mult))
                for j in range(3):
                    PL.dma_start(mask_line[j, :].rearrange("(p c) -> p c", c=NG), maskf[:, j, :])\
                        .then_inc(S("mask_out"), 16)
                for i in range(NGROUP):
                    w, r = width(i), i % 2
                    pool.wait_ge(S("k1_evac"), i + 1)
                    if i >= 2:
                        pool.wait_ge(S(f"k1_out{r}"), 16 * (i // 2))
                    pchain(PL.tensor_copy(kl1[:, r, 0, 0:w], k1f[:, 0:w]))
                    pchain(PL.tensor_tensor(res1[:, 0:w], k1f[:, 0:w], kl1[:, r, 0, 0:w], ALU.subtract))
                    pchain(PL.tensor_copy(kl1[:, r, 1, 0:w], res1[:, 0:w]))
                    PL.tensor_tensor(kl1[:, r, 2, 0:w], res1[:, 0:w], kl1[:, r, 1, 0:w], ALU.subtract)\
                        .then_inc(S("k1_split"), 1)
                    pool.wait_ge(S("k1_split"), i + 1)

            @block.scalar
            def _(act):
                ln_sqrt(1, S("ln_var"), S("ln_sd"))
                act.wait_ge(S("xnT_ps"), 1)
                C.copy(xnT[:, :], ps[:, 0:2, :].rearrange("p a b -> p (a b)")).then_inc(S("xnT_sb"), 1)
                act.wait_ge(S("q_ps"), 1)
                C.mul(Q0[:, :], ps[:, 2:4, :].rearrange("p a b -> p (a b)"), float(DH0) ** -0.5).then_inc(S("q0"), 1)
                act.wait_ge(S("bk_in"), 16)
                for i in range(NGROUP):
                    w, r = width(i), i % 2
                    act.wait_ge(S("ctxT_ps"), i + 1)
                    if i >= 2:
                        act.wait_ge(S("v_ps"), i - 1)
                    C.copy(ctxT[:, r, 0:w], ps[0:DC, 4, 0:w]).then_inc(S("ctxT_sb"), 1)
                    act.wait_ge(S("k_ps"), i + 1)
                    if i >= 1:
                        act.wait_ge(S("k1_split"), i)
                        act.wait_ge(S("k1_seen"), i)
                    C.activation(k1f[:, 0:w], ps[:, 6, 0:w], ACT.Identity, bias=bk1[:, 0:1]).then_inc(S("k1_evac"), 1)
                    C.copy(K0[:, i * GROUP:i * GROUP + w], ps[:, 5, 0:w]).then_inc(S("k0_evac"), 1)
                    act.wait_ge(S("v_ps"), i + 1)
                    C.copy(V0[:, 4 * i:4 * i + w // P, :],
                           ps[:, 7, 0:w].rearrange("p (c k) -> p c k", k=P)).then_inc(S("v0_evac"), 1)
                    for j in ([i - 1] if i else []) + ([i] if i == NGROUP - 1 else []):
                        wj = width(j)
                        act.wait_ge(S("k1_split"), j + 1)
                        C.dma_start(k1_parts[:, :, j * GROUP:j * GROUP + wj].rearrange("l p g -> p l g"),
                                    kl1[:, j % 2, :, 0:wj]).then_inc(S(f"k1_out{j % 2}"), 16)
                        act.wait_ge(S("v1_evac"), j + 1)
                        C.dma_start(v1_rows[:, 4 * j:4 * j + wj // P, :],
                                    v1g[:, j % 2, 0:wj // P, :, :].rearrange("p c h v -> p c (h v)"))\
                            .then_inc(S(f"v1_out{j % 2}"), 16)

            @block.vector
            def _(dve):
                dchain(V.memset(ones[:, :], 1.0))
                dve.wait_ge(S("x_in"), 16)
                ln_stats(x_sb, S("ln_var"))
                ln_apply(xn, x_sb, S("ln_sd"), 1, S("xn_ready"))
                dve.wait_ge(S("mask_in"), 32)
                dchain(V.tensor_copy(openf[:, :], mask8[:, :]))
                dchain(V.reduce_sum(masked[:, :], openf[:, :], AX.X))
                dve.wait_ge(S("bv_in"), 16)
                dve.wait_ge(S("v1_ones"), 1)
                for i in range(NGROUP):
                    w, r = width(i), i % 2
                    if i == NGROUP - 4:
                        dve.wait_ge(S("ctxT_ps"), NGROUP - NR)
                        V.memset(ctx_in[:, (NGROUP - 1) % NR, :, :], 0.0).then_inc(S("ctx_pad"), 1)
                    dve.wait_ge(S("k1_evac"), i + 1)
                    dchain(V.tensor_reduce(kabs[:, i:i + 1], k1f[:, 0:w], AX.X, ALU.max, apply_absolute_value=True))
                    V.sem_inc(S("k1_seen"), 1)
                    dve.wait_ge(S("v_ps"), i + 1)
                    if i >= 2:
                        dve.wait_ge(S(f"v1_out{r}"), 16 * (i // 2))
                    n = w // P
                    V.tensor_tensor(v1g[:, r, 0:n, :, 0:DH1],
                                    ps[:, 0, 0:w].rearrange("p (c h v) -> p c h v", h=H1, v=DH1),
                                    bv1[:, :].rearrange("p (h v) -> p h v", v=DH1).unsqueeze(1)
                                    .to_broadcast([P, n, H1, DH1]), ALU.add).then_inc(S("v1_evac"), 1)

            @block.tensor
            def _(pe):
                pe.wait_ge(S("w_in"), 16 * 6)
                pe.wait_ge(S("xn_ready"), NT)
                transpose_tiles(xn, 0, S("xnT_ps"))
                pe.wait_ge(S("xnT_sb"), 1)
                for b in range(NB):
                    last = M.matmul(ps[:, 2 + b, :], wq0[:, :], xnT[:, b * TB:(b + 1) * TB], start=True, stop=True)
                last.then_inc(S("q_ps"), 1)

                def turn(i):
                    pe.wait_ge(S(f"ctx_in{i % NR}"), 16 * (i // NR + 1) + (16 if i == NGROUP - 1 else 0))
                    if i >= 1:
                        pe.wait_ge(S("ctxT_sb"), i)
                    for c in range(width(i) // P):
                        last = M.transpose(ps[0:DC, 4, c * P:(c + 1) * P], ctx_in[:, i % NR, c, :], ident[:, :])
                    last.then_inc(S("ctxT_ps"), 1)
                turn(0)
                for i in range(NGROUP):
                    w, r = width(i), i % 2
                    pe.wait_ge(S("ctxT_sb"), i + 1)
                    if i + 1 < NGROUP:
                        turn(i + 1)
                    if i >= 1:
                        pe.wait_ge(S("k0_evac"), i)
                        pe.wait_ge(S("k1_evac"), i)
                    M.matmul(ps[:, 5, 0:w], wk0[:, :], ctxT[:, r, 0:w], start=True, stop=True)
                    M.matmul(ps[:, 6, 0:w], wk1[:, :], ctxT[:, r, 0:w], start=True, stop=True).then_inc(S("k_ps"), 1)
                    if i >= 1:
                        pe.wait_ge(S("v0_evac"), i)
                        pe.wait_ge(S("v1_evac"), i)
                    for c in range(w // P):
                        for bank, cols in ((7, slice(0, P)), (0, slice(P, 2 * P))):
                            last = M.matmul(ps[:, bank, c * P:(c + 1) * P], ctxT[:, r, c * P:(c + 1) * P],
                                            wv[:, cols], start=True, stop=True)
                    last.then_inc(S("v_ps"), 1)

    NI = H0 * NT
    NBK = -(-GP // 512)
    GBANK = 2
    GCOL = GBANK * 512
    NGRP = -(-G // GCOL)
    NTURN = -(-NG // 4)
    CH_OF = [2, 3, 3, 5]
    NCH = len(CH_OF)
    CUTS = [min(4 * P * sum(CH_OF[:c]), G) for c in range(NCH + 1)]
    AFTER = {0: (), 1: (0, 1, 2), 2: (3,), 3: ()}
    MASK = {0: 3, 1: 4, 2: 5}
    PENALTY = {3: 1}
    NM, NP_ = len(MASK), len(PENALTY)
    NADD = (H0 - 1) * NCH
    STEEP = 2.0 ** 100
    with ExitStack() as b2:
        srow = sb(b2, "srow", [P, 2, G])
        ex = sb(b2, "ex", [P, 2, G])
        mean = sb(b2, "mean", [P, G])
        meanT = sb(b2, "meanT", [P, 2, 4 * P])
        qst = sb(b2, "qst", [P, H0, P])
        cand = sb(b2, "cand", [P, NPIECE, 8])
        cand2 = sb(b2, "cand2", [P, NCAND])
        top40 = sb(b2, "top40", [P, 2, 40])
        nmax = sb(b2, "nmax", [P, 2])
        steep = sb(b2, "steep", [P, 2])
        zsum = sb(b2, "zsum", [P, 2])
        lnz = sb(b2, "lnz", [P, 2])
        shift = sb(b2, "shift", [P, 2])
        junk = sb(b2, "junk", [P, 2, TOPK])
        edge = sb(b2, "edge", [P, NI, 2])
        hidden = sb(b2, "hidden", [P, NI])
        odd = sb(b2, "odd", [P, NI])
        odd2 = sb(b2, "odd2", [P, NI])
        odd1 = sb(b2, "odd1", [P, 1])
        miss = sb(b2, "miss", [1, 1])
        BOTH_TABLE = "natural_log_exp_and_others"
        SELECT = 12

        def group(g):
            return g * GCOL, min((g + 1) * GCOL, G)

        def done(n, c, kinds):
            return n * len(kinds) + (list(kinds).index(c) + 1)

        with nc.Block() as block:
            @block.tensor
            def _(pe):
                def scores(t, h, first):
                    pe.wait_ge(S("q_placed"), t * H0 + (h + 1))
                    for g in range(NGRP):
                        k = h * NGRP + g
                        if not (first and k < 2):
                            pe.wait_ge(S("evac"), t * (H0 * NGRP) + (k - 1))
                        g0, g1 = group(g)
                        for b in range(-(-(g1 - g0) // 512)):
                            c0, c1 = g0 + b * 512, min(g0 + b * 512 + 512, g1)
                            last = M.matmul(ps[:, GBANK * (k % 2) + b, 0:c1 - c0], qst[:, h, :], K0[:, c0:c1],
                                            start=True, stop=True)
                        last.then_inc(S("scored"), 1)

                def turn_group(u, j, first):
                    if not (first and j < 2):
                        pe.wait_ge(S("meanT_sb"), u * NTURN + (j - 1))
                    for c in range(4 * j, min(4 * j + 4, NG)):
                        n = min(P, G - c * P)
                        last = M.transpose(ps[0:n, 4 + j % 2, (c % 4) * P:(c % 4 + 1) * P], mean[:, c * P:c * P + n],
                                           ident[:, :])
                    last.then_inc(S("turned"), 1)

                def value_group(u, j, first):
                    pe.wait_ge(S("meanT_sb"), u * NTURN + (j + 1))
                    if j == 0 and not first:
                        pe.wait_ge(S("c_read"), u)
                    for c in range(4 * j, min(4 * j + 4, NG)):
                        n = min(P, G - c * P)
                        last = M.matmul(ps[:, 6, 0:D], meanT[0:n, j % 2, (c % 4) * P:(c % 4 + 1) * P], V0[0:n, c, :],
                                        start=c == 0, stop=c == NG - 1)
                    last.then_inc(S("summed"), 1)

                def chunk(u, c, first):
                    pe.wait_ge(S("added"), u * NADD + (NADD - NCH + c + 1))
                    j0 = sum(CH_OF[:c])
                    for j in range(j0, j0 + CH_OF[c]):
                        turn_group(u, j, first)
                        if j > 0:
                            value_group(u, j - 1, first)
                    if c == NCH - 1:
                        value_group(u, NTURN - 1, first)

                for h in range(H0):
                    scores(0, h, True)

                def turn(t, first):
                    for h in range(H0):
                        scores(t, h, False)
                        for c in AFTER[h]:
                            chunk(t - 1, c, first)
                turn(1, True)
                with pe.Fori(2, NT) as t:
                    turn(t, False)
                for c in range(NCH):
                    chunk(NT - 1, c, False)
                pe.wait_ge(S("odd_ready"), 1)
                M.matmul(ps[0:1, 7, 0:1], odd1[:, :], ones[:, :], start=True, stop=True)
                M.matmul(ps[0:1, 7, 1:2], masked[:, :], ones[:, :], start=True, stop=True).then_inc(S("odd_ps"), 1)

            @block.scalar
            def _(act):
                def evac(t, h, g, first):
                    g0, g1 = group(g)
                    if not (first and h < 2):
                        m = t * H0 + (h - 2)
                        below = [c for c in range(NCH) if CUTS[c] < g1]
                        act.wait_ge(S("kept"), done(m, [c for c in below if c in MASK][-1], MASK))
                        if below[-1] in PENALTY:
                            act.wait_ge(S("lowered"), done(m, below[-1], PENALTY))
                    act.wait_ge(S("scored"), t * (H0 * NGRP) + (h * NGRP + g + 1))
                    b = GBANK * ((h * NGRP + g) % 2)
                    C.copy(srow[:, h % 2, g0:g1], ps[:, b:b + GBANK, :].rearrange("p a b -> p (a b)")[:, 0:g1 - g0])\
                        .then_inc(S("evac"), 1)

                def ex_free(t, h, c, first):
                    if h == 2:
                        if c in MASK:
                            act.wait_ge(S("kept"), done(t * H0, c, MASK))
                        else:
                            act.wait_ge(S("exped_low"), done(t * H0, c, PENALTY))
                    elif h == 3:
                        act.wait_ge(S("added"), t * NADD + (c + 1))
                    elif not first:
                        act.wait_ge(S("added"), (t - 1) * NADD + ((h + 1) * NCH + (c + 1)))

                def exps(t, h, first):
                    n, s = t * H0 + h, slice(h % 2, h % 2 + 1)
                    act.wait_ge(S("edge_ready"), n + 1)
                    achain(C.activation(junk[:, h % 2, :], top40[:, h % 2, 0:TOPK], ACT.Exp, bias=nmax[:, s],
                                        accum_out=zsum[:, s]))
                    achain(C.activation(lnz[:, s], zsum[:, s], ACT.Ln, scale=float(H0)))
                    achain(C.activation(shift[:, s], lnz[:, s], ACT.Identity, scale=-1.0, bias=nmax[:, s]))
                    for c in MASK:
                        ex_free(t, h, c, first)
                        C.activation(ex[:, h % 2, CUTS[c]:CUTS[c + 1]], srow[:, h % 2, CUTS[c]:CUTS[c + 1]], ACT.Exp,
                                     bias=shift[:, s]).then_inc(S("exped"), 1)
                    for c in PENALTY:
                        ex_free(t, h, c, first)
                        C.activation(ex[:, h % 2, CUTS[c]:CUTS[c + 1]], srow[:, h % 2, CUTS[c]:CUTS[c + 1]], ACT.Relu,
                                     scale=-STEEP, bias=steep[:, s]).then_inc(S("penalty"), 1)

                def exp_lowered(t, h, c, first):
                    act.wait_ge(S("lowered"), done(t * H0 + h, c, PENALTY))
                    if h == 0 and not first:
                        act.wait_ge(S("turned"), (t - 1) * NTURN + sum(CH_OF[:c + 1]))
                    C.activation((ex[:, h % 2, :] if h else mean)[:, CUTS[c]:CUTS[c + 1]], ex[:, h % 2, CUTS[c]:CUTS[c + 1]], ACT.Exp,
                                 bias=shift[:, h % 2:h % 2 + 1]).then_inc(S("exped_low"), 1)

                def queries(t, h, first):
                    if not first:
                        act.wait_ge(S("scored"), (t - 1) * (H0 * NGRP) + (h + 1) * NGRP)
                    rows_ = slice(DH0 * h, DH0 * (h + 1))
                    C.copy(qst[rows_, h, :], Q0[rows_, bass.ds(t * P, P)]).then_inc(S("q_placed"), 1)

                def turned(u, c, first):
                    j0 = sum(CH_OF[:c])
                    for j in range(j0, j0 + CH_OF[c]):
                        act.wait_ge(S("turned"), u * NTURN + (j + 1))
                        if not (first and j < 2):
                            act.wait_ge(S("summed"), u * NTURN + (j - 1))
                        n = min(4, NG - 4 * j) * P
                        if j == NTURN - 1:
                            full, part = n - P, G - (NG - 1) * P
                            C.copy(meanT[:, j % 2, 0:full], ps[:, 4 + j % 2, 0:full]).then_inc(S("meanT_full"), 1)
                            act.wait_ge(S("meanT_full"), u + 1)
                            C.copy(meanT[0:part, j % 2, full:n], ps[0:part, 4 + j % 2, full:n]).then_inc(S("meanT_sb"), 1)
                        else:
                            C.copy(meanT[:, j % 2, 0:n], ps[:, 4 + j % 2, 0:n]).then_inc(S("meanT_sb"), 1)
                    if c == NCH - 1:
                        act.wait_ge(S("summed"), u * NTURN + NTURN)
                        C.copy(c_t[:, bass.ds(u, 1), :].rearrange("p a d -> p (a d)"), ps[:, 6, 0:D]).then_inc(S("c_read"), 1)

                C.preload_act_table_set(BOTH_TABLE)
                act.wait_ge(S("qst_zero"), 1)
                for h in range(H0):
                    queries(0, h, True)
                STEPS = 3 * H0

                def turn(t, behind, first=False, last=False):
                    for h in range(H0):
                        tm, hm = (t, h - 2) if h >= 2 else (t - 1, h + 2)
                        older = not first or h >= 2
                        if older:
                            exps(tm, hm, first)
                        for g in range(NGRP):
                            evac(t, h, g, first)
                            for c in PENALTY:
                                if older and hm and PENALTY[c] == g:
                                    exp_lowered(tm, hm, c, False)
                        if not last:
                            queries(t + 1, h, False)
                        if behind is not None:
                            for c in AFTER[h]:
                                turned(behind, c, isinstance(behind, int) and behind == 0)
                        if older and not hm:
                            for c in PENALTY:
                                exp_lowered(tm, hm, c, first)

                turn(0, None, first=True)
                turn(1, 0)
                with act.Fori(2, NT - 1) as t:
                    achain.loop(t - 2, STEPS)
                    n0 = achain.n
                    turn(t, t - 1)
                    assert achain.n - n0 == STEPS
                achain.looped(STEPS, NT - 3)
                turn(NT - 1, NT - 2, last=True)
                for h in range(2, H0):
                    exps(NT - 1, h, False)
                    for c in PENALTY:
                        exp_lowered(NT - 1, h, c, False)
                for c in range(NCH):
                    turned(NT - 1, c, False)

            @block.vector
            def _(dve):
                def mask_chunk(t, h, c, first):
                    s = h % 2
                    dve.wait_ge(S("exped"), done(t * H0 + h, c, MASK))
                    if h == 0 and not first:
                        dve.wait_ge(S("turned"), (t - 1) * NTURN + sum(CH_OF[:c + 1]))
                    V.scalar_tensor_tensor((ex[:, s, :] if h else mean)[:, CUTS[c]:CUTS[c + 1]], srow[:, s, CUTS[c]:CUTS[c + 1]],
                                           top40[:, s, TOPK - 1:TOPK], ex[:, s, CUTS[c]:CUTS[c + 1]],
                                           ALU.is_ge, ALU.mult).then_inc(S("kept"), 1)

                def event(t, h, first):
                    n, s = t * H0 + h, h % 2
                    for g in range(NGRP):
                        dve.wait_ge(S("evac"), t * (H0 * NGRP) + (h * NGRP + g + 1))
                        take_wait(dve)
                        g0, g1 = group(g)
                        for q in range((g1 - g0) // PIECE):
                            c0 = g0 + q * PIECE
                            c1 = G if G - c0 < 2 * PIECE else c0 + PIECE
                            last = V.max(cand[:, c0 // PIECE, :], srow[:, s, c0:c1])
                        last.then_inc(S("maxed"), 1)
                        for c in MASK:
                            if MASK[c] == g and not (first and h == 0):
                                mask_chunk(*((t, h - 1) if h else (t - 1, H0 - 1)), c, first)
                    dve.wait_ge(S("maxed"), t * (H0 * NGRP) + (h + 1) * NGRP)
                    dchain(V.reduce_max(hidden[:, bass.ds(n, 1)], cand[:, :, 7], AX.X), before_max=True)
                    for r in range(5):
                        top = top40[:, s, 8 * r:8 * r + 8]
                        src = cand[:, :, :].rearrange("p a b -> p (a b)") if r == 0 else cand2[:, :]
                        dchain(V.max(top, src), before_max=r < 4)
                        if r < 4:
                            dchain(V.match_replace(cand2[:, :], top, src, LOWEST), before_max=True)
                    dchain(V.tensor_copy(edge[:, bass.ds(n, 1), :], top40[:, s, TOPK - 1:TOPK + 1].unsqueeze(1)))
                    dchain(V.tensor_scalar(steep[:, s:s + 1], top40[:, s, TOPK - 1:TOPK], STEEP, None, ALU.mult))
                    V.tensor_scalar(nmax[:, s:s + 1], top40[:, s, 0:1], -1.0, None, ALU.mult).then_inc(S("edge_ready"), 1)

                for h in range(H0):
                    event(0, h, True)
                with dve.Fori(1, NT) as t:
                    dchain.loop(t - 1, H0 * SELECT)
                    n0 = dchain.n
                    for h in range(H0):
                        event(t, h, False)
                    assert dchain.n - n0 == H0 * SELECT
                dchain.looped(H0 * SELECT, NT - 1)
                for c in MASK:
                    mask_chunk(NT - 1, H0 - 1, c, False)
                dchain(V.tensor_tensor(odd[:, :], hidden[:, :], edge[:, :, 1], ALU.is_gt))
                dchain(V.tensor_tensor(odd2[:, :], edge[:, :, 0], edge[:, :, 1], ALU.subtract))
                dchain(V.tensor_scalar(odd2[:, :], odd2[:, :], 2.0 ** -80, None, ALU.is_lt))
                dchain(V.tensor_tensor(odd[:, :], odd[:, :], odd2[:, :], ALU.add))
                dchain(V.tensor_tensor(odd2[:, :], edge[:, :, 0], edge[:, :, 0], ALU.mult))
                dchain(V.tensor_scalar(odd2[:, :], odd2[:, :], 2.0 ** 50, None, ALU.is_gt))
                dchain(V.tensor_tensor(odd[:, :], odd[:, :], odd2[:, :], ALU.add))
                V.reduce_max(odd1[:, :], odd[:, :], AX.X).then_inc(S("odd_ready"), 1)
                dve.wait_ge(S("odd_ps"), 1)
                dchain(V.tensor_scalar(miss[:, :], ps[0:1, 7, 1:2], -1.0, float(G), ALU.mult, ALU.add))
                dchain(V.tensor_tensor(miss[:, :], miss[:, :], ps[0:1, 7, 0:1], ALU.add))
                dchain(V.tensor_copy(general[0:1, 0:1], miss[:, :]))

            @block.gpsimd
            def _(pool):
                PL.memset(qst[:, :, :], 0.0).then_inc(S("qst_zero"), 1)

                def event(t, h):
                    n, s = t * H0 + h, h % 2
                    for c in PENALTY:
                        pool.wait_ge(S("penalty"), done(n, c, PENALTY))
                        PL.tensor_tensor(ex[:, s, CUTS[c]:CUTS[c + 1]], srow[:, s, CUTS[c]:CUTS[c + 1]],
                                         ex[:, s, CUTS[c]:CUTS[c + 1]], ALU.subtract).then_inc(S("lowered"), 1)
                    if h == 0:
                        return
                    for c in range(NCH):
                        if c in MASK:
                            pool.wait_ge(S("kept"), done(n, c, MASK))
                        else:
                            pool.wait_ge(S("exped_low"), done(n, c, PENALTY))
                        if h > 1:
                            pool.wait_ge(S("added"), t * NADD + ((h - 2) * NCH + c + 1))
                        PL.tensor_tensor(mean[:, CUTS[c]:CUTS[c + 1]], mean[:, CUTS[c]:CUTS[c + 1]],
                                         ex[:, s, CUTS[c]:CUTS[c + 1]], ALU.add).then_inc(S("added"), 1)

                with pool.Fori(0, NT) as t:
                    for h in range(H0):
                        event(t, h)

            @block.sync
            def _(sp):
                take_part(sp)

    next_stage()
    l0_general = nc.values_load(general[0:1, 0:1], min_val=0, max_val=G + P)
    with nc.If(l0_general > 0):
        with ExitStack() as b3:
            row = sb(b3, "row", [P, GP])
            t40 = sb(b3, "t40", [P, TOPK])
            nmax = sb(b3, "nmaxg", [P, 1])
            zsum, zinv = sb(b3, "zsumg", [P, 1]), sb(b3, "zinvg", [P, 1])
            junk = sb(b3, "junkg", [P, TOPK])
            junk2 = sb(b3, "junk2", [P, D])
            exg, pg, pgT = (sb(b3, n, [P, 2, 512]) for n in ("exg", "pg", "pgT"))
            QZ = sb(b3, "QZ", [P, H0, T])
            qg = sb(b3, "qg", [P, P])
            mrow = sb(b3, "mrow", [1, GP], BF16)
            onesb = sb(b3, "onesb", [1, P], BF16)

            def bank_width(j):
                return min(512, GP - j * 512)

            with nc.Block() as block:
                @block.gpsimd
                def _(pool):
                    PL.memset(c_t[:, :, :], 0.0).then_inc(S("c_zero"), 1)
                    PL.memset(onesb[:, :], 1.0).then_inc(S("g_ones"), 1)
                    PL.memset(QZ[:, :, :], 0.0).then_inc(S("qz"), 1)
                    pool.wait_ge(S("qz"), 1)
                    for h in range(H0):
                        rows_ = slice(DH0 * h, DH0 * (h + 1))
                        PL.tensor_copy(QZ[rows_, h, :], Q0[rows_, :]).then_inc(S("qz"), 1)
                        pool.wait_ge(S("qz"), h + 2)
                    with pool.Fori(0, NI) as i:
                        pool.wait_ge(S("g_added"), i + 1)
                        PL.tensor_copy(qg[:, :], QZ[:, :, :].rearrange("p h t -> p (h t)")[:, bass.ds(i * P, P)])\
                            .then_inc(S("g_q"), 1)

                @block.sync
                def _(sp):
                    sp.dma_start(mrow[0:1, :], mask_line[0:1, :]).then_inc(S("g_mask"), 16)

                @block.tensor
                def _(pe):
                    def scores(h, i, e):
                        j, w = e % NBK, bank_width(e % NBK)
                        pe.wait_ge(S("g_read"), i * 2 * NBK + e + 1)
                        M.matmul(ps[:, e % 2, 0:w], qg[:, :], K0[:, j * 512:j * 512 + w], start=True, stop=False)
                        M.matmul(ps[:, e % 2, 0:w], onesb[:, :], mrow[0:1, j * 512:j * 512 + w], start=False, stop=True)\
                            .then_inc(S("g_scored"), 1)

                    pe.wait_ge(S("g_ones"), 1)
                    pe.wait_ge(S("g_mask"), 16)
                    with pe.Fori(0, H0) as h:
                        with pe.Fori(0, NT) as t:
                            i = h * NT + t
                            pe.wait_ge(S("g_q"), i + 1)
                            for e in range(NBK):
                                scores(h, i, e)
                            for j in range(NBK):
                                scores(h, i, NBK + j)
                                pe.wait_ge(S("g_kept"), i * NBK + j + 2)
                                for c in range(bank_width(j) // P):
                                    last = M.transpose(ps[:, 2 + j % 2, c * P:(c + 1) * P], pg[:, j % 2, c * P:(c + 1) * P],
                                                       ident[:, :])
                                last.then_inc(S("g_turned"), 1)
                                pe.wait_ge(S("g_placed"), i * NBK + j + 1)
                                if j == 0:
                                    pe.wait_ge(S("g_added"), i + 1)
                                n = bank_width(j) // P
                                for c in range(n):
                                    last = M.matmul(ps[:, 4, 0:D], pgT[:, j % 2, c * P:(c + 1) * P], V0[:, 4 * j + c, :],
                                                    start=j == 0 and c == 0, stop=j == NBK - 1 and c == n - 1)
                                last.then_inc(S("g_summed"), 1)

                @block.scalar
                def _(act):
                    act.sem_inc(S("g_read"), 2)
                    with act.Fori(0, NI) as i:
                        for j in range(NBK):
                            w = bank_width(j)
                            act.wait_ge(S("g_scored"), i * 2 * NBK + j + 1)
                            if j == 0:
                                act.wait_ge(S("g_kept"), i * NBK + 1)
                            C.copy(row[:, j * 512:j * 512 + w], ps[:, j % 2, 0:w]).then_inc(S("g_read"), 1)
                        act.wait_ge(S("g_max"), i + 1)
                        C.activation(junk[:, :], t40[:, :], ACT.Exp, bias=nmax[:, 0:1], accum_out=zsum[:, :]).then_inc(S("g_z"), 1)
                        for j in range(NBK):
                            w, e = bank_width(j), NBK + j
                            act.wait_ge(S("g_scored"), i * 2 * NBK + e + 1)
                            if j >= 2:
                                act.wait_ge(S("g_kept"), i * NBK + j)
                            C.activation(exg[:, j % 2, 0:w], ps[:, e % 2, 0:w], ACT.Exp, bias=nmax[:, 0:1])\
                                .then_inc(S("g_read"), 1)

                @block.vector
                def _(dve):
                    steps_ = 2 * (TOPK // 8) + 4
                    dve.wait_ge(S("c_zero"), 1)
                    dve.sem_inc(S("g_added"), 1)
                    dve.sem_inc(S("g_kept"), 1)
                    with dve.Fori(0, H0) as h:
                        with dve.Fori(0, NT) as t:
                            i = h * NT + t
                            dchain.loop(i, steps_)
                            n0 = dchain.n
                            dve.wait_ge(S("g_read"), i * 2 * NBK + NBK + 2)
                            take_wait(dve)
                            for r in range(TOPK // 8):
                                top = t40[:, 8 * r:8 * r + 8]
                                dchain(V.max(top, row[:, :]), before_max=True)
                                dchain(V.match_replace(row[:, :], top, row[:, :], LOWEST), before_max=True)
                            V.tensor_scalar(nmax[:, :], t40[:, 0:1], -1.0, None, ALU.mult).then_inc(S("g_max"), 1)
                            for j in range(NBK):
                                w = bank_width(j)
                                dve.wait_ge(S("g_read"), i * 2 * NBK + NBK + j + 3)
                                V.scalar_tensor_tensor(pg[:, j % 2, 0:w], row[:, j * 512:j * 512 + w], LOWEST,
                                                       exg[:, j % 2, 0:w], ALU.is_equal, ALU.mult).then_inc(S("g_kept"), 1)
                                dve.wait_ge(S("g_turned"), i * NBK + j + 1)
                                if j >= 2:
                                    dve.wait_ge(S("g_summed"), i * NBK + j - 1)
                                V.tensor_copy(pgT[:, j % 2, 0:w], ps[:, 2 + j % 2, 0:w]).then_inc(S("g_placed"), 1)
                            dve.wait_ge(S("g_z"), i + 1)
                            dchain(V.tensor_scalar(zinv[:, :], zsum[:, :], float(H0), None, ALU.mult))
                            dchain(V.reciprocal(zinv[:, :], zinv[:, :]))
                            dve.wait_ge(S("g_summed"), i * NBK + NBK)
                            dchain(V.tensor_scalar(junk2[:, :], ps[:, 4, 0:D], zinv[:, 0:1], None, ALU.mult))
                            tile = c_t[:, bass.ds(t, 1), :]
                            dchain(V.tensor_tensor(tile, tile, junk2[:, :].unsqueeze(1), ALU.add))
                            dve.sem_inc(S("g_added"), 1)
                            assert dchain.n - n0 == steps_
                    dchain.looped(steps_, NI)
    next_stage()
    l0.close()



    taps = sb(whole, "taps", [P, NT, D])
    with ExitStack() as b4:
        small = lambda name, n=NS: sb(b4, name, [P, n])
        a_re, a_im, c_re, c_im = (small(n) for n in ("a_re", "a_im", "c_re", "c_im"))
        ldt, dt = small("ldt", 1), small("dt", 1)
        rr, tau, z, q, e1 = (small(n) for n in ("rr", "tau", "z", "q", "e1"))
        sh, sn, cs = (small(n) for n in ("sh", "sn", "cs"))
        er, ei, nr, ni, den, t1, t2 = (small(n) for n in ("er", "ei", "nr", "ni", "den", "t1", "t2"))
        rows = sb(b4, "rows", [P, 4, 2 * NS])
        rowsT = sb(b4, "rowsT", [P, 4, D])
        turnsA = sb(b4, "turnsA", [P, D])
        rateA = sb(b4, "rateA", [P, D])
        steps = sb(b4, "steps", [P, KTAP])
        dskip = sb(b4, "dskip", [1, D])
        table = lambda name: sb(b4, name, [P, KTAP, D])
        phase, mag, work = table("phase"), table("mag"), table("work")
        zb, ua, ub = table("zb"), table("ua"), table("ub")
        QUARTER = float(np.pi / 2)
        TURN = float(2 * np.pi * (1 - 1e-7))

        with nc.Block() as block:
            @block.sync
            def _(sp):
                for dst, name in ((a_re, "A_re"), (a_im, "A_im"), (c_re, "C_re"), (c_im, "C_im")):
                    sp.dma_start(dst[:, :], A["L0_xattn_" + name]).then_inc(S("s4_in"), 16)
                sp.dma_start(ldt[:, :], A["L0_xattn_log_dt"].rearrange("(p a) -> p a", a=1)).then_inc(S("s4_in"), 16)
                sp.dma_start(steps[:, :], A["steps"].partition_broadcast(P)).then_inc(S("s4_in"), 16)
                sp.dma_start(dskip[:, :], A["L0_xattn_D_skip"].unsqueeze(0)).then_inc(S("s4_in"), 16)

            @block.vector
            def _(dve):
                tt = lambda o, a, b, op: dchain(V.tensor_tensor(o, a, b, op))
                ts = lambda o, a, s1, s2, o1, o2=ALU.bypass: dchain(V.tensor_scalar(o, a, s1, s2, o1, o2))
                a = lambda t: t[:, :]
                dve.wait_ge(S("dt_ready"), 1)
                dve.wait_ge(S("s4_in"), 16 * 7)
                ts(a(rr), a(a_re), dt[:, 0:1], None, ALU.mult)
                ts(a(t1), a(a_im), dt[:, 0:1], float(0.5 / np.pi), ALU.mult, ALU.mult)
                ts(a(t2), a(t1), ROUND, ROUND, ALU.add, ALU.subtract)
                V.tensor_tensor(a(tau), a(t1), a(t2), ALU.subtract).then_inc(S("tau_ready"), 1)
                ts(a(z), a(rr), -18.0, 1.0 / 16, ALU.max, ALU.mult)
                ts(a(q), a(z), 1.0 / 9, 1.0, ALU.mult, ALU.add)
                for k in range(8, 1, -1):
                    dchain(V.scalar_tensor_tensor(a(q), a(z), 1.0 / k, a(q), ALU.mult, ALU.mult))
                    ts(a(q), a(q), 1.0, None, ALU.add)
                tt(a(e1), a(z), a(q), ALU.mult)
                for _ in range(4):
                    dchain(V.scalar_tensor_tensor(a(e1), a(e1), 2.0, a(e1), ALU.add, ALU.mult))
                dve.wait_ge(S("trig_ready"), 2)
                tt(a(t1), a(sh), a(sh), ALU.mult)
                ts(a(cs), a(t1), -2.0, 1.0, ALU.mult, ALU.add)
                tt(a(er), a(e1), a(cs), ALU.mult)
                dchain(V.scalar_tensor_tensor(a(er), a(t1), -2.0, a(er), ALU.mult, ALU.add))
                dchain(V.scalar_tensor_tensor(a(ei), a(e1), 1.0, a(sn), ALU.add, ALU.mult))
                tt(a(nr), a(c_re), a(er), ALU.mult)
                tt(a(t1), a(c_im), a(ei), ALU.mult)
                tt(a(nr), a(nr), a(t1), ALU.subtract)
                tt(a(ni), a(c_re), a(ei), ALU.mult)
                tt(a(t1), a(c_im), a(er), ALU.mult)
                tt(a(ni), a(ni), a(t1), ALU.add)
                tt(a(den), a(a_re), a(a_re), ALU.mult)
                tt(a(t1), a(a_im), a(a_im), ALU.mult)
                tt(a(den), a(den), a(t1), ALU.add)
                dchain(V.reciprocal(a(den), a(den)))
                tt(a(t1), a(nr), a(a_re), ALU.mult)
                tt(a(t2), a(ni), a(a_im), ALU.mult)
                tt(a(t1), a(t1), a(t2), ALU.add)
                tt(a(t1), a(t1), a(den), ALU.mult)
                tt(a(t2), a(ni), a(a_re), ALU.mult)
                tt(a(z), a(nr), a(a_im), ALU.mult)
                tt(a(t2), a(t2), a(z), ALU.subtract)
                tt(a(t2), a(t2), a(den), ALU.mult)
                for half, sign in ((slice(0, NS), 2.0), (slice(NS, 2 * NS), -2.0)):
                    dchain(V.tensor_copy(rows[:, 0, half], a(rr)))
                    dchain(V.tensor_copy(rows[:, 1, half], a(tau)))
                    ts(rows[:, 2, half], a(t1), sign, None, ALU.mult)
                    ts(rows[:, 3, half], a(t2), -2.0, None, ALU.mult)
                V.tensor_copy(dt[:, :], dt[:, :]).then_inc(S("rows_ready"), 1)
                dve.wait_ge(S("rowsT_ps"), 1)
                dchain(V.tensor_copy(rowsT[:, :, :], ps[:, 0, :].rearrange("p (a d) -> p a d", d=D)))
                ts(a(rateA), rowsT[:, 0, :], float(KTAP), None, ALU.mult)
                ts(a(turnsA), rowsT[:, 1, :], float(KTAP), None, ALU.mult)
                ts(work[:, 0, :], a(turnsA), ROUND, ROUND, ALU.add, ALU.subtract)
                tt(a(turnsA), a(turnsA), work[:, 0, :], ALU.subtract)
                V.tensor_copy(dt[:, :], dt[:, :]).then_inc(S("rates_ready"), 1)

                over_d = lambda t: t.unsqueeze(1).to_broadcast([P, KTAP, D])
                over_steps = steps[:, :].unsqueeze(2).to_broadcast([P, KTAP, D])
                w = lambda t: t[:, :, :]

                def phases(turns):
                    tt(w(phase), over_d(turns), over_steps, ALU.mult)
                    ts(w(work), w(phase), ROUND, ROUND, ALU.add, ALU.subtract)
                    V.tensor_tensor(w(phase), w(phase), w(work), ALU.subtract).then_inc(S("phase_ready"), 1)

                phases(rowsT[:, 1, :])
                dve.wait_ge(S("zb_trig"), 1)
                dve.wait_ge(S("mag_exp"), 1)
                dchain(V.tensor_tensor(w(zb), w(zb), w(mag), ALU.mult))
                V.tensor_copy(dt[:, :], dt[:, :]).then_inc(S("zb_ready"), 1)
                phases(a(turnsA))
                dve.wait_ge(S("mag_exp"), 2)
                dve.wait_ge(S("ua_trig"), 1)
                tt(w(ua), w(ua), over_d(rowsT[:, 2, :]), ALU.mult)
                tt(w(ub), w(ub), over_d(rowsT[:, 3, :]), ALU.mult)
                tt(w(ua), w(ua), w(ub), ALU.add)
                V.tensor_tensor(w(ua), w(ua), w(mag), ALU.mult).then_inc(S("ua_ready"), 1)
                for h in range(2):
                    dve.wait_ge(S("taps_ps"), h + 1)
                    for r in range(4):
                        src = ps[0:KTAP, 4 * h:4 * h + 4, :].rearrange("p k (d m r) -> p m k d r", m=NT, r=4)
                        for kk in range(4):
                            d0 = 64 * h + 16 * kk
                            V.tensor_copy(taps[KTAP * r:KTAP * (r + 1), :, d0:d0 + 16], src[:, :, kk, :, r])\
                                .then_inc(S("taps_ready"), 1)
                dve.wait_ge(S("taps_ready"), 32)
                V.tensor_tensor(taps[0:1, 0, :], taps[0:1, 0, :], dskip[0:1, :], ALU.add).then_inc(S("taps_ready"), 1)

            @block.scalar
            def _(act):
                act.wait_ge(S("s4_in"), 16 * 7)
                C.activation(dt[:, :], ldt[:, :], ACT.Exp).then_inc(S("dt_ready"), 1)
                act.wait_ge(S("tau_ready"), 1)
                C.activation(sn[:, :], tau[:, :], ACT.Sin, scale=TURN).then_inc(S("trig_ready"), 1)
                C.activation(sh[:, :], tau[:, :], ACT.Sin, scale=TURN / 2).then_inc(S("trig_ready"), 1)
                w = lambda t: t[:, :, :]

                def trig(dst, rows_, sine):
                    if sine:
                        C.activation(dst[rows_, :, :], phase[rows_, :, :], ACT.Sin, scale=TURN)\
                            .then_inc(S("trig_done"), 1)
                    else:
                        C.activation(dst[rows_, :, :], work[rows_, :, :], ACT.Sin, scale=-TURN, bias=quarter[rows_, 0:1])\
                            .then_inc(S("trig_done"), 1)

                lo, hi = slice(0, NS), slice(NS, P)
                act.wait_ge(S("mag_ready"), 1)
                C.activation(w(mag), w(mag), ACT.Exp).then_inc(S("mag_exp"), 1)
                act.wait_ge(S("phase_ready"), 1)
                achain(C.activation(w(work), w(phase), ACT.Abs))
                act.wait_ge(S("quarter_ready"), 1)
                trig(zb, lo, False)
                trig(zb, hi, True)
                act.wait_ge(S("trig_done"), 2)
                act.sem_inc(S("zb_trig"), 1)
                act.wait_ge(S("phase_ready"), 2)
                achain(C.activation(w(work), w(phase), ACT.Abs))
                for dst, cos_rows, sin_rows in ((ua, lo, hi), (ub, hi, lo)):
                    trig(dst, cos_rows, False)
                    trig(dst, sin_rows, True)
                act.wait_ge(S("trig_done"), 6)
                act.sem_inc(S("ua_trig"), 1)
                act.wait_ge(S("mag_ready"), 2)
                C.activation(w(mag), w(mag), ACT.Exp).then_inc(S("mag_exp"), 1)

            @block.gpsimd
            def _(pool):
                PL.memset(quarter[:, :], QUARTER).then_inc(S("quarter_ready"), 1)
                over_steps = steps[:, :].unsqueeze(2).to_broadcast([P, KTAP, D])
                for n, rate in ((0, rowsT[:, 0, :]), (1, rateA[:, :])):
                    pool.wait_ge(S("rates_ready"), 1)
                    if n:
                        pool.wait_ge(S("zb_ready"), 1)
                    PL.tensor_tensor(mag[:, :, :], rate.unsqueeze(1).to_broadcast([P, KTAP, D]), over_steps,
                                     ALU.mult).then_inc(S("mag_ready"), 1)

            @block.tensor
            def _(pe):
                pe.wait_ge(S("rows_ready"), 1)
                for k in range(4):
                    last = M.transpose(ps[:, 0, k * D:(k + 1) * D], rows[:, k, :], ident[:, :])
                last.then_inc(S("rowsT_ps"), 1)
                pe.wait_ge(S("zb_ready"), 1)
                pe.wait_ge(S("ua_ready"), 1)
                for d in range(D):
                    last = M.matmul(ps[0:KTAP, d // 16, (d % 16) * KTAP:(d % 16 + 1) * KTAP],
                                    zb[:, :, d], ua[:, :, d], start=True, stop=True)
                    if d % 64 == 63:
                        last.then_inc(S("taps_ps"), 1)

    xt = sb(whole, "xt", [P, NT, D])
    wT = sb(whole, "wT", [P, T])
    with ExitStack() as b5:
        mask_t8 = sb(b5, "mask_t8", [P, NT], U8)
        mask_t = sb(b5, "mask_t", [P, NT])
        mg = sb(b5, "mg", [P, 1])
        wf = sb(b5, "wf", [P, HID])
        bf = sb(b5, "bf", [P, HID])
        rowsb = {n: sb(b5, "row_" + n, [P, D]) for n in ("g_norm_in", "b_norm_in", "g_ffn", "b_ffn")}
        dft = sb(b5, "dft", [P, 9, P])
        cT5 = sb(b5, "cT5", [P, T])
        film = sb(b5, "film", [P, NT, 4, D])
        xf = sb(b5, "xf", [P, NT, D])
        spec_x = sb(b5, "spec_x", [P, 2, NT, D])
        spec_k = sb(b5, "spec_k", [P, 2, NT, D])
        prod = sb(b5, "prod", [P, 2, 4, NT, D])
        FX, FK0, FK1, IFR, IFN, IFI = 0, 2, 4, 6, 7, 8
        with nc.Block() as block:
            @block.sync
            def _(sp):
                sp.dma_start(wf[:, 0:2 * D], A["L0_xattn_W_film_in"]).then_inc(S("b5_in"), 16)
                sp.dma_start(wf[:, 2 * D:], A["L0_xattn_W_film_out"]).then_inc(S("b5_in"), 16)
                sp.dma_start(bf[:, 0:2 * D], A["L0_xattn_b_film_in"].partition_broadcast(P)).then_inc(S("b5_in"), 16)
                sp.dma_start(bf[:, 2 * D:], A["L0_xattn_b_film_out"].partition_broadcast(P)).then_inc(S("b5_in"), 16)
                sp.dma_start(dft[:, :, :], A["dft"]).then_inc(S("b5_in"), 16)
                sp.dma_start(mg[:, :], A["L0_xattn_mod_gate"].partition_broadcast(P)).then_inc(S("b5_in"), 16)
                sp.dma_start(mask_t8[:, :], A["mask_BxS_bf1"].rearrange("o (n p) -> p (o n)", p=P),
                             allow_slow_non_contiguous=True).then_inc(S("b5_in"), 16)
                for n, tile in rowsb.items():
                    sp.dma_start(tile[:, :], A["L0_xattn_" + n].partition_broadcast(P)).then_inc(S("b5_in"), 16)

            @block.tensor
            def _(pe):
                pe.wait_ge(S("cm_ready"), NT)
                pe.wait_ge(S("b5_in"), 16 * 11)
                transpose_tiles(c_t, 0, S("cm_turned"))
                for part in range(2):
                    for half in range(2):
                        bank = ps[:, 2 + 2 * part + half, :]
                        if half == 0:
                            M.matmul(bank[:, D:4 * D], dft[:, FK0 + part, :], taps[:, 0:3, :], start=True, stop=False,
                                     skip_group_check=True)
                        else:
                            M.matmul(bank, dft[:, FK0 + part, :], taps[:, 3:7, :], start=True, stop=False,
                                     skip_group_check=True)
                        last = M.matmul(bank, dft[:, FK1 + part, :], taps[:, 4 * half:4 * half + 4, :],
                                        start=False, stop=True, skip_group_check=True)
                last.then_inc(S("spec_k_ps"), 1)
                pe.wait_ge(S("cT5_ready"), 1)
                pe.wait_ge(S("spec_k_ready"), 1)
                for t in range(NT):
                    if t >= 6:
                        pe.wait_ge(S("film_read"), t - 5)
                    M.matmul(ps[:, 2 + t % 6, :], cT5[:, t * P:(t + 1) * P], wf[:, :], start=True, stop=True)\
                        .then_inc(S("film_ps"), 1)
                pe.wait_ge(S("xf_ready"), 1)
                for part in range(2):
                    for half in range(2):
                        last = M.matmul(ps[:, 2 + 2 * part + half, :], dft[:, FX + part, :],
                                        xf[:, 4 * half:4 * half + 4, :], start=True, stop=True)
                last.then_inc(S("spec_x_ps"), 1)
                started = [False, False]
                for n, m in enumerate(reversed(range(NT))):
                    pe.wait_ge(S("prod_ready"), 4 * (n + 1))
                    for k, table in enumerate((IFR, IFN, IFI, IFI)):
                        for half in range(2):
                            lo_, hi_ = max(m, 4 * half), 4 * half + 4
                            if hi_ <= lo_:
                                continue
                            end = m == 0 and k == 3
                            last = M.matmul(ps[:, half, (lo_ - 4 * half) * D:(hi_ - 4 * half) * D],
                                            dft[:, table, :], prod[:, n % 2, k, lo_ - m:hi_ - m, :],
                                            start=not started[half], stop=end, skip_group_check=True)
                            started[half] = True
                    last.then_inc(S("prod_used"), 1)

            @block.scalar
            def _(act):
                act.wait_ge(S("cm_turned"), 1)
                C.copy(cT5[:, :], flat(ps[:, 0:2, :])).then_inc(S("cT5_ready"), 1)
                act.wait_ge(S("spec_k_ps"), 1)
                C.copy(spec_k[:, :, :, :].rearrange("p a b c -> p (a b c)"), flat(ps[:, 2:6, :])).then_inc(S("spec_k_ready"), 1)
                ln_sqrt(1, S("ln_in_var"), S("ln_in_sd"))
                act.wait_ge(S("spec_x_ps"), 1)
                C.copy(spec_x[:, :, :, :].rearrange("p a b c -> p (a b c)"), flat(ps[:, 2:6, :])).then_inc(S("spec_x_ready"), 1)
                ln_sqrt(1, S("ln_f_var"), S("ln_f_sd"))

            @block.vector
            def _(dve):
                dve.wait_ge(S("b5_in"), 16 * 11)
                dchain(V.tensor_copy(mask_t[:, :], mask_t8[:, :]))
                for t in range(NT):
                    V.tensor_scalar(c_t[:, t, :], c_t[:, t, :], mask_t[:, t:t + 1], None, ALU.mult).then_inc(S("cm_ready"), 1)
                ln_stats(xn, S("ln_in_var"))
                ln_apply(xf, xn, S("ln_in_sd"), 1, S("xl_ready"))
                dve.wait_ge(S("xl_ready"), NT)
                w = lambda t: t[:, :, :]
                dchain(V.tensor_tensor(w(xf), w(xf), every_tile(rowsb["g_norm_in"]), ALU.mult))
                dchain(V.tensor_tensor(w(xf), w(xf), every_tile(rowsb["b_norm_in"]), ALU.add))
                for t in range(NT):
                    dve.wait_ge(S("film_ps"), t + 1)
                    V.tensor_tensor(film[:, t, :, :].rearrange("p a b -> p (a b)"), ps[:, 2 + t % 6, :], bf[:, :], ALU.add)\
                        .then_inc(S("film_read"), 1)
                dve.wait_ge(S("film_read"), NT)
                dchain(V.tensor_scalar(film[:, :, :, :], film[:, :, :, :], mg[:, 0:1], None, ALU.mult))
                for k in (0, 2):
                    dchain(V.tensor_scalar(film[:, :, k, :], film[:, :, k, :], 1.0, None, ALU.add))
                dchain(V.tensor_tensor(w(xf), w(xf), film[:, :, 0, :], ALU.mult))
                V.tensor_tensor(w(xf), w(xf), film[:, :, 1, :], ALU.add).then_inc(S("xf_ready"), 1)
                dve.wait_ge(S("spec_x_ready"), 1)
                dve.wait_ge(S("spec_k_ready"), 1)
                for r, m in enumerate(reversed(range(NT))):
                    if r >= 2:
                        dve.wait_ge(S("prod_used"), r - 1)
                    n = NT - m
                    for k, (kp, xp) in enumerate(((0, 0), (1, 1), (0, 1), (1, 0))):
                        V.tensor_tensor(prod[:, r % 2, k, 0:n, :], spec_x[:, xp, 0:n, :],
                                        spec_k[:, kp, m, :].unsqueeze(1).to_broadcast([P, n, D]), ALU.mult)\
                            .then_inc(S("prod_ready"), 1)
                dve.wait_ge(S("prod_used"), NT)
                dchain(V.tensor_tensor(w(xt), ps[:, 0:2, :].rearrange("p a (b d) -> p (a b) d", d=D), film[:, :, 2, :], ALU.mult))
                dchain(V.tensor_tensor(w(xt), w(xt), film[:, :, 3, :], ALU.add))
                dchain(V.tensor_tensor(w(xt), w(xt), w(xn), ALU.add))
                ln_stats(xt, S("ln_f_var"))
                ln_apply(xf, xt, S("ln_f_sd"), 1, S("xl_ready"))
                dve.wait_ge(S("xl_ready"), 2 * NT)
                dchain(V.tensor_tensor(w(xf), w(xf), every_tile(rowsb["g_ffn"]), ALU.mult))
                dchain(V.tensor_tensor(w(xf), w(xf), every_tile(rowsb["b_ffn"]), ALU.add))
        with nc.Block() as block:
            @block.tensor
            def _(pe):
                transpose_tiles(xf, 0, S("xfT_ps"))

            @block.scalar
            def _(act):
                act.wait_ge(S("xfT_ps"), 1)
                C.copy(wT[:, :], flat(ps[:, 0:2, :])).then_inc(S("wT_ready"), 1)

    NF = HID // P

    NQ = H1 // 4
    ROW1 = 6 * DH1
    KIN = 12
    oq, k1s = ExitStack(), ExitStack()
    o1 = sb(oq, "o1", [P, NQ, T])
    K1 = sb(k1s, "K1", [P, 2, 2, GP], BF16)
    V1 = sb(k1s, "V1", [P, 2, NG, 4 * VW])
    vs1 = sb(k1s, "vs1", [P, UNROLL, 4, 32])

    def load_quad(sp, quad, keys_in, values_in):
        b = quad % 2
        for par in range(2):
            for r, lv in enumerate((0, 1, 2, 0, 1, 0)):
                r0 = 64 * par + DH1 * r
                src = k1_parts[lv].rearrange("(q j a d) g -> q d j a g", j=2, a=2, d=DH1)
                sp.dma_start(K1[r0:r0 + DH1, b, :, :], src[quad, :, :, par, :]).then_inc(keys_in, 16)
        sp.dma_start(V1[:, b, :, :], v1_rows[:, :, quad * 4 * VW:(quad + 1) * 4 * VW]).then_inc(values_in, 16)

    with ExitStack() as b6:
        w1 = sb(b6, "w1", [P, HID])
        w2 = sb(b6, "w2", [P, NF, D])
        b1c = sb(b6, "b1c", [P, NF])
        row6 = {n: sb(b6, "row6_" + n, [P, D]) for n in ("b2", "g_norm_out", "b_norm_out")}
        hid = sb(b6, "hid", [P, NB, NF, TB])
        yo = sb(b6, "yo", [P, NT, D])
        with nc.Block() as block:
            @block.sync
            def _(sp):
                sp.dma_start(w1[:, :], A["L0_xattn_W1"]).then_inc(S("b6_in"), 16)
                sp.dma_start(w2[:, :, :], A["L0_xattn_W2"].rearrange("(f p) d -> p f d", p=P)).then_inc(S("b6_in"), 16)
                sp.dma_start(b1c[:, :], A["L0_xattn_b1"].rearrange("(f p) -> p f", p=P),
                             allow_slow_non_contiguous=True).then_inc(S("b6_in"), 16)
                for n, tile in row6.items():
                    sp.dma_start(tile[:, :], A["L0_xattn_" + n].partition_broadcast(P)).then_inc(S("b6_in"), 16)
                sp.dma_start(gates[:, 0:2], A["g_xattn"].partition_broadcast(P)).then_inc(S("b6_in"), 16)
                sp.dma_start(gates[:, 2:4], A["g_ffn"].partition_broadcast(P)).then_inc(S("b6_in"), 16)
                for quad in range(2):
                    sp.wait_ge(S("k1_zero"), quad + 1)
                    for par in range(2):
                        r0 = 64 * par + ROW1
                        for pr in range(2):
                            sp.dma_start(K1[r0:r0 + LEVELS, quad, pr, :], mask_line[2, :].partition_broadcast(LEVELS))\
                                .then_inc(S("k1_ahead"), 16)
                            sp.dma_start(K1[r0 + LEVELS:r0 + LEVELS + 1, quad, pr, :], mask_line[1:2, :])\
                                .then_inc(S("k1_ahead"), 16)
                    load_quad(sp, quad, S("k1_ahead"), S("v1_ahead"))
                sp.wait_ge(S("k1_ahead"), 16 * 2 * (8 + KIN))
                sp.wait_ge(S("v1_ahead"), 16 * 2)

            @block.gpsimd
            def _(pool):
                for r in range(2):
                    PL.memset(K1[:, r, :, :], 0.0).then_inc(S("k1_zero"), 1)
                    pool.wait_ge(S("k1_zero"), r + 1)
                PL.memset(vs1[:, :, :, :], 0.0).then_inc(S("vs1_zero"), 1)
                pool.wait_ge(S("vs1_zero"), 1)

            @block.tensor
            def _(pe):
                pe.wait_ge(S("b6_in"), 16 * 8)
                for tb in range(NB):
                    for f in range(NF):
                        if tb:
                            pe.wait_ge(S("hid6"), (tb - 1) * NF + f + 1)
                        M.matmul(ps[:, f, :], w1[:, f * P:(f + 1) * P], wT[:, tb * TB:(tb + 1) * TB],
                                 start=True, stop=True).then_inc(S("hid6_ps"), 1)
                for t in range(NT):
                    pe.wait_ge(S("hid6"), (t // 4 + 1) * NF)
                    for f in range(NF):
                        last = M.matmul(ps[:, 4 + t // 4, (t % 4) * P:(t % 4 + 1) * P],
                                        hid[:, t // 4, f, (t % 4) * P:(t % 4 + 1) * P], w2[:, f, :],
                                        start=f == 0, stop=f == NF - 1)
                last.then_inc(S("out6_ps"), 1)
                pe.wait_ge(S("xn6"), NT)
                transpose_tiles(xn, 0, S("xn6T_ps"))

            @block.scalar
            def _(act):
                act.wait_ge(S("b6_in"), 16 * 8)
                C.activation(gt[:, :], gates[:, :], ACT.Tanh).then_inc(S("gt_ready"), 1)
                for u in range(NB * NF):
                    act.wait_ge(S("hid6_ps"), u + 1)
                    C.activation(hid[:, u // NF, u % NF, :], ps[:, u % NF, :], ACT.Gelu,
                                 bias=b1c[:, u % NF:u % NF + 1]).then_inc(S("hid6"), 1)
                ln_sqrt(1, S("ln_o_var"), S("ln_o_sd"))
                ln_sqrt(1, S("ln_x1_var"), S("ln_x1_sd"))
                act.wait_ge(S("xn6T_ps"), 1)
                C.copy(wT[:, :], flat(ps[:, 0:2, :])).then_inc(S("wT6"), 1)

            @block.vector
            def _(dve):
                w = lambda t: t[:, :, :]
                dve.wait_ge(S("b6_in"), 16 * 8)
                dchain(V.tensor_tensor(w(xt), w(xt), every_tile(row6["b2"]), ALU.add))
                dve.wait_ge(S("out6_ps"), 1)
                dchain(V.tensor_tensor(w(xt), ps[:, 4:6, :].rearrange("p a (b d) -> p (a b) d", d=D), w(xt), ALU.add))
                ln_stats(xt, S("ln_o_var"))
                ln_apply(yo, xt, S("ln_o_sd"), 1, S("yo_ready"))
                dve.wait_ge(S("yo_ready"), NT)
                dchain(V.tensor_tensor(w(yo), w(yo), every_tile(row6["g_norm_out"]), ALU.mult))
                dchain(V.tensor_tensor(w(yo), w(yo), every_tile(row6["b_norm_out"]), ALU.add))
                dve.wait_ge(S("gt_ready"), 1)
                dchain(V.scalar_tensor_tensor(flat(x_sb), flat(yo), gt[:, 0:1], flat(x_sb), ALU.mult, ALU.add))
                ln_stats(x_sb, S("ln_x1_var"))
                ln_apply(xn, x_sb, S("ln_x1_sd"), 1, S("xn6"))

    q1s = ExitStack()
    Q1 = sb(q1s, "Q1", [P, H1, T], BF16)
    Q1v = Q1[:, :, :].rearrange("p (j a) t -> p j a t", a=2)
    with ExitStack() as b7:
        u1 = sb(b7, "u1", [P, RANK])
        v1w = sb(b7, "v1w", [RANK, HID])
        b1c = sb(b7, "b1c7", [P, NF])
        u2 = sb(b7, "u2", [P, NF, RANK])
        v2w = sb(b7, "v2w", [RANK, D])
        b2r = sb(b7, "b2r7", [P, D])
        lowT = sb(b7, "lowT", [RANK, T])
        lowT2 = sb(b7, "lowT2", [RANK, T])
        hid = sb(b7, "hid7", [P, NB, NF, TB])
        yo = sb(b7, "yo7", [P, NT, D])
        wq1 = sb(b7, "wq1", [P, P])
        bq1 = sb(b7, "bq1", [P, 1])
        bq1s = sb(b7, "bq1s", [P, 1])
        qs = sb(b7, "qs7", [P, T])
        ql = sb(b7, "ql7", [P, LEVELS, T], BF16)
        qabs, bound = sb(b7, "qabs", [P, 1]), sb(b7, "bound", [P, 1])
        boundh, bound1 = sb(b7, "boundh", [1, H1]), sb(b7, "bound1", [1, 1])
        SC1 = float(DH1) ** -0.5
        with nc.Block() as block:
            @block.sync
            def _(sp):
                for dst, name in ((u1, "L0_ffn_U1"), (v1w, "L0_ffn_V1"), (v2w, "L0_ffn_V2"), (wq1, "L1_xattn_wq")):
                    sp.dma_start(dst[:, :], A[name]).then_inc(S("b7_in"), 16)
                sp.dma_start(u2[:, :, :], A["L0_ffn_U2"].rearrange("(f p) r -> p f r", p=P)).then_inc(S("b7_in"), 16)
                sp.dma_start(b1c[:, :], A["L0_ffn_b1"].rearrange("(f p) -> p f", p=P),
                             allow_slow_non_contiguous=True).then_inc(S("b7_in"), 16)
                sp.dma_start(bq1[:, :], A["L1_xattn_bq"].rearrange("(p a) -> p a", a=1)).then_inc(S("b7_in"), 16)
                sp.dma_start(b2r[:, :], A["L0_ffn_b2"].partition_broadcast(P)).then_inc(S("b7_in"), 16)
                sp.wait_ge(S("q1_split"), 1)
                sp.dma_start(q1_parts.rearrange("l p t -> p l t"), ql[:, :, :]).then_inc(S("q1_out"), 16)
                sp.wait_ge(S("q1_out"), 16)
                sp.wait_ge(S("q1_zero"), 1)
                for par in range(2):
                    r0 = 64 * par
                    for r, lv in enumerate((0, 0, 0, 1, 1, 2)):
                        sp.dma_start(Q1v[r0 + DH1 * r:r0 + DH1 * (r + 1), :, par, :],
                                     q1_parts[lv].rearrange("(j a d) t -> d j a t", a=2, d=DH1)[:, :, par, :])\
                          .then_inc(S("q1_gathered"), 16)
                    sp.dma_start(Q1v[r0 + ROW1 + LEVELS:r0 + ROW1 + LEVELS + 1, :, par, :],
                                 mask_line[2:3, 0:T].unsqueeze(1).to_broadcast([1, H1 // 2, T]))\
                        .then_inc(S("q1_gathered"), 16)
                sp.wait_ge(S("q1_gathered"), 16 * 14)

            @block.gpsimd
            def _(pool):
                PL.memset(Q1[:, :, :], 0.0).then_inc(S("q1_zero"), 1)

            @block.tensor
            def _(pe):
                pe.wait_ge(S("b7_in"), 16 * 8)
                for tb in range(NB):
                    last = M.matmul(ps[0:RANK, 6 + tb, :], u1[:, :], wT[:, tb * TB:(tb + 1) * TB], start=True, stop=True)
                last.then_inc(S("low_ps"), 1)
                pe.wait_ge(S("low_sb"), 1)
                for tb in range(NB):
                    for f in range(NF):
                        if tb:
                            pe.wait_ge(S("hid7"), (tb - 1) * NF + f + 1)
                        M.matmul(ps[:, f, :], v1w[:, f * P:(f + 1) * P], lowT[:, tb * TB:(tb + 1) * TB],
                                 start=True, stop=True).then_inc(S("hid7_ps"), 1)
                for tb in range(NB):
                    pe.wait_ge(S("hid7"), (tb + 1) * NF)
                    for f in range(NF):
                        last = M.matmul(ps[0:RANK, 6 + tb, :], u2[:, f, :], hid[:, tb, f, :], start=f == 0, stop=f == NF - 1)
                last.then_inc(S("low_ps"), 1)
                pe.wait_ge(S("low_sb"), 2)
                for t in range(NT):
                    last = M.matmul(ps[:, 4 + t // 4, (t % 4) * P:(t % 4 + 1) * P], lowT2[:, t * P:(t + 1) * P], v2w[:, :],
                                    start=True, stop=True)
                last.then_inc(S("out7_ps"), 1)
                pe.wait_ge(S("xn7"), NT)
                transpose_tiles(xn, 0, S("xn7T_ps"))
                pe.wait_ge(S("wT7"), 1)
                for tb in range(NB):
                    last = M.matmul(ps[:, 2 + tb, :], wq1[:, :], wT[:, tb * TB:(tb + 1) * TB], start=True, stop=True)
                last.then_inc(S("q1_ps"), 1)
                pe.wait_ge(S("bound_ready"), 1)
                M.matmul(ps[0:1, 6, 0:P], bound[:, :], ident[:, :], start=True, stop=True).then_inc(S("bound_ps"), 1)

            @block.scalar
            def _(act):
                act.wait_ge(S("low_ps"), 1)
                C.copy(lowT[:, :], flat(ps[0:RANK, 6:8, :])).then_inc(S("low_sb"), 1)
                for u in range(NB * NF):
                    act.wait_ge(S("hid7_ps"), u + 1)
                    C.activation(hid[:, u // NF, u % NF, :], ps[:, u % NF, :], ACT.Gelu_apprx_tanh,
                                 bias=b1c[:, u % NF:u % NF + 1]).then_inc(S("hid7"), 1)
                act.wait_ge(S("low_ps"), 2)
                C.copy(lowT2[:, :], flat(ps[0:RANK, 6:8, :])).then_inc(S("low_sb"), 1)
                ln_sqrt(1, S("ln_x2_var"), S("ln_x2_sd"))
                act.wait_ge(S("xn7T_ps"), 1)
                C.copy(wT[:, :], flat(ps[:, 0:2, :])).then_inc(S("wT7"), 1)
                act.wait_ge(S("q1_ps"), 1)
                act.wait_ge(S("bq1s"), 1)
                C.activation(qs[:, :], flat(ps[:, 2:4, :]), ACT.Identity, bias=bq1s[:, 0:1], scale=SC1).then_inc(S("q1_sb"), 1)

            @block.vector
            def _(dve):
                w = lambda t: t[:, :, :]
                dve.wait_ge(S("b7_in"), 16 * 8)
                V.tensor_scalar(bq1s[:, :], bq1[:, :], SC1, None, ALU.mult).then_inc(S("bq1s"), 1)
                dve.wait_ge(S("out7_ps"), 1)
                dchain(V.tensor_tensor(w(yo), ps[:, 4:6, :].rearrange("p a (b d) -> p (a b) d", d=D), every_tile(b2r), ALU.add))
                dchain(V.scalar_tensor_tensor(flat(x_sb), flat(yo), gt[:, 2:3], flat(x_sb), ALU.mult, ALU.add))
                ln_stats(x_sb, S("ln_x2_var"))
                ln_apply(xn, x_sb, S("ln_x2_sd"), 1, S("xn7"))
                dve.wait_ge(S("q1_sb"), 1)
                dchain(V.tensor_reduce(qabs[:, :], qs[:, :], AX.X, ALU.max, apply_absolute_value=True))
                dchain(V.reduce_max(kabs1[:, :], kabs[:, :], AX.X))
                V.tensor_tensor(bound[:, :], qabs[:, :], kabs1[:, :], ALU.mult).then_inc(S("bound_ready"), 1)
                dchain(V.tensor_copy(ql[:, 0, :], qs[:, :]))
                dchain(V.tensor_tensor(qs[:, :], qs[:, :], ql[:, 0, :], ALU.subtract))
                dchain(V.tensor_copy(ql[:, 1, :], qs[:, :]))
                V.tensor_tensor(ql[:, 2, :], qs[:, :], ql[:, 1, :], ALU.subtract).then_inc(S("q1_split"), 1)
                dve.wait_ge(S("bound_ps"), 1)
                dchain(V.reduce_sum(boundh[:, :], ps[0:1, 6, 0:P].rearrange("p (h d) -> p h d", d=DH1), AX.X))
                dchain(V.reduce_max(bound1[:, :], boundh[:, :], AX.X))
                dchain(V.tensor_scalar(bound1[:, :], bound1[:, :], EXP_RANGE, None, ALU.is_gt))
                dchain(V.tensor_copy(general[0:1, 1:2], bound1[:, :]))

    l1_general = nc.values_load(general[0:1, 1:2], min_val=0, max_val=1)
    with nc.If(l1_general > 0):
        with ExitStack() as b7g:
            gmax = sb(b7g, "gmax", [P, 16])
            nshift = sb(b7g, "nshift", [P, H1 * NT])
            nsT = sb(b7g, "nsT", [P, P])
            nsR = sb(b7g, "nsR", [P, P])
            nsl = sb(b7g, "nsl", [P, LEVELS, P], BF16)
            NBK = -(-GP // 512)
            BANKS = 7
            HALF = H1 * NT // 2
            gchain = Chain(V, S("g1_chain"))
            with nc.Block() as block:
                @block.gpsimd
                def _(pool):
                    take_part(pool)

                @block.sync
                def _(sp):
                    sp.wait_ge(S("g1_scored"), HALF * NBK)
                    for quad in range(2, NQ):
                        load_quad(sp, quad, S("g1_late"), S("g1_late"))
                    sp.wait_ge(S("g1_scored"), 2 * HALF * NBK)
                    sp.wait_ge(S("g1_late"), 16 * 2 * (KIN + 1))
                    for quad in range(2):
                        load_quad(sp, quad, S("g1_again"), S("g1_again"))
                    sp.wait_ge(S("g1_again"), 16 * 2 * (KIN + 1))
                    sp.wait_ge(S("nsl_ready"), 1)
                    sp.dma_start(ns_lines.rearrange("l (i p) -> i l p", p=P), nsl[:, :, :]).then_inc(S("ns_out"), 16)
                    sp.wait_ge(S("ns_out"), 16)
                    for par in range(2):
                        r0 = 64 * par + ROW1
                        sp.dma_start(Q1v[r0:r0 + LEVELS, :, par, :],
                                     ns_lines.rearrange("l (j a t) -> l j a t", a=2, t=T)[:, :, par, :])\
                            .then_inc(S("ns_in"), 16)
                    sp.wait_ge(S("ns_in"), 32)

                @block.tensor
                def _(pe):
                    for half in range(2):
                        if half:
                            pe.wait_ge(S("g1_late"), 16 * 2 * (KIN + 1))
                        with pe.Fori(0, HALF) as i:
                            n = i + half * HALF
                            for j in range(NBK):
                                w = min(512, GP - j * 512)
                                used = j - BANKS if j >= BANKS else (j + BANKS - NBK if j + BANKS < NBK else j - NBK)
                                pe.wait_ge(S("g1_read"), n * NBK + (NBK + used + 1))
                                M.matmul(ps[:, j % BANKS, 0:w],
                                         Q1[:, :, :].rearrange("p h t -> p (h t)")[:, bass.ds(n * P, P)],
                                         K1[:, :, :, :].rearrange("p q j g -> p (q j g)")
                                         [:, bass.ds((i // (2 * NT)) * GP + j * 512, w)],
                                         start=True, stop=True).then_inc(S("g1_scored"), 1)
                    pe.wait_ge(S("nshift_ready"), 1)
                    M.transpose(ps[:, 7, 0:P], nshift[:, :], ident[:, :]).then_inc(S("nsT_ps"), 1)

                @block.scalar
                def _(act):
                    act.wait_ge(S("nsT_ps"), 1)
                    C.copy(nsT[:, :], ps[:, 7, 0:P]).then_inc(S("nsT_sb"), 1)

                @block.vector
                def _(dve):
                    dve.sem_inc(S("g1_read"), NBK)
                    with dve.Fori(0, H1 * NT) as i:
                        gchain.loop(i, 1)
                        for j in range(NBK):
                            w = min(512, GP - j * 512)
                            dve.wait_ge(S("g1_scored"), i * NBK + j + 1)
                            V.reduce_max(gmax[:, j:j + 1], ps[:, j % BANKS, 0:w], AX.X).then_inc(S("g1_read"), 1)
                        dve.wait_ge(S("g1_read"), i * NBK + NBK + NBK)
                        gchain(V.reduce_max(nshift[:, bass.ds(i, 1)], gmax[:, 0:NBK], AX.X))
                    gchain.looped(1, H1 * NT)
                    V.tensor_scalar(nshift[:, :], nshift[:, :], -1.0, None, ALU.mult).then_inc(S("nshift_ready"), 1)
                    dve.wait_ge(S("nsT_sb"), 1)
                    gchain(V.tensor_copy(nsl[:, 0, :], nsT[:, :]))
                    gchain(V.tensor_tensor(nsR[:, :], nsT[:, :], nsl[:, 0, :], ALU.subtract))
                    gchain(V.tensor_copy(nsl[:, 1, :], nsR[:, :]))
                    V.tensor_tensor(nsl[:, 2, :], nsR[:, :], nsl[:, 1, :], ALU.subtract).then_inc(S("nsl_ready"), 1)

    next_stage()

    with ExitStack() as b8:
        ex1 = sb(b8, "ex1", [P, 2 * UNROLL, 2, TB])
        UNITS = 2 * UNROLL
        RING = 3
        NPASS = NQ * NB
        with nc.Block() as block:
            @block.gpsimd
            def _(pool):
                for w in range(NPASS):
                    quad, tb = divmod(w, NB)
                    if quad >= 2:
                        pool.wait_ge(S(f"v1_in{quad % 2}"), 16 * (quad // 2))

                    def place(k, g, n, first):
                        if not first:
                            pool.wait_ge(S("summed1"), n - UNROLL + 1)
                        PL.tensor_copy(vs1[:, k, :, 0:VW].unsqueeze(1),
                                       V1[:, quad % 2, bass.ds(g, 1), :].rearrange("p c (h v) -> p c h v", v=VW))\
                            .then_inc(S("v1_placed"), 1)

                    for k in range(UNROLL):
                        place(k, k, w * NG + k, w == 0)
                    with pool.Fori(1, TURNS) as i:
                        for k in range(UNROLL):
                            place(k, i * UNROLL + k, i * UNROLL + (w * NG + k), False)

            @block.sync
            def _(sp):
                for quad in range(2, NQ):
                    sp.wait_ge(S("scored1"), (quad - 1) * NB * 2 * NG)
                    sp.wait_ge(S("v1_placed"), (quad - 1) * NB * NG)
                    load_quad(sp, quad, S(f"k1_in{quad % 2}"), S(f"v1_in{quad % 2}"))

            @block.tensor
            def _(pe):
                for w in range(NPASS):
                    quad, tb = divmod(w, NB)
                    U0, G0 = w * 2 * NG, w * NG
                    if quad >= 2:
                        pe.wait_ge(S(f"k1_in{quad % 2}"), 16 * KIN * (quad // 2))

                    def scores(k, g, free):
                        if free is not None:
                            pe.wait_ge(S("exped1"), free)
                        for hh in range(2):
                            last = M.matmul(ps[:, 2 * (k % RING) + hh, :], K1[:, quad % 2, k % 2, bass.ds(g * P, P)],
                                            Q1[:, 4 * quad + 2 * (k % 2) + hh, tb * TB:(tb + 1) * TB], start=True, stop=True)
                        last.then_inc(S("scored1"), 1)

                    def values(t, n, start, stop):
                        pe.wait_ge(S("exped1"), 2 * n + 2)
                        pe.wait_ge(S("v1_placed"), n + 1)
                        if start and w >= 2:
                            pe.wait_ge(S("o1_read"), w - 1)
                        for j in range(4):
                            last = M.matmul(ps[32 * j:32 * j + 32, 6 + w % 2, :], vs1[:, t, j, :],
                                            ex1[:, 2 * t + j // 2, j % 2, :], start=start, stop=stop,
                                            tile_position=(0, 32 * j))
                        last.then_inc(S("summed1"), 1)

                    def turn(i, first=False, last=False):
                        for t in range(UNROLL):
                            for q in range(2):
                                k = 2 * t + q
                                free = None if first and w == 0 and k < RING else i * UNITS + (U0 + k - RING + 1)
                                scores(k, i * UNROLL + t, free)
                            if not (first and t == 0):
                                n = i * UNROLL + (G0 + t - 1)
                                values((t - 1) % UNROLL, n, first and t == 1, False)
                        if last:
                            values(UNROLL - 1, i * UNROLL + (G0 + UNROLL - 1), False, True)

                    turn(0, first=True)
                    with pe.Fori(1, TURNS - 1) as i:
                        turn(i)
                    turn(TURNS - 1, last=True)

            @block.scalar
            def _(act):
                for w in range(NPASS):
                    U0, G0 = w * 2 * NG, w * NG

                    def unit(k, i, first):
                        act.wait_ge(S("scored1"), i * UNITS + (U0 + k + 1))
                        if not first:
                            act.wait_ge(S("summed1"), i * UNROLL + (G0 + k // 2 - UNROLL + 1))
                        C.activation(ex1[:, k, :, :], ps[:, 2 * (k % RING):2 * (k % RING) + 2, :], ACT.Exp)\
                            .then_inc(S("exped1"), 1)

                    for k in range(UNITS):
                        unit(k, 0, w == 0)
                    with act.Fori(1, TURNS) as i:
                        for k in range(UNITS):
                            unit(k, i, False)

            @block.vector
            def _(dve):
                for w in range(NPASS):
                    quad, tb = divmod(w, NB)
                    dve.wait_ge(S("summed1"), (w + 1) * NG)
                    V.tensor_copy(o1[:, quad, tb * TB:(tb + 1) * TB], ps[:, 6 + w % 2, :]).then_inc(S("o1_read"), 1)

    q1s.close()
    k1s.close()

    moe = ExitStack()
    gw = sb(moe, "gw", [P, E])
    gb = sb(moe, "gb", [P, E])
    w1 = sb(moe, "w1m", [P, E, HID])
    w2 = sb(moe, "w2m", [P, E, NF, D])
    b1c = sb(moe, "b1m", [P, E, NF])
    b2e = sb(moe, "b2m", [E, D])
    sel = sb(moe, "sel", [E, E, P])
    experts = sb(moe, "experts", [P, E])
    row10 = {n: sb(moe, "row10_" + n, [P, D]) for n in ("ln_g", "ln_b")}

    with ExitStack() as b9:
        wo = sb(b9, "wo", [P, D])
        bo = sb(b9, "bo", [P, D])
        rs = sb(b9, "rs", [P, NT, H1])
        on = sb(b9, "on", [P, NT, H1, DH1])
        onT = sb(b9, "onT", [P, T])
        yo = sb(b9, "yo9", [P, NT, D])
        with nc.Block() as block:
            @block.sync
            def _(sp):
                sp.dma_start(wo[:, :], A["L1_xattn_wo"]).then_inc(S("b9_in"), 16)
                sp.dma_start(bo[:, :], A["L1_xattn_bo"].partition_broadcast(P)).then_inc(S("b9_in"), 16)
                sp.dma_start(gw[:, :], A["L1_ffn_gate_w"]).then_inc(S("moe_in"), 16)
                sp.dma_start(gb[:, :], A["L1_ffn_gate_b"].partition_broadcast(P)).then_inc(S("moe_in"), 16)
                sp.dma_start(experts[:, :], A["steps"][0:E].partition_broadcast(P)).then_inc(S("moe_in"), 16)
                sp.dma_start(b2e[:, :], A["L1_ffn_b2"]).then_inc(S("moe_in"), 16)
                sp.dma_start(sel[:, :, :], A["select"]).then_inc(S("moe_in"), 16)
                for e in range(E):
                    sp.dma_start(b1c[:, e, :], A["L1_ffn_b1"][e].rearrange("(f p) -> p f", p=P),
                                 allow_slow_non_contiguous=True).then_inc(S("moe_in"), 16)
                for n, tile in row10.items():
                    sp.dma_start(tile[:, :], A["L1_ffn_" + n].partition_broadcast(P)).then_inc(S("moe_in"), 16)
                sp.dma_start(w1[:, :, :], A["L1_ffn_w1"].rearrange("e d f -> d e f")).then_inc(S("moe_in"), 16)
                sp.dma_start(w2[:, :, :, :].rearrange("p e f d -> p (e f) d"),
                             A["L1_ffn_w2"].rearrange("e (f p) d -> p (e f) d", p=P)).then_inc(S("moe_in"), 16)
                sp.wait_ge(S("moe_in"), 16 * (5 + E + 2 + 2))

            @block.tensor
            def _(pe):
                for t in range(NT):
                    for quad in range(NQ):
                        last = M.transpose(ps[:, t, quad * P:(quad + 1) * P], o1[:, quad, t * P:(t + 1) * P], ident[:, :])
                    last.then_inc(S("o1T_ps"), 1)
                pe.wait_ge(S("on_ready"), NT)
                for t in range(NT):
                    last = M.transpose(ps[:, t // 4, (t % 4) * P:(t % 4 + 1) * P],
                                       on[:, t, :, :].rearrange("p h v -> p (h v)"), ident[:, :])
                last.then_inc(S("onT_ps"), 1)
                pe.wait_ge(S("onT"), 1)
                pe.wait_ge(S("b9_in"), 32)
                for t in range(NT):
                    last = M.matmul(ps[:, 4 + t // 4, (t % 4) * P:(t % 4 + 1) * P], onT[:, t * P:(t + 1) * P], wo[:, :],
                                    start=True, stop=True)
                last.then_inc(S("out9_ps"), 1)
                pe.wait_ge(S("xn9"), NT)
                transpose_tiles(xn, 0, S("xn9T_ps"))

            @block.scalar
            def _(act):
                act.wait_ge(S("onT_ps"), 1)
                C.copy(onT[:, :], flat(ps[:, 0:2, :])).then_inc(S("onT"), 1)
                ln_sqrt(1, S("ln_x3_var"), S("ln_x3_sd"))
                act.wait_ge(S("xn9T_ps"), 1)
                C.copy(wT[:, :], flat(ps[:, 0:2, :])).then_inc(S("wT9"), 1)

            @block.vector
            def _(dve):
                for t in range(NT):
                    dve.wait_ge(S("o1T_ps"), t + 1)
                    rows_ = ps[:, t, :].rearrange("p (h v) -> p h v", v=32)
                    dchain(V.reciprocal(rs[:, t, :], rows_[:, :, DH1]))
                    V.tensor_tensor(on[:, t, :, :], rows_[:, :, 0:DH1],
                                    rs[:, t, :].unsqueeze(2).to_broadcast([P, H1, DH1]), ALU.mult).then_inc(S("on_ready"), 1)
                w = lambda t: t[:, :, :]
                dve.wait_ge(S("b9_in"), 32)
                dve.wait_ge(S("out9_ps"), 1)
                dchain(V.tensor_tensor(w(yo), ps[:, 4:6, :].rearrange("p a (b d) -> p (a b) d", d=D), every_tile(bo), ALU.add))
                dchain(V.scalar_tensor_tensor(flat(x_sb), flat(yo), gt[:, 1:2], flat(x_sb), ALU.mult, ALU.add))
                ln_stats(x_sb, S("ln_x3_var"))
                ln_apply(xn, x_sb, S("ln_x3_sd"), 1, S("xn9"))
    next_stage()

    with ExitStack() as b10:
        lg, lw = sb(b10, "lg", [P, NT, E]), sb(b10, "lw", [P, NT, E])
        t8 = sb(b10, "t8", [P, NT, 8])
        i8 = sb(b10, "i8", [P, NT, 8], U32)
        i8f = sb(b10, "i8f", [P, NT, 2])
        keep, keep2 = sb(b10, "keep", [P, NT, E]), sb(b10, "keep2", [P, NT, E])
        pr = sb(b10, "pr", [P, NT, E])
        psum_ = sb(b10, "psm", [P, NT])
        pT = sb(b10, "pT", [E, T])
        hid = sb(b10, "hidm", [P, 2, NF, TB])
        hidp = sb(b10, "hidp", [P, 2, NF, TB])
        oT = sb(b10, "oT", [P, T])
        oo = sb(b10, "oo", [P, NT, D])
        NJ = E * NB
        with nc.Block() as block:
            @block.sync
            def _(sp):
                sp.wait_ge(S("x4_ready"), 1)
                sp.dma_start(A["out"][0].rearrange("(n p) d -> p n d", p=P), x_sb[:, :, :]).then_inc(S("stored"), 16)
                sp.wait_ge(S("stored"), 16)

            @block.tensor
            def _(pe):
                for t in range(NT):
                    last = M.matmul(ps[:, 0, t * E:(t + 1) * E], wT[:, t * P:(t + 1) * P], gw[:, :], start=True, stop=True)
                last.then_inc(S("logits_ps"), 1)

                def hidden(j):
                    e, tb = divmod(j, NB)
                    for f in range(NF):
                        if j:
                            pe.wait_ge(S("hidm"), (j - 1) * NF + f + 1)
                        elif f == 0:
                            pe.wait_ge(S("logits_read"), 1)
                        M.matmul(ps[:, f, :], w1[:, e, f * P:(f + 1) * P], wT[:, tb * TB:(tb + 1) * TB],
                                 start=True, stop=True).then_inc(S("hidm_ps"), 1)

                def share(j):
                    e, tb = divmod(j, NB)
                    if j >= 2:
                        pe.wait_ge(S("hidp"), j - 1)
                    M.matmul(ps[:, 4 + j % 2, :], sel[:, e, :], pT[:, tb * TB:(tb + 1) * TB], start=True, stop=True)\
                        .then_inc(S("share_ps"), 1)

                hidden(0)
                pe.wait_ge(S("pr_ready"), 1)
                for t in range(NT):
                    last = M.transpose(ps[0:E, 4 + t // 4, (t % 4) * P:(t % 4 + 1) * P], pr[:, t, :], ident[:, :])
                last.then_inc(S("pT_ps"), 1)
                pe.wait_ge(S("pT_ready"), 1)
                share(0)
                for j in range(NJ):
                    e, tb = divmod(j, NB)
                    if j + 1 < NJ:
                        hidden(j + 1)
                        share(j + 1)
                    pe.wait_ge(S("hidp"), j + 1)
                    for f in range(NF):
                        M.matmul(ps[:, 6 + tb, :], w2[:, e, f, :], hidp[:, j % 2, f, :], start=e == 0 and f == 0, stop=False)\
                            .then_inc(S("outm"), 1)
                for tb in range(NB):
                    last = M.matmul(ps[:, 6 + tb, :], b2e[:, :], pT[:, tb * TB:(tb + 1) * TB], start=False, stop=True)
                last.then_inc(S("oT_ps"), 1)
                pe.wait_ge(S("oT"), 1)
                for t in range(NT):
                    last = M.transpose(ps[:, 4 + t // 4, (t % 4) * P:(t % 4 + 1) * P], oT[:, t * P:(t + 1) * P], ident[:, :])
                last.then_inc(S("oo_ps"), 1)

            @block.scalar
            def _(act):
                act.wait_ge(S("lw_ready"), 1)
                C.activation(pr[:, :, :], lw[:, :, :], ACT.Exp).then_inc(S("pr_exp"), 1)
                act.wait_ge(S("pT_ps"), 1)
                C.copy(pT[:, :], flat(ps[0:E, 4:6, :])).then_inc(S("pT_ready"), 1)
                for j in range(NJ):
                    e, tb = divmod(j, NB)
                    for f in range(NF):
                        act.wait_ge(S("hidm_ps"), j * NF + f + 1)
                        if j >= 2:
                            act.wait_ge(S("hidp"), j - 1)
                        C.activation(hid[:, j % 2, f, :], ps[:, f, :], ACT.Gelu, bias=b1c[:, e, f:f + 1]).then_inc(S("hidm"), 1)
                act.wait_ge(S("oT_ps"), 1)
                C.copy(oT[:, :], flat(ps[:, 6:8, :])).then_inc(S("oT"), 1)
                ln_sqrt(1, S("ln_m_var"), S("ln_m_sd"))

            @block.vector
            def _(dve):
                w = lambda t: t[:, :, :]
                over_e = lambda t: t.unsqueeze(2).to_broadcast([P, NT, E])
                dve.wait_ge(S("logits_ps"), 1)
                dchain(V.tensor_tensor(w(lg), ps[:, 0, 0:NT * E].rearrange("p (t e) -> p t e", e=E),
                                       gb[:, :].unsqueeze(1).to_broadcast([P, NT, E]), ALU.add))
                V.tensor_scalar(w(lg), w(lg), float(1 / 0.9), None, ALU.mult).then_inc(S("logits_read"), 1)
                dve.wait_ge(S("logits_read"), 1)
                for t in range(NT):
                    V.max(t8[:, t, :], lg[:, t, :]).then_inc(S("t8"), 1)
                dve.wait_ge(S("t8"), NT)
                V.tensor_tensor(w(lw), w(lg), over_e(t8[:, :, 0]), ALU.subtract).then_inc(S("lw_ready"), 1)
                for t in range(NT):
                    V.max_index(i8[:, t, :], t8[:, t, :], lg[:, t, :]).then_inc(S("i8"), 1)
                dve.wait_ge(S("i8"), NT)
                dchain(V.tensor_copy(w(i8f), i8[:, :, 0:2]))
                each = experts[:, :].unsqueeze(1).to_broadcast([P, NT, E])
                dchain(V.tensor_tensor(w(keep), each, over_e(i8f[:, :, 0]), ALU.is_equal))
                dchain(V.tensor_tensor(w(keep2), each, over_e(i8f[:, :, 1]), ALU.is_equal))
                dchain(V.tensor_tensor(w(keep), w(keep), w(keep2), ALU.add))
                dve.wait_ge(S("pr_exp"), 1)
                dchain(V.tensor_tensor(w(pr), w(pr), w(keep), ALU.mult))
                dchain(V.reduce_sum(psum_[:, :], w(pr), AX.X))
                dchain(V.reciprocal(psum_[:, :], psum_[:, :]))
                V.tensor_tensor(w(pr), w(pr), over_e(psum_[:, :]), ALU.mult).then_inc(S("pr_ready"), 1)
                for j in range(NJ):
                    dve.wait_ge(S("share_ps"), j + 1)
                    dve.wait_ge(S("hidm"), (j + 1) * NF)
                    if j >= 2:
                        dve.wait_ge(S("outm"), (j - 1) * NF)
                    V.tensor_tensor(hidp[:, j % 2, :, :], hid[:, j % 2, :, :],
                                    ps[:, 4 + j % 2, :].unsqueeze(1).to_broadcast([P, NF, TB]), ALU.mult).then_inc(S("hidp"), 1)
                dve.wait_ge(S("oo_ps"), 1)
                dchain(V.tensor_copy(w(oo), ps[:, 4:6, :].rearrange("p a (b d) -> p (a b) d", d=D)))
                ln_stats(oo, S("ln_m_var"))
                ln_apply(xn, oo, S("ln_m_sd"), 1, S("xn10"))
                dve.wait_ge(S("xn10"), NT)
                dchain(V.tensor_tensor(w(xn), w(xn), every_tile(row10["ln_g"]), ALU.mult))
                dchain(V.tensor_tensor(w(xn), w(xn), every_tile(row10["ln_b"]), ALU.add))
                V.scalar_tensor_tensor(flat(x_sb), flat(xn), gt[:, 3:4], flat(x_sb), ALU.mult, ALU.add).then_inc(S("x4_ready"), 1)

    next_stage()
    moe.close()
    oq.close()


def constants():
    n = 2 * P
    om = 2 * np.pi * (np.arange(P) + 0.5) / n
    j = np.arange(P)
    fx = np.exp(-1j * np.outer(j, om))
    fk1 = np.exp(-1j * np.outer(P - 1 + j, om))
    fk0 = np.exp(-1j * np.outer(j - 1, om))
    fk0[0] = 0
    inv = np.exp(1j * np.outer(om, P - 1 + j)) / P
    dft = np.stack([fx.real, fx.imag, fk0.real, fk0.imag, fk1.real, fk1.imag, inv.real, -inv.real, -inv.imag], axis=1)
    return {"ident": np.eye(P, dtype=np.float32), "steps": np.arange(KTAP, dtype=np.float32),
            "select": np.ascontiguousarray(np.repeat(np.eye(E, dtype=np.float32)[:, :, None], P, axis=2)),
            "dft": np.ascontiguousarray(dft.astype(np.float32))}


def kernel(**inputs):
    import concourse.bacc as _bacc
    from concourse.bass_utils import run_bass_kernel_spmd as _run

    nc = _bacc.Bacc("TRN2", target_bir_lowering=False, num_devices=1)
    arrays, args = {}, {}
    for name, a in list(inputs.items()) + list(constants().items()):
        a = np.ascontiguousarray(a)
        if a.dtype.kind == "b":
            a = a.view(np.uint8)
        if a.ndim == 0:
            a = a.reshape(1)
        arrays[f"in_{name}"] = a
        args[name] = nc.dram_tensor(f"in_{name}", a.shape, mybir.dt.from_np(a.dtype), kind="ExternalInput").ap()
    args["out"] = nc.dram_tensor("out", (1, T, D), F32, kind="ExternalOutput").ap()
    build(nc, args)
    r = _run(nc, [arrays], core_ids=[0])
    return r.results[0]["out"]
```

```python
import numpy as np
import concourse.bass as bass
from concourse import mybir
from contextlib import ExitStack

F32 = mybir.dt.float32
BF16 = mybir.dt.bfloat16
U8 = mybir.dt.uint8
U32 = mybir.dt.uint32
I32 = mybir.dt.int32
ALU = mybir.AluOpType
ACT = mybir.ActivationFunctionType
AX = mybir.AxisListType

P = 128
T = 1024
NT = T // P
TB = 512
NB = T // TB
D = 128
DC = 96
G = 6404
NG = -(-G // P)
GP = NG * P
GROUP = 512
NGROUP = -(-GP // GROUP)
H0, DH0, TOPK = 4, 32, 32
H1, DH1 = 16, 8
VW = DH1 + 1
NS = 64
KTAP = 32
HID = 512
RANK = 32
E = 8
LEVELS = 3
PIECE = 128
NPIECE = G // PIECE
UNROLL = 3
TURNS = NG // UNROLL
MASKED = -1.0e30
LOWEST = -3.0e38
EXP_RANGE = 60.0
LN_EPS = 1e-5
ROUND = 12582912.0
assert GP == NG * P and NG % UNROLL == 0


SPARE = []


def take_wait(eng, spare=SPARE):
    eng.sem_inc(spare[0], 1)


def take_part(eng, spare=SPARE):
    eng.sem_inc(spare[0], 1)


class Chain:

    def __init__(self, eng, sem):
        self.eng, self.sem, self.n, self.turn = eng, sem, 0, 0

    def __call__(self, ins, before_max=False):
        ins.then_inc(self.sem, 1)
        self.n += 1
        self.eng.wait_ge(self.sem, self.turn + self.n)
        if before_max:
            take_wait(self.eng)

    def loop(self, i, steps):
        self.turn = i * steps

    def looped(self, steps, turns):
        self.turn = 0
        self.n += steps * (turns - 1)


def build(nc, A):
    with ExitStack() as whole:
        program(nc, A, whole)


def program(nc, A, whole):
    stage_sems = {}
    stage = [0]

    def S(name):
        if name not in stage_sems:
            stage_sems[name] = nc.alloc_semaphore(name=f"{name}_{stage[0]}")
        return stage_sems[name]

    def next_stage():
        nc.clear_and_free_semaphores(list(stage_sems.values()))
        nc.all_engine_barrier()
        stage_sems.clear()
        stage[0] += 1
        for chain, name in chains:
            chain.sem, chain.n = S(name), 0
        ln_stats.n = 0


    def sb(ctx, name, shape, dt=F32):
        return ctx.enter_context(nc.sbuf_tensor(name, shape, dt))

    SPARE[:] = [whole.enter_context(nc.semaphore("spare"))]
    V, C, M, PL = nc.vector, nc.scalar, nc.tensor, nc.gpsimd
    dchain = Chain(V, S("dve_chain"))
    achain = Chain(C, S("act_chain"))
    pchain = Chain(PL, S("pool_chain"))
    chains = ((dchain, "dve_chain"), (achain, "act_chain"), (pchain, "pool_chain"))

    ps = whole.enter_context(nc.psum_tensor("ps", [P, 8, 512], F32))

    k1_parts = nc.dram_tensor("k1_parts", [LEVELS, P, GP], BF16).ap()
    v1_rows = nc.dram_tensor("v1_rows", [P, NG, H1 * VW], F32).ap()
    ns_lines = nc.dram_tensor("ns_lines", [LEVELS, H1 * T], BF16).ap()
    mask_line = nc.dram_tensor("mask_line", [3, GP], BF16).ap()

    ident = sb(whole, "ident", [P, P])
    x_sb = sb(whole, "x_sb", [P, NT, D])
    xn = sb(whole, "xn", [P, NT, D])
    gates = sb(whole, "gates", [P, 4])
    ones = sb(whole, "ones", [P, 1])
    general = sb(whole, "general", [1, 2], I32)
    kabs = sb(whole, "kabs", [P, NGROUP])
    kabs1 = sb(whole, "kabs1", [P, 1])
    quarter = sb(whole, "quarter", [P, 1])
    gt = sb(whole, "gt", [P, 4])
    stats = sb(whole, "stats", [P, NT, 6])
    mv = sb(whole, "mv", [P, NT, 2])
    vare = sb(whole, "vare", [P, NT])
    sdev = sb(whole, "sdev", [P, NT])
    rstd = sb(whole, "rstd", [P, NT])
    c_t = sb(whole, "c_t", [P, NT, D])
    q1_parts = nc.dram_tensor("q1_parts", [LEVELS, P, T], BF16).ap()

    def every_tile(row):
        return row[:, :].unsqueeze(1).to_broadcast([P, NT, D])

    def flat(tile):
        return tile[:, :, :].rearrange("p a b -> p (a b)")

    def ln_stats(src, ready, wait=True):
        for t in range(NT):
            V.bn_stats(stats[:, t, :], src[:, t, :]).then_inc(S("ln_stats"), 1)
        ln_stats.n += NT
        V.wait_ge(S("ln_stats"), ln_stats.n)
        for t in range(NT):
            last = V.bn_aggr(mv[:, t, :], stats[:, t, :])
            last.then_inc(S("ln_stats"), 1)
        ln_stats.n += NT
        V.wait_ge(S("ln_stats"), ln_stats.n)
        V.tensor_scalar(vare[:, :], mv[:, :, 1], LN_EPS, None, ALU.add).then_inc(ready, 1)

    ln_stats.n = 0

    def ln_sqrt(count, ready, done):
        C.wait_ge(ready, count)
        C.activation(sdev[:, :], vare[:, :], ACT.Sqrt).then_inc(done, 1)

    def ln_apply(dst, src, done, count, out_sem):
        V.wait_ge(done, count)
        dchain(V.reciprocal(rstd[:, :], sdev[:, :]))
        for t in range(NT):
            V.tensor_scalar(dst[:, t, :], src[:, t, :], mv[:, t, 0:1], rstd[:, t:t + 1],
                            ALU.subtract, ALU.mult).then_inc(out_sem, 1)

    def transpose_tiles(src, bank, done):
        for t in range(NT):
            last = M.transpose(ps[:, bank + t // 4, (t % 4) * P:(t % 4 + 1) * P], src[:, t, :], ident[:, :])
        last.then_inc(done, 1)

    taps = sb(whole, "taps", [P, NT, D])

    l0 = ExitStack()
    K0 = sb(l0, "K0", [P, GP])
    Q0 = sb(l0, "Q0", [P, T + P])
    V0 = sb(l0, "V0", [P, NG, D])
    opened = sb(l0, "opened", [P, 1])

    with ExitStack() as b1:
        xnT = flat(c_t)
        wq0 = sb(b1, "wq0", [P, P])
        wk0 = sb(b1, "wk0", [DC, P])
        wk1 = sb(b1, "wk1", [DC, P])
        wv = sb(b1, "wv", [DC, 2 * P])
        bk1 = sb(b1, "bk1", [P, 1])
        bv1 = sb(b1, "bv1", [P, P])
        NR = 3
        ctx_in = sb(b1, "ctx_in", [P, NR, 4, DC])
        ctxT = sb(b1, "ctxT", [DC, 2, GROUP])
        res1 = sb(b1, "res1", [P, GROUP])
        k1f = sb(b1, "k1f", [P, 2, GROUP])
        kl1 = sb(b1, "kl1", [P, 2, LEVELS, GROUP], BF16)
        v1g = sb(b1, "v1g", [P, 2, 4, H1, VW])
        mask8 = sb(b1, "mask8", [P, NG], U8)
        maskf = sb(b1, "maskf", [P, 3, NG], BF16)
        openf = sb(b1, "openf", [P, NG])
        lastv = G - (NG - 1) * P

        small = lambda name, n=NS: sb(b1, name, [P, n])
        a_re, a_im, c_re, c_im = (small(n) for n in ("a_re", "a_im", "c_re", "c_im"))
        ldt, dt = small("ldt", 1), small("dt", 1)
        rr, tau, z, q, e1 = (small(n) for n in ("rr", "tau", "z", "q", "e1"))
        sh, sn, cs = (small(n) for n in ("sh", "sn", "cs"))
        er, ei, nr, ni, den, t1, t2 = (small(n) for n in ("er", "ei", "nr", "ni", "den", "t1", "t2"))
        rows = sb(b1, "rows", [P, 4, 2 * NS])
        rowsT = sb(b1, "rowsT", [P, 4, D])
        turnsA = sb(b1, "turnsA", [P, D])
        rateA = sb(b1, "rateA", [P, D])
        steps = sb(b1, "steps", [P, KTAP])
        dskip = sb(b1, "dskip", [1, D])
        table = lambda name: sb(b1, name, [P, KTAP, D])
        phase, mag, work = table("phase"), table("mag"), table("work")
        zb, ua, ub = table("zb"), table("ua"), table("ub")
        QUARTER = float(np.pi / 2)
        TURN = float(2 * np.pi * (1 - 1e-7))

        S4_AT = {"coefficients": 0, "rows": 0, "phases": 1, "b_rates": 1, "b_trig": 2, "b_table": 3,
                 "a_rates": 4, "a_trig": 5, "a_table": 7}

        STORE_LAG = 3

        def width(i):
            return min(GROUP, GP - i * GROUP)

        def stores(n, r):
            return (n + 1 - r) // 2

        with nc.Block() as block:
            @block.sync
            def _(sp):
                sp.dma_start(x_sb[:, :, :], A["x"][0].rearrange("(n p) d -> p n d", p=P)).then_inc(S("x_in"), 16)
                sp.dma_start(ident[:, :], A["ident"]).then_inc(S("w_in"), 16)
                sp.dma_start(wk0[:, :], A["L0_xattn_Wk"]).then_inc(S("w_in"), 16)
                sp.dma_start(wk1[:, :], A["L1_xattn_wk"]).then_inc(S("w_in"), 16)
                sp.dma_start(wv[:, 0:P], A["L0_xattn_Wv"]).then_inc(S("w_in"), 16)
                sp.dma_start(wv[:, P:2 * P], A["L1_xattn_wv"]).then_inc(S("w_in"), 16)
                sp.dma_start(wq0[:, :], A["L0_xattn_Wq"]).then_inc(S("w_in"), 16)
                for dst, name in ((a_re, "A_re"), (a_im, "A_im"), (c_re, "C_re"), (c_im, "C_im")):
                    sp.dma_start(dst[:, :], A["L0_xattn_" + name]).then_inc(S("s4_in"), 16)
                sp.dma_start(ldt[:, :], A["L0_xattn_log_dt"].rearrange("(p a) -> p a", a=1)).then_inc(S("s4_in"), 16)
                sp.dma_start(steps[:, :], A["steps"].partition_broadcast(P)).then_inc(S("s4_in"), 16)
                sp.dma_start(dskip[:, :], A["L0_xattn_D_skip"].unsqueeze(0)).then_inc(S("s4_in"), 16)
                def store(j):
                    wj = width(j)
                    sp.wait_ge(S("k1_h"), j + 1)
                    sp.wait_ge(S("k1_split"), j + 1)
                    sp.dma_start(k1_parts[:, :, j * GROUP:j * GROUP + wj].rearrange("l p g -> p l g"),
                                 kl1[:, j % 2, :, 0:wj]).then_inc(S(f"k1_out{j % 2}"), 16)
                    sp.wait_ge(S("v1_evac"), j + 1)
                    sp.dma_start(v1_rows[:, 4 * j:4 * j + wj // P, :],
                                 v1g[:, j % 2, 0:wj // P, :, :].rearrange("p c h v -> p c (h v)"))\
                        .then_inc(S(f"v1_out{j % 2}"), 16)

                for i in range(NGROUP):
                    if i >= STORE_LAG:
                        store(i - STORE_LAG)
                    if i >= NR:
                        sp.wait_ge(S("ctxT_ps"), i - NR + 1)
                    if i == NGROUP - 1:
                        sp.wait_ge(S("ctx_pad"), 1)
                        full = (G - i * GROUP) // P
                        sp.dma_start(ctx_in[:, i % NR, 0:full, :],
                                     A["ctx_768"][0, i * GROUP:i * GROUP + full * P, :]
                                     .rearrange("(c p) d -> p c d", p=P)).then_inc(S(f"ctx_in{i % NR}"), 16)
                        sp.dma_start(ctx_in[0:lastv, i % NR, full, :],
                                     A["ctx_768"][0, G - lastv:G, :]).then_inc(S(f"ctx_in{i % NR}"), 16)
                    else:
                        sp.dma_start(ctx_in[:, i % NR, :, :],
                                     A["ctx_768"][0, i * GROUP:(i + 1) * GROUP, :]
                                     .rearrange("(c p) d -> p c d", p=P)).then_inc(S(f"ctx_in{i % NR}"), 16)
                for i in range(NGROUP - STORE_LAG, NGROUP):
                    store(i)
                sp.wait_ge(S("mask_out"), 48)
                for r in range(2):
                    sp.wait_ge(S(f"k1_out{r}"), 16 * stores(NGROUP, r))
                    sp.wait_ge(S(f"v1_out{r}"), 16 * stores(NGROUP, r))

            @block.gpsimd
            def _(pool):
                def s4_magnitudes(rate):
                    pool.wait_ge(S("rates_ready"), 1)
                    PL.tensor_tensor(mag[:, :, :], rate.unsqueeze(1).to_broadcast([P, KTAP, D]),
                                     steps[:, :].unsqueeze(2).to_broadcast([P, KTAP, D]), ALU.mult)\
                        .then_inc(S("mag_ready"), 1)

                PL.memset(quarter[:, :], QUARTER).then_inc(S("quarter_ready"), 1)
                PL.memset(mask8[:, :], 0).then_inc(S("mask8_zero"), 1)
                pool.wait_ge(S("mask8_zero"), 1)
                PL.memset(v1g[:, :, :, :, DH1:VW], 1.0).then_inc(S("v1_ones"), 1)
                pool.wait_ge(S("v1_ones"), 1)
                PL.dma_start(bv1[:, :], A["L1_xattn_bv"].partition_broadcast(P)).then_inc(S("bv_in"), 16)
                PL.dma_start(bk1[:, :], A["L1_xattn_bk"].rearrange("(p a) -> p a", a=1)).then_inc(S("bk_in"), 16)
                pool.wait_ge(S("mask8_zero"), 1)
                full = G // NG
                PL.dma_start(mask8[0:full, :], A["mask_BxS2_bf1"][0, 0:full * NG].rearrange("(p c) -> p c", c=NG))\
                    .then_inc(S("mask_in"), 16)
                PL.dma_start(mask8[full:full + 1, 0:G - full * NG],
                             A["mask_BxS2_bf1"][0:1, full * NG:G]).then_inc(S("mask_in"), 16)
                pchain(PL.memset(maskf[:, 2, :], 1.0))
                pchain(PL.memset(maskf[:, 1, :], 0.0))
                pchain(PL.affine_select(out=maskf[:, 1, :], in_=maskf[:, 1, :], pattern=[[-1, NG]],
                                        compare_op=ALU.is_gt, fill=MASKED, base=G, channel_multiplier=-NG))
                pool.wait_ge(S("mask_in"), 32)
                pchain(PL.tensor_scalar(maskf[:, 0, :], mask8[:, :], -1.0, -MASKED, ALU.add, ALU.mult))
                for j in range(3):
                    PL.dma_start(mask_line[j, :].rearrange("(p c) -> p c", c=NG), maskf[:, j, :])\
                        .then_inc(S("mask_out"), 16)
                for i in range(NGROUP):
                    w, r = width(i), i % 2
                    pool.wait_ge(S("k1_h"), i + 1)
                    pchain(PL.tensor_tensor(res1[:, 0:w], k1f[:, r, 0:w], kl1[:, r, 0, 0:w], ALU.subtract))
                    pchain(PL.tensor_copy(kl1[:, r, 1, 0:w], res1[:, 0:w]))
                    PL.tensor_tensor(kl1[:, r, 2, 0:w], res1[:, 0:w], kl1[:, r, 1, 0:w], ALU.subtract)\
                        .then_inc(S("k1_split"), 1)
                    pool.wait_ge(S("k1_split"), i + 1)
                    if i == S4_AT["b_rates"]:
                        s4_magnitudes(rowsT[:, 0, :])
                    if i == S4_AT["a_rates"]:
                        pool.wait_ge(S("zb_ready"), 1)
                        s4_magnitudes(rateA[:, :])

            @block.scalar
            def _(act):
                table_ = lambda t: t[:, :, :]

                def trig(dst, rows_, sine):
                    if sine:
                        C.activation(dst[rows_, :, :], phase[rows_, :, :], ACT.Sin, scale=TURN)\
                            .then_inc(S("trig_done"), 1)
                    else:
                        C.activation(dst[rows_, :, :], work[rows_, :, :], ACT.Sin, scale=-TURN, bias=quarter[rows_, 0:1])\
                            .then_inc(S("trig_done"), 1)

                lo, hi = slice(0, NS), slice(NS, P)

                def s4_b_trig():
                    act.wait_ge(S("mag_ready"), 1)
                    C.activation(table_(mag), table_(mag), ACT.Exp).then_inc(S("mag_exp"), 1)
                    act.wait_ge(S("phase_ready"), 1)
                    achain(C.activation(table_(work), table_(phase), ACT.Abs))
                    act.wait_ge(S("quarter_ready"), 1)
                    trig(zb, lo, False)
                    trig(zb, hi, True)
                    act.wait_ge(S("trig_done"), 2)
                    act.sem_inc(S("zb_trig"), 1)

                def s4_a_trig():
                    act.wait_ge(S("phase_ready"), 2)
                    achain(C.activation(table_(work), table_(phase), ACT.Abs))
                    for dst, cos_rows, sin_rows in ((ua, lo, hi), (ub, hi, lo)):
                        trig(dst, cos_rows, False)
                        trig(dst, sin_rows, True)
                    act.wait_ge(S("trig_done"), 6)
                    act.sem_inc(S("ua_trig"), 1)
                    act.wait_ge(S("mag_ready"), 2)
                    C.activation(table_(mag), table_(mag), ACT.Exp).then_inc(S("mag_exp"), 1)

                ln_sqrt(1, S("ln_var"), S("ln_sd"))
                act.wait_ge(S("s4_in"), 16 * 7)
                C.activation(dt[:, :], ldt[:, :], ACT.Exp).then_inc(S("dt_ready"), 1)
                act.wait_ge(S("xnT_ps"), 1)
                C.copy(xnT[:, :], ps[:, 0:2, :].rearrange("p a b -> p (a b)")).then_inc(S("xnT_sb"), 1)
                act.wait_ge(S("q_ps"), 1)
                C.mul(Q0[:, 0:T], ps[:, 2:4, :].rearrange("p a b -> p (a b)"), float(DH0) ** -0.5).then_inc(S("q0"), 1)
                act.wait_ge(S("tau_ready"), 1)
                C.activation(sn[:, :], tau[:, :], ACT.Sin, scale=TURN).then_inc(S("trig_ready"), 1)
                C.activation(sh[:, :], tau[:, :], ACT.Sin, scale=TURN / 2).then_inc(S("trig_ready"), 1)
                act.wait_ge(S("bk_in"), 16)
                for i in range(NGROUP):
                    w, r = width(i), i % 2
                    for n in ([0] if i == 0 else []) + ([i + 1] if i + 1 < NGROUP else []):
                        act.wait_ge(S("ctxT_ps"), n + 1)
                        if n >= 2:
                            act.wait_ge(S("v_ps"), n - 1)
                        C.copy(ctxT[:, n % 2, 0:width(n)], ps[0:DC, 4, 0:width(n)]).then_inc(S("ctxT_sb"), 1)
                    act.wait_ge(S("k_ps"), i + 1)
                    if i >= 2:
                        act.wait_ge(S("k1_split"), i - 1)
                        act.wait_ge(S("k1_seen"), i - 1)
                        act.wait_ge(S("k1_h"), i - 1)
                    C.activation(k1f[:, r, 0:w], ps[:, 6, 0:w], ACT.Identity, bias=bk1[:, 0:1]).then_inc(S("k1_evac"), 1)
                    act.wait_ge(S("k1_evac"), i + 1)
                    if i >= 2:
                        act.wait_ge(S(f"k1_out{r}"), 16 * (i // 2))
                    C.copy(kl1[:, r, 0, 0:w], k1f[:, r, 0:w]).then_inc(S("k1_h"), 1)
                    C.copy(K0[:, i * GROUP:i * GROUP + w], ps[:, 5, 0:w]).then_inc(S("k0_evac"), 1)
                    act.wait_ge(S("v_ps"), i + 1)
                    C.copy(V0[:, 4 * i:4 * i + w // P, :],
                           ps[:, 7, 0:w].rearrange("p (c k) -> p c k", k=P)).then_inc(S("v0_evac"), 1)
                    if i == S4_AT["b_trig"]:
                        s4_b_trig()
                    if i == S4_AT["a_trig"]:
                        s4_a_trig()

            @block.vector
            def _(dve):
                tt = lambda o, a, b, op: dchain(V.tensor_tensor(o, a, b, op))
                ts = lambda o, a, s1, s2, o1, o2=ALU.bypass: dchain(V.tensor_scalar(o, a, s1, s2, o1, o2))
                a = lambda t: t[:, :]
                over_d = lambda t: t.unsqueeze(1).to_broadcast([P, KTAP, D])
                over_steps = steps[:, :].unsqueeze(2).to_broadcast([P, KTAP, D])
                table_ = lambda t: t[:, :, :]

                def phases(turns):
                    tt(table_(phase), over_d(turns), over_steps, ALU.mult)
                    ts(table_(work), table_(phase), ROUND, ROUND, ALU.add, ALU.subtract)
                    V.tensor_tensor(table_(phase), table_(phase), table_(work), ALU.subtract).then_inc(S("phase_ready"), 1)

                def s4_rates():
                    dve.wait_ge(S("dt_ready"), 1)
                    dve.wait_ge(S("s4_in"), 16 * 7)
                    ts(a(rr), a(a_re), dt[:, 0:1], None, ALU.mult)
                    ts(a(t1), a(a_im), dt[:, 0:1], float(0.5 / np.pi), ALU.mult, ALU.mult)
                    ts(a(t2), a(t1), ROUND, ROUND, ALU.add, ALU.subtract)
                    V.tensor_tensor(a(tau), a(t1), a(t2), ALU.subtract).then_inc(S("tau_ready"), 1)
                    ts(a(z), a(rr), -18.0, 1.0 / 16, ALU.max, ALU.mult)
                    ts(a(q), a(z), 1.0 / 9, 1.0, ALU.mult, ALU.add)
                    for k in range(8, 1, -1):
                        dchain(V.scalar_tensor_tensor(a(q), a(z), 1.0 / k, a(q), ALU.mult, ALU.mult))
                        ts(a(q), a(q), 1.0, None, ALU.add)
                    tt(a(e1), a(z), a(q), ALU.mult)
                    for _ in range(4):
                        dchain(V.scalar_tensor_tensor(a(e1), a(e1), 2.0, a(e1), ALU.add, ALU.mult))

                def s4_coefficients():
                    dve.wait_ge(S("trig_ready"), 2)
                    tt(a(t1), a(sh), a(sh), ALU.mult)
                    ts(a(cs), a(t1), -2.0, 1.0, ALU.mult, ALU.add)
                    tt(a(er), a(e1), a(cs), ALU.mult)
                    dchain(V.scalar_tensor_tensor(a(er), a(t1), -2.0, a(er), ALU.mult, ALU.add))
                    dchain(V.scalar_tensor_tensor(a(ei), a(e1), 1.0, a(sn), ALU.add, ALU.mult))
                    tt(a(nr), a(c_re), a(er), ALU.mult)
                    tt(a(t1), a(c_im), a(ei), ALU.mult)
                    tt(a(nr), a(nr), a(t1), ALU.subtract)
                    tt(a(ni), a(c_re), a(ei), ALU.mult)
                    tt(a(t1), a(c_im), a(er), ALU.mult)
                    tt(a(ni), a(ni), a(t1), ALU.add)
                    tt(a(den), a(a_re), a(a_re), ALU.mult)
                    tt(a(t1), a(a_im), a(a_im), ALU.mult)
                    tt(a(den), a(den), a(t1), ALU.add)
                    dchain(V.reciprocal(a(den), a(den)))
                    tt(a(t1), a(nr), a(a_re), ALU.mult)
                    tt(a(t2), a(ni), a(a_im), ALU.mult)
                    tt(a(t1), a(t1), a(t2), ALU.add)
                    tt(a(t1), a(t1), a(den), ALU.mult)
                    tt(a(t2), a(ni), a(a_re), ALU.mult)
                    tt(a(z), a(nr), a(a_im), ALU.mult)
                    tt(a(t2), a(t2), a(z), ALU.subtract)
                    tt(a(t2), a(t2), a(den), ALU.mult)
                    for half, sign in ((slice(0, NS), 2.0), (slice(NS, 2 * NS), -2.0)):
                        dchain(V.tensor_copy(rows[:, 0, half], a(rr)))
                        dchain(V.tensor_copy(rows[:, 1, half], a(tau)))
                        ts(rows[:, 2, half], a(t1), sign, None, ALU.mult)
                        ts(rows[:, 3, half], a(t2), -2.0, None, ALU.mult)
                    V.tensor_copy(dt[:, :], dt[:, :]).then_inc(S("rows_ready"), 1)

                def s4_phases():
                    dve.wait_ge(S("rowsT_ps"), 1)
                    dchain(V.tensor_copy(rowsT[:, :, :], ps[:, 3, :].rearrange("p (a d) -> p a d", d=D)))
                    ts(a(rateA), rowsT[:, 0, :], float(KTAP), None, ALU.mult)
                    ts(a(turnsA), rowsT[:, 1, :], float(KTAP), None, ALU.mult)
                    ts(work[:, 0, :], a(turnsA), ROUND, ROUND, ALU.add, ALU.subtract)
                    tt(a(turnsA), a(turnsA), work[:, 0, :], ALU.subtract)
                    V.tensor_copy(dt[:, :], dt[:, :]).then_inc(S("rates_ready"), 1)
                    phases(rowsT[:, 1, :])

                def s4_b_table():
                    dve.wait_ge(S("zb_trig"), 1)
                    dve.wait_ge(S("mag_exp"), 1)
                    dchain(V.tensor_tensor(table_(zb), table_(zb), table_(mag), ALU.mult))
                    V.tensor_copy(dt[:, :], dt[:, :]).then_inc(S("zb_ready"), 1)
                    phases(a(turnsA))

                def s4_a_table():
                    dve.wait_ge(S("mag_exp"), 2)
                    dve.wait_ge(S("ua_trig"), 1)
                    tt(table_(ua), table_(ua), over_d(rowsT[:, 2, :]), ALU.mult)
                    tt(table_(ub), table_(ub), over_d(rowsT[:, 3, :]), ALU.mult)
                    tt(table_(ua), table_(ua), table_(ub), ALU.add)
                    V.tensor_tensor(table_(ua), table_(ua), table_(mag), ALU.mult).then_inc(S("ua_ready"), 1)

                def s4_taps():
                    for h in range(2):
                        dve.wait_ge(S("taps_ps"), h + 1)
                        for r in range(4):
                            src = ps[0:KTAP, 4 * h:4 * h + 4, :].rearrange("p k (d m r) -> p m k d r", m=NT, r=4)
                            for kk in range(4):
                                d0 = 64 * h + 16 * kk
                                V.tensor_copy(taps[KTAP * r:KTAP * (r + 1), :, d0:d0 + 16], src[:, :, kk, :, r])\
                                    .then_inc(S("taps_ready"), 1)
                    dve.wait_ge(S("taps_ready"), 32)
                    V.tensor_tensor(taps[0:1, 0, :], taps[0:1, 0, :], dskip[0:1, :], ALU.add).then_inc(S("taps_ready"), 1)

                dchain(V.memset(ones[:, :], 1.0))
                dchain(V.memset(Q0[:, T:T + P], 0.0))
                dve.wait_ge(S("x_in"), 16)
                ln_stats(x_sb, S("ln_var"))
                ln_apply(xn, x_sb, S("ln_sd"), 1, S("xn_ready"))
                s4_rates()
                dve.wait_ge(S("mask_in"), 32)
                dchain(V.tensor_copy(openf[:, :], mask8[:, :]))
                dchain(V.reduce_sum(opened[:, :], openf[:, :], AX.X))
                dve.wait_ge(S("bv_in"), 16)
                dve.wait_ge(S("v1_ones"), 1)
                for i in range(NGROUP):
                    w, r = width(i), i % 2
                    if i == NGROUP - 4:
                        dve.wait_ge(S("ctxT_ps"), NGROUP - NR)
                        V.memset(ctx_in[:, (NGROUP - 1) % NR, :, :], 0.0).then_inc(S("ctx_pad"), 1)
                    dve.wait_ge(S("k1_evac"), i + 1)
                    dchain(V.tensor_reduce(kabs[:, i:i + 1], k1f[:, r, 0:w], AX.X, ALU.max, apply_absolute_value=True))
                    V.sem_inc(S("k1_seen"), 1)
                    dve.wait_ge(S("v_ps"), i + 1)
                    if i >= 2:
                        dve.wait_ge(S(f"v1_out{r}"), 16 * (i // 2))
                    n = w // P
                    V.tensor_tensor(v1g[:, r, 0:n, :, 0:DH1],
                                    ps[:, 0, 0:w].rearrange("p (c h v) -> p c h v", h=H1, v=DH1),
                                    bv1[:, :].rearrange("p (h v) -> p h v", v=DH1).unsqueeze(1)
                                    .to_broadcast([P, n, H1, DH1]), ALU.add).then_inc(S("v1_evac"), 1)
                    if i == S4_AT["coefficients"]:
                        s4_coefficients()
                    if i == S4_AT["phases"]:
                        s4_phases()
                    if i == S4_AT["b_table"]:
                        s4_b_table()
                    if i == S4_AT["a_table"]:
                        s4_a_table()
                s4_taps()

            @block.tensor
            def _(pe):
                pe.wait_ge(S("w_in"), 16 * 6)
                pe.wait_ge(S("xn_ready"), NT)
                transpose_tiles(xn, 0, S("xnT_ps"))
                pe.wait_ge(S("xnT_sb"), 1)
                for b in range(NB):
                    last = M.matmul(ps[:, 2 + b, :], wq0[:, :], xnT[:, b * TB:(b + 1) * TB], start=True, stop=True)
                last.then_inc(S("q_ps"), 1)

                def turn(i):
                    pe.wait_ge(S(f"ctx_in{i % NR}"), 16 * (i // NR + 1) + (16 if i == NGROUP - 1 else 0))
                    if i >= 1:
                        pe.wait_ge(S("ctxT_sb"), i)
                    for c in range(width(i) // P):
                        last = M.transpose(ps[0:DC, 4, c * P:(c + 1) * P], ctx_in[:, i % NR, c, :], ident[:, :])
                    last.then_inc(S("ctxT_ps"), 1)
                turn(0)
                for i in range(NGROUP):
                    w, r = width(i), i % 2
                    pe.wait_ge(S("ctxT_sb"), i + 1)
                    if i + 1 < NGROUP:
                        turn(i + 1)
                    if i >= 1:
                        pe.wait_ge(S("k0_evac"), i)
                        pe.wait_ge(S("k1_evac"), i)
                    M.matmul(ps[:, 5, 0:w], wk0[:, :], ctxT[:, r, 0:w], start=True, stop=True)
                    M.matmul(ps[:, 6, 0:w], wk1[:, :], ctxT[:, r, 0:w], start=True, stop=True).then_inc(S("k_ps"), 1)
                    if i >= 1:
                        pe.wait_ge(S("v0_evac"), i)
                        pe.wait_ge(S("v1_evac"), i)
                    for c in range(w // P):
                        for bank, cols in ((7, slice(0, P)), (0, slice(P, 2 * P))):
                            last = M.matmul(ps[:, bank, c * P:(c + 1) * P], ctxT[:, r, c * P:(c + 1) * P],
                                            wv[:, cols], start=True, stop=True)
                    last.then_inc(S("v_ps"), 1)
                    if i == S4_AT["rows"]:
                        pe.wait_ge(S("q0"), 1)
                        pe.wait_ge(S("rows_ready"), 1)
                        for k in range(4):
                            last = M.transpose(ps[:, 3, k * D:(k + 1) * D], rows[:, k, :], ident[:, :])
                        last.then_inc(S("rowsT_ps"), 1)
                pe.wait_ge(S("v0_evac"), NGROUP)
                pe.wait_ge(S("v1_evac"), NGROUP)
                pe.wait_ge(S("k0_evac"), NGROUP)
                pe.wait_ge(S("k1_evac"), NGROUP)
                pe.wait_ge(S("zb_ready"), 1)
                pe.wait_ge(S("ua_ready"), 1)
                for d in range(D):
                    last = M.matmul(ps[0:KTAP, d // 16, (d % 16) * KTAP:(d % 16 + 1) * KTAP],
                                    zb[:, :, d], ua[:, :, d], start=True, stop=True)
                    if d % 64 == 63:
                        last.then_inc(S("taps_ps"), 1)

    NI = H0 * NT
    NBK = -(-GP // 512)
    GBANK = 2
    GCOL = GBANK * 512
    NGRP = -(-G // GCOL)
    NTURN = -(-NG // 4)
    CH_OF = [2, 3, 3, 5]
    NCH = len(CH_OF)
    CUTS = [min(4 * P * sum(CH_OF[:c]), G) for c in range(NCH + 1)]
    TURN_AT = {(1, 6): (0, 1, 2), (2, 0): (3,), (2, 1): (4,), (2, 2): (5,), (2, 3): (6,), (2, 4): (7,), (2, 5): (8,),
               (2, 6): (9,), (3, 0): (10, 11), (3, 1): (12,)}
    LAST_AT, SUMS_AT = (3, 1), (3, 4)
    FIRST_OF = {sum(CH_OF[:c]): c for c in range(NCH)}
    MASK = {0: 2, 1: 3, 2: 5}
    PENALTY = {3: 5}
    EXP_AFTER = {0: 0, 1: 1, 2: 3, 3: 2}
    SLOTS = 3
    LOOPED = 3
    LOOP_TURNS = (NT - 2) // LOOPED
    NADD = (H0 - 1) * NCH
    STEEP = 2.0 ** 100
    with ExitStack() as b2:
        srow = sb(b2, "srow", [P, SLOTS, G])
        ex = sb(b2, "ex", [P, G])
        mean = sb(b2, "mean", [P, G])
        meanT = sb(b2, "meanT", [P, 2, 4 * P])
        qst = sb(b2, "qst", [P, H0, P])
        cand = sb(b2, "cand", [P, NPIECE, 8])
        top40 = sb(b2, "top40", [P, SLOTS, 40])
        nmax = sb(b2, "nmax", [P, SLOTS])
        steep = sb(b2, "steep", [P, SLOTS])
        zsum = sb(b2, "zsum", [P, SLOTS])
        lnz = sb(b2, "lnz", [P, SLOTS])
        shift = sb(b2, "shift", [P, SLOTS])
        junk = sb(b2, "junk", [P, SLOTS, TOPK])
        edge = sb(b2, "edge", [P, NI, 2])
        hidden = sb(b2, "hidden", [P, NI])
        odd = sb(b2, "odd", [P, NI])
        odd2 = sb(b2, "odd2", [P, NI])
        odd1 = sb(b2, "odd1", [P, 1])
        miss = sb(b2, "miss", [1, 1])
        BOTH_TABLE = "natural_log_exp_and_others"
        SELECT = 12

        def group(g):
            return g * GCOL, min((g + 1) * GCOL, G)

        def slot(m, h):
            return (H0 * m + h) % SLOTS

        assert SLOTS == LOOPED and (NT - 2) % LOOPED == 0

        def done(n, c, kinds):
            return n * len(kinds) + (list(kinds).index(c) + 1)

        with nc.Block() as block:
            @block.tensor
            def _(pe):
                def scores(t, h, first, behind=None):
                    pe.wait_ge(S("q_placed"), t * H0 + (h + 1))
                    for g in range(NGRP):
                        k = h * NGRP + g
                        if not (first and k < 2):
                            pe.wait_ge(S("evac"), t * (H0 * NGRP) + (k - 1))
                        g0, g1 = group(g)
                        for b in range(-(-(g1 - g0) // 512)):
                            c0, c1 = g0 + b * 512, min(g0 + b * 512 + 512, g1)
                            last = M.matmul(ps[:, GBANK * (k % 2) + b, 0:c1 - c0], qst[:, h, :], K0[:, c0:c1],
                                            start=True, stop=True)
                        last.then_inc(S("scored"), 1)
                        if behind is not None:
                            for j in TURN_AT.get((h, g), ()):
                                mean_group(behind, j, isinstance(behind, int))

                def turn_group(u, j, first):
                    if not (first and j < 2):
                        pe.wait_ge(S("meanT_sb"), u * NTURN + (j - 1))
                    for c in range(4 * j, min(4 * j + 4, NG)):
                        n = min(P, G - c * P)
                        last = M.transpose(ps[0:n, 4 + j % 2, (c % 4) * P:(c % 4 + 1) * P], mean[:, c * P:c * P + n],
                                           ident[:, :])
                    last.then_inc(S("turned"), 1)

                def value_group(u, j, first):
                    pe.wait_ge(S("meanT_sb"), u * NTURN + (j + 1))
                    if j == 0 and not first:
                        pe.wait_ge(S("c_read"), u)
                    for c in range(4 * j, min(4 * j + 4, NG)):
                        n = min(P, G - c * P)
                        last = M.matmul(ps[:, 6, 0:D], meanT[0:n, j % 2, (c % 4) * P:(c % 4 + 1) * P], V0[0:n, c, :],
                                        start=c == 0, stop=c == NG - 1)
                    last.then_inc(S("summed"), 1)

                def mean_group(u, j, first):
                    if j in FIRST_OF:
                        pe.wait_ge(S("added"), u * NADD + (NADD - NCH + FIRST_OF[j] + 1))
                    turn_group(u, j, first)
                    if j > 0:
                        value_group(u, j - 1, first)
                    if j == NTURN - 1:
                        value_group(u, j, first)

                for h in range(H0):
                    scores(0, h, True)

                for h in range(H0):
                    scores(1, h, False, behind=0)
                with pe.Fori(2, NT) as t:
                    for h in range(H0):
                        scores(t, h, False, behind=t - 1)
                for j in range(NTURN):
                    mean_group(NT - 1, j, False)
                pe.wait_ge(S("odd_ready"), 1)
                M.matmul(ps[0:1, 7, 0:1], odd1[:, :], ones[:, :], start=True, stop=True)
                M.matmul(ps[0:1, 7, 1:2], opened[:, :], ones[:, :], start=True, stop=True).then_inc(S("odd_ps"), 1)

            @block.scalar
            def _(act):
                def evac(t, m, h, g, first):
                    g0, g1 = group(g)
                    if not (first and h < SLOTS):
                        n = t * H0 + (h - SLOTS)
                        below = [c for c in range(NCH) if CUTS[c] < g1]
                        act.wait_ge(S("kept"), done(n, [c for c in below if c in MASK][-1], MASK))
                        if below[-1] in PENALTY:
                            act.wait_ge(S("lowered"), done(n, below[-1], PENALTY))
                    act.wait_ge(S("scored"), t * (H0 * NGRP) + (h * NGRP + g + 1))
                    b = GBANK * ((h * NGRP + g) % 2)
                    C.copy(srow[:, slot(m, h), g0:g1], ps[:, b:b + GBANK, :].rearrange("p a b -> p (a b)")[:, 0:g1 - g0])\
                        .then_inc(S("evac"), 1)

                def ex_free(t, h, c, first):
                    if h == 1:
                        if c in MASK:
                            act.wait_ge(S("kept"), done(t * H0, c, MASK))
                        else:
                            act.wait_ge(S("exped_low"), done(t * H0, c, PENALTY))
                    elif h:
                        act.wait_ge(S("added"), t * NADD + ((h - 2) * NCH + c + 1))
                    elif not first:
                        act.wait_ge(S("added"), t * NADD + (c + 1 - NCH))

                def exp_shift(t, m, h):
                    k = slot(m, h)
                    s = slice(k, k + 1)
                    act.wait_ge(S("edge_ready"), t * H0 + h + 1)
                    achain(C.activation(junk[:, k, :], top40[:, k, 0:TOPK], ACT.Exp, bias=nmax[:, s], accum_out=zsum[:, s]))
                    achain(C.activation(lnz[:, s], zsum[:, s], ACT.Ln, scale=float(H0)))
                    achain(C.activation(shift[:, s], lnz[:, s], ACT.Identity, scale=-1.0, bias=nmax[:, s]))

                def exp_or_penalty(t, m, h, c, first):
                    k = slot(m, h)
                    s = slice(k, k + 1)
                    ex_free(t, h, c, first)
                    src = srow[:, k, CUTS[c]:CUTS[c + 1]]
                    if c in MASK:
                        C.activation(ex[:, CUTS[c]:CUTS[c + 1]], src, ACT.Exp, bias=shift[:, s])\
                            .then_inc(S("exped"), 1)
                    else:
                        C.activation(ex[:, CUTS[c]:CUTS[c + 1]], src, ACT.Relu, scale=-STEEP, bias=steep[:, s])\
                            .then_inc(S("penalty"), 1)

                def exp_lowered(t, m, h, c, first):
                    k = slot(m, h)
                    act.wait_ge(S("lowered"), done(t * H0 + h, c, PENALTY))
                    if h == 0 and not first:
                        act.wait_ge(S("turned"), (t - 1) * NTURN + sum(CH_OF[:c + 1]))
                    C.activation((ex if h else mean)[:, CUTS[c]:CUTS[c + 1]], ex[:, CUTS[c]:CUTS[c + 1]],
                                 ACT.Exp, bias=shift[:, k:k + 1]).then_inc(S("exped_low"), 1)

                def queries(t, h, first):
                    if not first:
                        act.wait_ge(S("scored"), (t - 1) * (H0 * NGRP) + (h + 1) * NGRP)
                    rows_ = slice(DH0 * h, DH0 * (h + 1))
                    C.copy(qst[rows_, h, :], Q0[rows_, bass.ds(t * P, P)]).then_inc(S("q_placed"), 1)

                def mean_copy(u, j, first):
                    act.wait_ge(S("turned"), u * NTURN + (j + 1))
                    if not (first and j < 2):
                        act.wait_ge(S("summed"), u * NTURN + (j - 1))
                    n = min(4, NG - 4 * j) * P
                    if j == NTURN - 1:
                        full, part = n - P, G - (NG - 1) * P
                        C.copy(meanT[:, j % 2, 0:full], ps[:, 4 + j % 2, 0:full]).then_inc(S("meanT_full"), 1)
                        act.wait_ge(S("meanT_full"), u + 1)
                        C.copy(meanT[0:part, j % 2, full:n], ps[0:part, 4 + j % 2, full:n]).then_inc(S("meanT_sb"), 1)
                    else:
                        C.copy(meanT[:, j % 2, 0:n], ps[:, 4 + j % 2, 0:n]).then_inc(S("meanT_sb"), 1)

                def sums_copy(u):
                    act.wait_ge(S("summed"), u * NTURN + NTURN)
                    C.copy(c_t[:, bass.ds(u, 1), :].rearrange("p a d -> p (a d)"), ps[:, 6, 0:D]).then_inc(S("c_read"), 1)

                C.preload_act_table_set(BOTH_TABLE)
                act.wait_ge(S("qst_zero"), 1)
                for h in range(H0):
                    queries(0, h, True)
                STEPS = 3 * H0

                def turn(t, m, behind, first=False):
                    for h in range(H0):
                        older = (t, m, h - 2) if h >= 2 else (t - 1, (m - 1) % SLOTS, h + 2)
                        if first and h < 2:
                            older = None
                        for g in range(NGRP):
                            evac(t, m, h, g, first)
                            if behind is not None:
                                for j in TURN_AT.get((h, g), ()):
                                    mean_copy(behind, j, isinstance(behind, int))
                                if (h, g) == SUMS_AT:
                                    sums_copy(behind)
                            if (h, g) == LAST_AT:
                                for c in PENALTY:
                                    exp_lowered(t, m, 0, c, first)
                            if older and g == 0:
                                exp_shift(*older)
                            for c in range(NCH):
                                if older and EXP_AFTER[c] == g:
                                    exp_or_penalty(*older, c, first)
                            for c in PENALTY:
                                if older and older[2] and PENALTY[c] == g:
                                    exp_lowered(*older, c, False)
                        queries(t + 1, h, False)

                turn(0, 0, None, first=True)
                turn(1, 1, 0)
                with act.Fori(0, LOOP_TURNS) as i:
                    achain.loop(i, LOOPED * STEPS)
                    n0 = achain.n
                    for r in range(LOOPED):
                        turn(i * LOOPED + (2 + r), (2 + r) % SLOTS, i * LOOPED + (1 + r))
                    assert achain.n - n0 == LOOPED * STEPS
                achain.looped(LOOPED * STEPS, LOOP_TURNS)
                for h in range(2, H0):
                    exp_shift(NT - 1, (NT - 1) % SLOTS, h)
                    for c in range(NCH):
                        exp_or_penalty(NT - 1, (NT - 1) % SLOTS, h, c, False)
                    for c in PENALTY:
                        exp_lowered(NT - 1, (NT - 1) % SLOTS, h, c, False)
                for j in range(NTURN):
                    mean_copy(NT - 1, j, False)
                sums_copy(NT - 1)

            @block.vector
            def _(dve):
                def mask_chunk(t, m, h, c, first):
                    s = slot(m, h)
                    dve.wait_ge(S("exped"), done(t * H0 + h, c, MASK))
                    if h == 0 and not first:
                        dve.wait_ge(S("turned"), (t - 1) * NTURN + sum(CH_OF[:c + 1]))
                    V.scalar_tensor_tensor((ex if h else mean)[:, CUTS[c]:CUTS[c + 1]], srow[:, s, CUTS[c]:CUTS[c + 1]],
                                           top40[:, s, TOPK - 1:TOPK], ex[:, CUTS[c]:CUTS[c + 1]],
                                           ALU.is_ge, ALU.mult).then_inc(S("kept"), 1)

                def event(t, m, h, first):
                    n, s = t * H0 + h, slot(m, h)
                    for g in range(NGRP):
                        dve.wait_ge(S("evac"), t * (H0 * NGRP) + (h * NGRP + g + 1))
                        take_wait(dve)
                        g0, g1 = group(g)
                        for q in range((g1 - g0) // PIECE):
                            c0 = g0 + q * PIECE
                            c1 = G if G - c0 < 2 * PIECE else c0 + PIECE
                            last = V.max(cand[:, c0 // PIECE, :], srow[:, s, c0:c1])
                        last.then_inc(S("maxed"), 1)
                        for c in MASK:
                            if MASK[c] == g and not (first and h == 0):
                                mask_chunk(*((t, m, h - 1) if h else (t - 1, (m - 1) % SLOTS, H0 - 1)), c, first)
                    dve.wait_ge(S("maxed"), t * (H0 * NGRP) + (h + 1) * NGRP)
                    dchain(V.reduce_max(hidden[:, bass.ds(n, 1)], cand[:, :, 7], AX.X), before_max=True)
                    for r in range(5):
                        top = top40[:, s, 8 * r:8 * r + 8]
                        rest = cand[:, :, :].rearrange("p a b -> p (a b)")
                        dchain(V.max(top, rest), before_max=r < 4)
                        if r < 4:
                            dchain(V.match_replace(rest, top, rest, LOWEST), before_max=True)
                    dchain(V.tensor_copy(edge[:, bass.ds(n, 1), :], top40[:, s, TOPK - 1:TOPK + 1].unsqueeze(1)))
                    dchain(V.tensor_scalar(steep[:, s:s + 1], top40[:, s, TOPK - 1:TOPK], STEEP, None, ALU.mult))
                    V.tensor_scalar(nmax[:, s:s + 1], top40[:, s, 0:1], -1.0, None, ALU.mult).then_inc(S("edge_ready"), 1)

                for t in range(2):
                    for h in range(H0):
                        event(t, t, h, t == 0)
                with dve.Fori(0, LOOP_TURNS) as i:
                    dchain.loop(i, LOOPED * H0 * SELECT)
                    n0 = dchain.n
                    for r in range(LOOPED):
                        for h in range(H0):
                            event(i * LOOPED + (2 + r), (2 + r) % SLOTS, h, False)
                    assert dchain.n - n0 == LOOPED * H0 * SELECT
                dchain.looped(LOOPED * H0 * SELECT, LOOP_TURNS)
                for c in MASK:
                    mask_chunk(NT - 1, (NT - 1) % SLOTS, H0 - 1, c, False)
                dchain(V.tensor_tensor(odd[:, :], hidden[:, :], edge[:, :, 1], ALU.is_gt))
                dchain(V.tensor_tensor(odd2[:, :], edge[:, :, 0], edge[:, :, 1], ALU.subtract))
                dchain(V.tensor_scalar(odd2[:, :], odd2[:, :], 2.0 ** -80, None, ALU.is_lt))
                dchain(V.tensor_tensor(odd[:, :], odd[:, :], odd2[:, :], ALU.add))
                dchain(V.tensor_tensor(odd2[:, :], edge[:, :, 0], edge[:, :, 0], ALU.mult))
                dchain(V.tensor_scalar(odd2[:, :], odd2[:, :], 2.0 ** 50, None, ALU.is_gt))
                dchain(V.tensor_tensor(odd[:, :], odd[:, :], odd2[:, :], ALU.add))
                V.reduce_max(odd1[:, :], odd[:, :], AX.X).then_inc(S("odd_ready"), 1)
                dve.wait_ge(S("odd_ps"), 1)
                dchain(V.tensor_scalar(miss[:, :], ps[0:1, 7, 1:2], -1.0, float(G), ALU.mult, ALU.add))
                dchain(V.tensor_tensor(miss[:, :], miss[:, :], ps[0:1, 7, 0:1], ALU.add))
                dchain(V.tensor_copy(general[0:1, 0:1], miss[:, :]))

            @block.gpsimd
            def _(pool):
                PL.memset(qst[:, :, :], 0.0).then_inc(S("qst_zero"), 1)

                def event(t, m, h):
                    n = t * H0 + h
                    for c in PENALTY:
                        pool.wait_ge(S("penalty"), done(n, c, PENALTY))
                        PL.tensor_tensor(ex[:, CUTS[c]:CUTS[c + 1]], srow[:, slot(m, h), CUTS[c]:CUTS[c + 1]],
                                         ex[:, CUTS[c]:CUTS[c + 1]], ALU.subtract).then_inc(S("lowered"), 1)
                    if h == 0:
                        return
                    for c in range(NCH):
                        if c in MASK:
                            pool.wait_ge(S("kept"), done(n, c, MASK))
                        else:
                            pool.wait_ge(S("exped_low"), done(n, c, PENALTY))
                        if h > 1:
                            pool.wait_ge(S("added"), t * NADD + ((h - 2) * NCH + c + 1))
                        PL.tensor_tensor(mean[:, CUTS[c]:CUTS[c + 1]], mean[:, CUTS[c]:CUTS[c + 1]],
                                         ex[:, CUTS[c]:CUTS[c + 1]], ALU.add).then_inc(S("added"), 1)

                for t in range(2):
                    for h in range(H0):
                        event(t, t, h)
                with pool.Fori(0, LOOP_TURNS) as i:
                    for r in range(LOOPED):
                        for h in range(H0):
                            event(i * LOOPED + (2 + r), (2 + r) % SLOTS, h)

            @block.sync
            def _(sp):
                take_part(sp)

    next_stage()
    l0_general = nc.values_load(general[0:1, 0:1], min_val=0, max_val=G + P)
    with nc.If(l0_general > 0):
        with ExitStack() as b3:
            row = sb(b3, "row", [P, GP])
            t40 = sb(b3, "t40", [P, TOPK])
            nmax = sb(b3, "nmaxg", [P, 1])
            zsum, zinv = sb(b3, "zsumg", [P, 1]), sb(b3, "zinvg", [P, 1])
            junk = sb(b3, "junkg", [P, TOPK])
            junk2 = sb(b3, "junk2", [P, D])
            exg, pg, pgT = (sb(b3, n, [P, 2, 512]) for n in ("exg", "pg", "pgT"))
            QZ = sb(b3, "QZ", [P, H0, T])
            qg = sb(b3, "qg", [P, P])
            mrow = sb(b3, "mrow", [1, GP], BF16)
            onesb = sb(b3, "onesb", [1, P], BF16)

            def bank_width(j):
                return min(512, GP - j * 512)

            with nc.Block() as block:
                @block.gpsimd
                def _(pool):
                    PL.memset(c_t[:, :, :], 0.0).then_inc(S("c_zero"), 1)
                    PL.memset(onesb[:, :], 1.0).then_inc(S("g_ones"), 1)
                    PL.memset(QZ[:, :, :], 0.0).then_inc(S("qz"), 1)
                    pool.wait_ge(S("qz"), 1)
                    for h in range(H0):
                        rows_ = slice(DH0 * h, DH0 * (h + 1))
                        PL.tensor_copy(QZ[rows_, h, :], Q0[rows_, 0:T]).then_inc(S("qz"), 1)
                        pool.wait_ge(S("qz"), h + 2)
                    with pool.Fori(0, NI) as i:
                        pool.wait_ge(S("g_added"), i + 1)
                        PL.tensor_copy(qg[:, :], QZ[:, :, :].rearrange("p h t -> p (h t)")[:, bass.ds(i * P, P)])\
                            .then_inc(S("g_q"), 1)

                @block.sync
                def _(sp):
                    sp.dma_start(mrow[0:1, :], mask_line[0:1, :]).then_inc(S("g_mask"), 16)

                @block.tensor
                def _(pe):
                    def scores(h, i, e):
                        j, w = e % NBK, bank_width(e % NBK)
                        pe.wait_ge(S("g_read"), i * 2 * NBK + e + 1)
                        M.matmul(ps[:, e % 2, 0:w], qg[:, :], K0[:, j * 512:j * 512 + w], start=True, stop=False)
                        M.matmul(ps[:, e % 2, 0:w], onesb[:, :], mrow[0:1, j * 512:j * 512 + w], start=False, stop=True)\
                            .then_inc(S("g_scored"), 1)

                    pe.wait_ge(S("g_ones"), 1)
                    pe.wait_ge(S("g_mask"), 16)
                    with pe.Fori(0, H0) as h:
                        with pe.Fori(0, NT) as t:
                            i = h * NT + t
                            pe.wait_ge(S("g_q"), i + 1)
                            for e in range(NBK):
                                scores(h, i, e)
                            for j in range(NBK):
                                scores(h, i, NBK + j)
                                pe.wait_ge(S("g_kept"), i * NBK + j + 2)
                                for c in range(bank_width(j) // P):
                                    last = M.transpose(ps[:, 2 + j % 2, c * P:(c + 1) * P], pg[:, j % 2, c * P:(c + 1) * P],
                                                       ident[:, :])
                                last.then_inc(S("g_turned"), 1)
                                pe.wait_ge(S("g_placed"), i * NBK + j + 1)
                                if j == 0:
                                    pe.wait_ge(S("g_added"), i + 1)
                                n = bank_width(j) // P
                                for c in range(n):
                                    last = M.matmul(ps[:, 4, 0:D], pgT[:, j % 2, c * P:(c + 1) * P], V0[:, 4 * j + c, :],
                                                    start=j == 0 and c == 0, stop=j == NBK - 1 and c == n - 1)
                                last.then_inc(S("g_summed"), 1)

                @block.scalar
                def _(act):
                    act.sem_inc(S("g_read"), 2)
                    with act.Fori(0, NI) as i:
                        for j in range(NBK):
                            w = bank_width(j)
                            act.wait_ge(S("g_scored"), i * 2 * NBK + j + 1)
                            if j == 0:
                                act.wait_ge(S("g_kept"), i * NBK + 1)
                            C.copy(row[:, j * 512:j * 512 + w], ps[:, j % 2, 0:w]).then_inc(S("g_read"), 1)
                        act.wait_ge(S("g_max"), i + 1)
                        C.activation(junk[:, :], t40[:, :], ACT.Exp, bias=nmax[:, 0:1], accum_out=zsum[:, :]).then_inc(S("g_z"), 1)
                        for j in range(NBK):
                            w, e = bank_width(j), NBK + j
                            act.wait_ge(S("g_scored"), i * 2 * NBK + e + 1)
                            if j >= 2:
                                act.wait_ge(S("g_kept"), i * NBK + j)
                            C.activation(exg[:, j % 2, 0:w], ps[:, e % 2, 0:w], ACT.Exp, bias=nmax[:, 0:1])\
                                .then_inc(S("g_read"), 1)

                @block.vector
                def _(dve):
                    steps_ = 2 * (TOPK // 8) + 4
                    dve.wait_ge(S("c_zero"), 1)
                    dve.sem_inc(S("g_added"), 1)
                    dve.sem_inc(S("g_kept"), 1)
                    with dve.Fori(0, H0) as h:
                        with dve.Fori(0, NT) as t:
                            i = h * NT + t
                            dchain.loop(i, steps_)
                            n0 = dchain.n
                            dve.wait_ge(S("g_read"), i * 2 * NBK + NBK + 2)
                            take_wait(dve)
                            for r in range(TOPK // 8):
                                top = t40[:, 8 * r:8 * r + 8]
                                dchain(V.max(top, row[:, :]), before_max=True)
                                dchain(V.match_replace(row[:, :], top, row[:, :], LOWEST), before_max=True)
                            V.tensor_scalar(nmax[:, :], t40[:, 0:1], -1.0, None, ALU.mult).then_inc(S("g_max"), 1)
                            for j in range(NBK):
                                w = bank_width(j)
                                dve.wait_ge(S("g_read"), i * 2 * NBK + NBK + j + 3)
                                V.scalar_tensor_tensor(pg[:, j % 2, 0:w], row[:, j * 512:j * 512 + w], LOWEST,
                                                       exg[:, j % 2, 0:w], ALU.is_equal, ALU.mult).then_inc(S("g_kept"), 1)
                                dve.wait_ge(S("g_turned"), i * NBK + j + 1)
                                if j >= 2:
                                    dve.wait_ge(S("g_summed"), i * NBK + j - 1)
                                V.tensor_copy(pgT[:, j % 2, 0:w], ps[:, 2 + j % 2, 0:w]).then_inc(S("g_placed"), 1)
                            dve.wait_ge(S("g_z"), i + 1)
                            dchain(V.tensor_scalar(zinv[:, :], zsum[:, :], float(H0), None, ALU.mult))
                            dchain(V.reciprocal(zinv[:, :], zinv[:, :]))
                            dve.wait_ge(S("g_summed"), i * NBK + NBK)
                            dchain(V.tensor_scalar(junk2[:, :], ps[:, 4, 0:D], zinv[:, 0:1], None, ALU.mult))
                            tile = c_t[:, bass.ds(t, 1), :]
                            dchain(V.tensor_tensor(tile, tile, junk2[:, :].unsqueeze(1), ALU.add))
                            dve.sem_inc(S("g_added"), 1)
                            assert dchain.n - n0 == steps_
                    dchain.looped(steps_, NI)
    next_stage()
    l0.close()



    NF = HID // P
    w1 = sb(whole, "w1", [P, HID])
    w2 = sb(whole, "w2", [P, NF, D])
    b1c = sb(whole, "b1c", [P, NF])
    row6 = {n: sb(whole, "row6_" + n, [P, D]) for n in ("b2", "g_norm_out", "b_norm_out")}
    u1 = sb(whole, "u1", [P, RANK])
    v1w = sb(whole, "v1w", [RANK, HID])
    b1c7 = sb(whole, "b1c7", [P, NF])
    u2 = sb(whole, "u2", [P, NF, RANK])
    v2w = sb(whole, "v2w", [RANK, D])
    b2r = sb(whole, "b2r7", [P, D])
    wq1 = sb(whole, "wq1", [P, P])
    bq1 = sb(whole, "bq1", [P, 1])

    xt = sb(whole, "xt", [P, NT, D])
    wT = sb(whole, "wT", [P, T])
    with ExitStack() as b5:
        mask_t8 = sb(b5, "mask_t8", [P, NT], U8)
        mask_t = sb(b5, "mask_t", [P, NT])
        mg = sb(b5, "mg", [P, 1])
        wf = sb(b5, "wf", [P, HID])
        bf = sb(b5, "bf", [P, HID])
        rowsb = {n: sb(b5, "row_" + n, [P, D]) for n in ("g_norm_in", "b_norm_in", "g_ffn", "b_ffn")}
        dft = sb(b5, "dft", [P, 9, P])
        cT5 = sb(b5, "cT5", [P, T])
        film = sb(b5, "film", [P, NT, 4, D])
        xf = sb(b5, "xf", [P, NT, D])
        spec_x = sb(b5, "spec_x", [P, 2, NT, D])
        spec_k = sb(b5, "spec_k", [P, 2, NT, D])
        prod = sb(b5, "prod", [P, 2, 4, NT, D])
        FX, FK0, FK1, IFR, IFN, IFI = 0, 2, 4, 6, 7, 8
        with nc.Block() as block:
            @block.sync
            def _(sp):
                sp.dma_start(wf[:, 0:2 * D], A["L0_xattn_W_film_in"]).then_inc(S("b5_in"), 16)
                sp.dma_start(wf[:, 2 * D:], A["L0_xattn_W_film_out"]).then_inc(S("b5_in"), 16)
                sp.dma_start(bf[:, 0:2 * D], A["L0_xattn_b_film_in"].partition_broadcast(P)).then_inc(S("b5_in"), 16)
                sp.dma_start(bf[:, 2 * D:], A["L0_xattn_b_film_out"].partition_broadcast(P)).then_inc(S("b5_in"), 16)
                sp.dma_start(dft[:, :, :], A["dft"]).then_inc(S("b5_in"), 16)
                sp.dma_start(mg[:, :], A["L0_xattn_mod_gate"].partition_broadcast(P)).then_inc(S("b5_in"), 16)
                sp.dma_start(mask_t8[:, :], A["mask_BxS_bf1"].rearrange("o (n p) -> p (o n)", p=P),
                             allow_slow_non_contiguous=True).then_inc(S("b5_in"), 16)
                for n, tile in rowsb.items():
                    sp.dma_start(tile[:, :], A["L0_xattn_" + n].partition_broadcast(P)).then_inc(S("b5_in"), 16)
                sp.dma_start(w1[:, :], A["L0_xattn_W1"]).then_inc(S("ffn_in"), 16)
                sp.dma_start(w2[:, :, :], A["L0_xattn_W2"].rearrange("(f p) d -> p f d", p=P)).then_inc(S("ffn_in"), 16)
                sp.dma_start(b1c[:, :], A["L0_xattn_b1"].rearrange("(f p) -> p f", p=P),
                             allow_slow_non_contiguous=True).then_inc(S("ffn_in"), 16)
                for n, tile in row6.items():
                    sp.dma_start(tile[:, :], A["L0_xattn_" + n].partition_broadcast(P)).then_inc(S("ffn_in"), 16)
                sp.dma_start(gates[:, 0:2], A["g_xattn"].partition_broadcast(P)).then_inc(S("ffn_in"), 16)
                sp.dma_start(gates[:, 2:4], A["g_ffn"].partition_broadcast(P)).then_inc(S("ffn_in"), 16)
                for dst, name in ((u1, "L0_ffn_U1"), (v1w, "L0_ffn_V1"), (v2w, "L0_ffn_V2"), (wq1, "L1_xattn_wq")):
                    sp.dma_start(dst[:, :], A[name]).then_inc(S("ffn_in"), 16)
                sp.dma_start(u2[:, :, :], A["L0_ffn_U2"].rearrange("(f p) r -> p f r", p=P)).then_inc(S("ffn_in"), 16)
                sp.dma_start(b1c7[:, :], A["L0_ffn_b1"].rearrange("(f p) -> p f", p=P),
                             allow_slow_non_contiguous=True).then_inc(S("ffn_in"), 16)
                sp.dma_start(bq1[:, :], A["L1_xattn_bq"].rearrange("(p a) -> p a", a=1)).then_inc(S("ffn_in"), 16)
                sp.dma_start(b2r[:, :], A["L0_ffn_b2"].partition_broadcast(P)).then_inc(S("ffn_in"), 16)
                sp.wait_ge(S("ffn_in"), 16 * (8 + 8))

            @block.tensor
            def _(pe):
                pe.wait_ge(S("cm_ready"), NT)
                pe.wait_ge(S("b5_in"), 16 * 11)
                transpose_tiles(c_t, 0, S("cm_turned"))
                for part in range(2):
                    for half in range(2):
                        bank = ps[:, 2 + 2 * part + half, :]
                        if half == 0:
                            M.matmul(bank[:, D:4 * D], dft[:, FK0 + part, :], taps[:, 0:3, :], start=True, stop=False,
                                     skip_group_check=True)
                        else:
                            M.matmul(bank, dft[:, FK0 + part, :], taps[:, 3:7, :], start=True, stop=False,
                                     skip_group_check=True)
                        last = M.matmul(bank, dft[:, FK1 + part, :], taps[:, 4 * half:4 * half + 4, :],
                                        start=False, stop=True, skip_group_check=True)
                last.then_inc(S("spec_k_ps"), 1)
                pe.wait_ge(S("cT5_ready"), 1)
                pe.wait_ge(S("spec_k_ready"), 1)
                for t in range(NT):
                    if t >= 6:
                        pe.wait_ge(S("film_read"), t - 5)
                    M.matmul(ps[:, 2 + t % 6, :], cT5[:, t * P:(t + 1) * P], wf[:, :], start=True, stop=True)\
                        .then_inc(S("film_ps"), 1)
                pe.wait_ge(S("xf_ready"), 1)
                for part in range(2):
                    for half in range(2):
                        last = M.matmul(ps[:, 2 + 2 * part + half, :], dft[:, FX + part, :],
                                        xf[:, 4 * half:4 * half + 4, :], start=True, stop=True)
                last.then_inc(S("spec_x_ps"), 1)
                started = [False, False]
                for n, m in enumerate(reversed(range(NT))):
                    pe.wait_ge(S("prod_ready"), 4 * (n + 1))
                    for k, table in enumerate((IFR, IFN, IFI, IFI)):
                        for half in range(2):
                            lo_, hi_ = max(m, 4 * half), 4 * half + 4
                            if hi_ <= lo_:
                                continue
                            end = m == 0 and k == 3
                            last = M.matmul(ps[:, half, (lo_ - 4 * half) * D:(hi_ - 4 * half) * D],
                                            dft[:, table, :], prod[:, n % 2, k, lo_ - m:hi_ - m, :],
                                            start=not started[half], stop=end, skip_group_check=True)
                            started[half] = True
                    last.then_inc(S("prod_used"), 1)

            @block.scalar
            def _(act):
                act.wait_ge(S("cm_turned"), 1)
                C.copy(cT5[:, :], flat(ps[:, 0:2, :])).then_inc(S("cT5_ready"), 1)
                act.wait_ge(S("spec_k_ps"), 1)
                C.copy(spec_k[:, :, :, :].rearrange("p a b c -> p (a b c)"), flat(ps[:, 2:6, :])).then_inc(S("spec_k_ready"), 1)
                ln_sqrt(1, S("ln_in_var"), S("ln_in_sd"))
                act.wait_ge(S("spec_x_ps"), 1)
                C.copy(spec_x[:, :, :, :].rearrange("p a b c -> p (a b c)"), flat(ps[:, 2:6, :])).then_inc(S("spec_x_ready"), 1)
                ln_sqrt(1, S("ln_f_var"), S("ln_f_sd"))

            @block.vector
            def _(dve):
                dve.wait_ge(S("b5_in"), 16 * 11)
                dchain(V.tensor_copy(mask_t[:, :], mask_t8[:, :]))
                for t in range(NT):
                    V.tensor_scalar(c_t[:, t, :], c_t[:, t, :], mask_t[:, t:t + 1], None, ALU.mult).then_inc(S("cm_ready"), 1)
                ln_stats(xn, S("ln_in_var"))
                ln_apply(xf, xn, S("ln_in_sd"), 1, S("xl_ready"))
                dve.wait_ge(S("xl_ready"), NT)
                w = lambda t: t[:, :, :]
                dchain(V.tensor_tensor(w(xf), w(xf), every_tile(rowsb["g_norm_in"]), ALU.mult))
                dchain(V.tensor_tensor(w(xf), w(xf), every_tile(rowsb["b_norm_in"]), ALU.add))
                for t in range(NT):
                    dve.wait_ge(S("film_ps"), t + 1)
                    V.tensor_tensor(film[:, t, :, :].rearrange("p a b -> p (a b)"), ps[:, 2 + t % 6, :], bf[:, :], ALU.add)\
                        .then_inc(S("film_read"), 1)
                dve.wait_ge(S("film_read"), NT)
                dchain(V.tensor_scalar(film[:, :, :, :], film[:, :, :, :], mg[:, 0:1], None, ALU.mult))
                for k in (0, 2):
                    dchain(V.tensor_scalar(film[:, :, k, :], film[:, :, k, :], 1.0, None, ALU.add))
                dchain(V.tensor_tensor(w(xf), w(xf), film[:, :, 0, :], ALU.mult))
                V.tensor_tensor(w(xf), w(xf), film[:, :, 1, :], ALU.add).then_inc(S("xf_ready"), 1)
                dve.wait_ge(S("spec_x_ready"), 1)
                dve.wait_ge(S("spec_k_ready"), 1)
                for r, m in enumerate(reversed(range(NT))):
                    if r >= 2:
                        dve.wait_ge(S("prod_used"), r - 1)
                    n = NT - m
                    for k, (kp, xp) in enumerate(((0, 0), (1, 1), (0, 1), (1, 0))):
                        V.tensor_tensor(prod[:, r % 2, k, 0:n, :], spec_x[:, xp, 0:n, :],
                                        spec_k[:, kp, m, :].unsqueeze(1).to_broadcast([P, n, D]), ALU.mult)\
                            .then_inc(S("prod_ready"), 1)
                dve.wait_ge(S("prod_used"), NT)
                dchain(V.tensor_tensor(w(xt), ps[:, 0:2, :].rearrange("p a (b d) -> p (a b) d", d=D), film[:, :, 2, :], ALU.mult))
                dchain(V.tensor_tensor(w(xt), w(xt), film[:, :, 3, :], ALU.add))
                dchain(V.tensor_tensor(w(xt), w(xt), w(xn), ALU.add))
                ln_stats(xt, S("ln_f_var"))
                ln_apply(xf, xt, S("ln_f_sd"), 1, S("xl_ready"))
                dve.wait_ge(S("xl_ready"), 2 * NT)
                dchain(V.tensor_tensor(w(xf), w(xf), every_tile(rowsb["g_ffn"]), ALU.mult))
                dchain(V.tensor_tensor(w(xf), w(xf), every_tile(rowsb["b_ffn"]), ALU.add))
        with nc.Block() as block:
            @block.tensor
            def _(pe):
                transpose_tiles(xf, 0, S("xfT_ps"))

            @block.scalar
            def _(act):
                act.wait_ge(S("xfT_ps"), 1)
                C.copy(wT[:, :], flat(ps[:, 0:2, :])).then_inc(S("wT_ready"), 1)


    NQ = H1 // 4
    ROW1 = 6 * DH1
    KIN = 12
    oq, k1s = ExitStack(), ExitStack()
    o1 = sb(oq, "o1", [P, NQ, T])
    K1 = sb(k1s, "K1", [P, 2, 2, GP], BF16)
    V1 = sb(k1s, "V1", [P, 2, NG, 4 * VW])
    vs1 = sb(k1s, "vs1", [P, UNROLL, 4, 32])

    def load_quad(sp, quad, keys_in, values_in):
        b = quad % 2
        for par in range(2):
            for r, lv in enumerate((0, 1, 2, 0, 1, 0)):
                r0 = 64 * par + DH1 * r
                src = k1_parts[lv].rearrange("(q j a d) g -> q d j a g", j=2, a=2, d=DH1)
                sp.dma_start(K1[r0:r0 + DH1, b, :, :], src[quad, :, :, par, :]).then_inc(keys_in, 16)
        sp.dma_start(V1[:, b, :, :], v1_rows[:, :, quad * 4 * VW:(quad + 1) * 4 * VW]).then_inc(values_in, 16)

    with ExitStack() as b6:
        hid = sb(b6, "hid", [P, NB, NF, TB])
        yo = sb(b6, "yo", [P, NT, D])
        with nc.Block() as block:
            @block.sync
            def _(sp):
                for quad in range(2):
                    sp.wait_ge(S("k1_zero"), quad + 1)
                    for par in range(2):
                        r0 = 64 * par + ROW1
                        for pr in range(2):
                            sp.dma_start(K1[r0:r0 + LEVELS, quad, pr, :], mask_line[2, :].partition_broadcast(LEVELS))\
                                .then_inc(S("k1_ahead"), 16)
                            sp.dma_start(K1[r0 + LEVELS:r0 + LEVELS + 1, quad, pr, :], mask_line[1:2, :])\
                                .then_inc(S("k1_ahead"), 16)
                    load_quad(sp, quad, S("k1_ahead"), S("v1_ahead"))
                sp.wait_ge(S("k1_ahead"), 16 * 2 * (8 + KIN))
                sp.wait_ge(S("v1_ahead"), 16 * 2)

            @block.gpsimd
            def _(pool):
                for r in range(2):
                    PL.memset(K1[:, r, :, :], 0.0).then_inc(S("k1_zero"), 1)
                    pool.wait_ge(S("k1_zero"), r + 1)
                PL.memset(vs1[:, :, :, :], 0.0).then_inc(S("vs1_zero"), 1)
                pool.wait_ge(S("vs1_zero"), 1)

            @block.tensor
            def _(pe):
                for tb in range(NB):
                    for f in range(NF):
                        if tb:
                            pe.wait_ge(S("hid6"), (tb - 1) * NF + f + 1)
                        M.matmul(ps[:, f, :], w1[:, f * P:(f + 1) * P], wT[:, tb * TB:(tb + 1) * TB],
                                 start=True, stop=True).then_inc(S("hid6_ps"), 1)
                for t in range(NT):
                    pe.wait_ge(S("hid6"), (t // 4 + 1) * NF)
                    for f in range(NF):
                        last = M.matmul(ps[:, 4 + t // 4, (t % 4) * P:(t % 4 + 1) * P],
                                        hid[:, t // 4, f, (t % 4) * P:(t % 4 + 1) * P], w2[:, f, :],
                                        start=f == 0, stop=f == NF - 1)
                last.then_inc(S("out6_ps"), 1)
                pe.wait_ge(S("xn6"), NT)
                transpose_tiles(xn, 0, S("xn6T_ps"))

            @block.scalar
            def _(act):
                C.activation(gt[:, :], gates[:, :], ACT.Tanh).then_inc(S("gt_ready"), 1)
                for u in range(NB * NF):
                    act.wait_ge(S("hid6_ps"), u + 1)
                    C.activation(hid[:, u // NF, u % NF, :], ps[:, u % NF, :], ACT.Gelu,
                                 bias=b1c[:, u % NF:u % NF + 1]).then_inc(S("hid6"), 1)
                ln_sqrt(1, S("ln_o_var"), S("ln_o_sd"))
                ln_sqrt(1, S("ln_x1_var"), S("ln_x1_sd"))
                act.wait_ge(S("xn6T_ps"), 1)
                C.copy(wT[:, :], flat(ps[:, 0:2, :])).then_inc(S("wT6"), 1)

            @block.vector
            def _(dve):
                w = lambda t: t[:, :, :]
                dchain(V.tensor_tensor(w(xt), w(xt), every_tile(row6["b2"]), ALU.add))
                dve.wait_ge(S("out6_ps"), 1)
                dchain(V.tensor_tensor(w(xt), ps[:, 4:6, :].rearrange("p a (b d) -> p (a b) d", d=D), w(xt), ALU.add))
                ln_stats(xt, S("ln_o_var"))
                ln_apply(yo, xt, S("ln_o_sd"), 1, S("yo_ready"))
                dve.wait_ge(S("yo_ready"), NT)
                dchain(V.tensor_tensor(w(yo), w(yo), every_tile(row6["g_norm_out"]), ALU.mult))
                dchain(V.tensor_tensor(w(yo), w(yo), every_tile(row6["b_norm_out"]), ALU.add))
                dve.wait_ge(S("gt_ready"), 1)
                dchain(V.scalar_tensor_tensor(flat(x_sb), flat(yo), gt[:, 0:1], flat(x_sb), ALU.mult, ALU.add))
                ln_stats(x_sb, S("ln_x1_var"))
                ln_apply(xn, x_sb, S("ln_x1_sd"), 1, S("xn6"))

    q1s = ExitStack()
    Q1 = sb(q1s, "Q1", [P, H1, T], BF16)
    Q1v = Q1[:, :, :].rearrange("p (j a) t -> p j a t", a=2)
    with ExitStack() as b7:
        lowT = sb(b7, "lowT", [RANK, T])
        lowT2 = sb(b7, "lowT2", [RANK, T])
        hid = sb(b7, "hid7", [P, NB, NF, TB])
        yo = sb(b7, "yo7", [P, NT, D])
        bq1s = sb(b7, "bq1s", [P, 1])
        qs = sb(b7, "qs7", [P, T])
        ql = sb(b7, "ql7", [P, LEVELS, T], BF16)
        qabs, bound = sb(b7, "qabs", [P, 1]), sb(b7, "bound", [P, 1])
        boundh, bound1 = sb(b7, "boundh", [1, H1]), sb(b7, "bound1", [1, 1])
        SC1 = float(DH1) ** -0.5
        with nc.Block() as block:
            @block.sync
            def _(sp):
                sp.wait_ge(S("q1_split"), 1)
                sp.dma_start(q1_parts.rearrange("l p t -> p l t"), ql[:, :, :]).then_inc(S("q1_out"), 16)
                sp.wait_ge(S("q1_out"), 16)
                sp.wait_ge(S("q1_zero"), 1)
                for par in range(2):
                    r0 = 64 * par
                    for r, lv in enumerate((0, 0, 0, 1, 1, 2)):
                        sp.dma_start(Q1v[r0 + DH1 * r:r0 + DH1 * (r + 1), :, par, :],
                                     q1_parts[lv].rearrange("(j a d) t -> d j a t", a=2, d=DH1)[:, :, par, :])\
                          .then_inc(S("q1_gathered"), 16)
                    sp.dma_start(Q1v[r0 + ROW1 + LEVELS:r0 + ROW1 + LEVELS + 1, :, par, :],
                                 mask_line[2:3, 0:T].unsqueeze(1).to_broadcast([1, H1 // 2, T]))\
                        .then_inc(S("q1_gathered"), 16)
                sp.wait_ge(S("q1_gathered"), 16 * 14)

            @block.gpsimd
            def _(pool):
                PL.memset(Q1[:, :, :], 0.0).then_inc(S("q1_zero"), 1)

            @block.tensor
            def _(pe):
                for tb in range(NB):
                    last = M.matmul(ps[0:RANK, 6 + tb, :], u1[:, :], wT[:, tb * TB:(tb + 1) * TB], start=True, stop=True)
                last.then_inc(S("low_ps"), 1)
                pe.wait_ge(S("low_sb"), 1)
                for tb in range(NB):
                    for f in range(NF):
                        if tb:
                            pe.wait_ge(S("hid7"), (tb - 1) * NF + f + 1)
                        M.matmul(ps[:, f, :], v1w[:, f * P:(f + 1) * P], lowT[:, tb * TB:(tb + 1) * TB],
                                 start=True, stop=True).then_inc(S("hid7_ps"), 1)
                for tb in range(NB):
                    pe.wait_ge(S("hid7"), (tb + 1) * NF)
                    for f in range(NF):
                        last = M.matmul(ps[0:RANK, 6 + tb, :], u2[:, f, :], hid[:, tb, f, :], start=f == 0, stop=f == NF - 1)
                last.then_inc(S("low_ps"), 1)
                pe.wait_ge(S("low_sb"), 2)
                for t in range(NT):
                    last = M.matmul(ps[:, 4 + t // 4, (t % 4) * P:(t % 4 + 1) * P], lowT2[:, t * P:(t + 1) * P], v2w[:, :],
                                    start=True, stop=True)
                last.then_inc(S("out7_ps"), 1)
                pe.wait_ge(S("xn7"), NT)
                transpose_tiles(xn, 0, S("xn7T_ps"))
                pe.wait_ge(S("wT7"), 1)
                for tb in range(NB):
                    last = M.matmul(ps[:, 2 + tb, :], wq1[:, :], wT[:, tb * TB:(tb + 1) * TB], start=True, stop=True)
                last.then_inc(S("q1_ps"), 1)
                pe.wait_ge(S("bound_ready"), 1)
                M.matmul(ps[0:1, 6, 0:P], bound[:, :], ident[:, :], start=True, stop=True).then_inc(S("bound_ps"), 1)

            @block.scalar
            def _(act):
                act.wait_ge(S("low_ps"), 1)
                C.copy(lowT[:, :], flat(ps[0:RANK, 6:8, :])).then_inc(S("low_sb"), 1)
                for u in range(NB * NF):
                    act.wait_ge(S("hid7_ps"), u + 1)
                    C.activation(hid[:, u // NF, u % NF, :], ps[:, u % NF, :], ACT.Gelu_apprx_tanh,
                                 bias=b1c7[:, u % NF:u % NF + 1]).then_inc(S("hid7"), 1)
                act.wait_ge(S("low_ps"), 2)
                C.copy(lowT2[:, :], flat(ps[0:RANK, 6:8, :])).then_inc(S("low_sb"), 1)
                ln_sqrt(1, S("ln_x2_var"), S("ln_x2_sd"))
                act.wait_ge(S("xn7T_ps"), 1)
                C.copy(wT[:, :], flat(ps[:, 0:2, :])).then_inc(S("wT7"), 1)
                act.wait_ge(S("q1_ps"), 1)
                act.wait_ge(S("bq1s"), 1)
                C.activation(qs[:, :], flat(ps[:, 2:4, :]), ACT.Identity, bias=bq1s[:, 0:1], scale=SC1).then_inc(S("q1_sb"), 1)

            @block.vector
            def _(dve):
                w = lambda t: t[:, :, :]
                V.tensor_scalar(bq1s[:, :], bq1[:, :], SC1, None, ALU.mult).then_inc(S("bq1s"), 1)
                dve.wait_ge(S("out7_ps"), 1)
                dchain(V.tensor_tensor(w(yo), ps[:, 4:6, :].rearrange("p a (b d) -> p (a b) d", d=D), every_tile(b2r), ALU.add))
                dchain(V.scalar_tensor_tensor(flat(x_sb), flat(yo), gt[:, 2:3], flat(x_sb), ALU.mult, ALU.add))
                ln_stats(x_sb, S("ln_x2_var"))
                ln_apply(xn, x_sb, S("ln_x2_sd"), 1, S("xn7"))
                dve.wait_ge(S("q1_sb"), 1)
                dchain(V.tensor_reduce(qabs[:, :], qs[:, :], AX.X, ALU.max, apply_absolute_value=True))
                dchain(V.reduce_max(kabs1[:, :], kabs[:, :], AX.X))
                V.tensor_tensor(bound[:, :], qabs[:, :], kabs1[:, :], ALU.mult).then_inc(S("bound_ready"), 1)
                dchain(V.tensor_copy(ql[:, 0, :], qs[:, :]))
                dchain(V.tensor_tensor(qs[:, :], qs[:, :], ql[:, 0, :], ALU.subtract))
                dchain(V.tensor_copy(ql[:, 1, :], qs[:, :]))
                V.tensor_tensor(ql[:, 2, :], qs[:, :], ql[:, 1, :], ALU.subtract).then_inc(S("q1_split"), 1)
                dve.wait_ge(S("bound_ps"), 1)
                dchain(V.reduce_sum(boundh[:, :], ps[0:1, 6, 0:P].rearrange("p (h d) -> p h d", d=DH1), AX.X))
                dchain(V.reduce_max(bound1[:, :], boundh[:, :], AX.X))
                dchain(V.tensor_scalar(bound1[:, :], bound1[:, :], EXP_RANGE, None, ALU.is_gt))
                dchain(V.tensor_copy(general[0:1, 1:2], bound1[:, :]))

    l1_general = nc.values_load(general[0:1, 1:2], min_val=0, max_val=1)
    with nc.If(l1_general > 0):
        with ExitStack() as b7g:
            gmax = sb(b7g, "gmax", [P, 16])
            nshift = sb(b7g, "nshift", [P, H1 * NT])
            nsT = sb(b7g, "nsT", [P, P])
            nsR = sb(b7g, "nsR", [P, P])
            nsl = sb(b7g, "nsl", [P, LEVELS, P], BF16)
            NBK = -(-GP // 512)
            BANKS = 7
            HALF = H1 * NT // 2
            gchain = Chain(V, S("g1_chain"))
            with nc.Block() as block:
                @block.gpsimd
                def _(pool):
                    take_part(pool)

                @block.sync
                def _(sp):
                    sp.wait_ge(S("g1_scored"), HALF * NBK)
                    for quad in range(2, NQ):
                        load_quad(sp, quad, S("g1_late"), S("g1_late"))
                    sp.wait_ge(S("g1_scored"), 2 * HALF * NBK)
                    sp.wait_ge(S("g1_late"), 16 * 2 * (KIN + 1))
                    for quad in range(2):
                        load_quad(sp, quad, S("g1_again"), S("g1_again"))
                    sp.wait_ge(S("g1_again"), 16 * 2 * (KIN + 1))
                    sp.wait_ge(S("nsl_ready"), 1)
                    sp.dma_start(ns_lines.rearrange("l (i p) -> i l p", p=P), nsl[:, :, :]).then_inc(S("ns_out"), 16)
                    sp.wait_ge(S("ns_out"), 16)
                    for par in range(2):
                        r0 = 64 * par + ROW1
                        sp.dma_start(Q1v[r0:r0 + LEVELS, :, par, :],
                                     ns_lines.rearrange("l (j a t) -> l j a t", a=2, t=T)[:, :, par, :])\
                            .then_inc(S("ns_in"), 16)
                    sp.wait_ge(S("ns_in"), 32)

                @block.tensor
                def _(pe):
                    for half in range(2):
                        if half:
                            pe.wait_ge(S("g1_late"), 16 * 2 * (KIN + 1))
                        with pe.Fori(0, HALF) as i:
                            n = i + half * HALF
                            for j in range(NBK):
                                w = min(512, GP - j * 512)
                                used = j - BANKS if j >= BANKS else (j + BANKS - NBK if j + BANKS < NBK else j - NBK)
                                pe.wait_ge(S("g1_read"), n * NBK + (NBK + used + 1))
                                M.matmul(ps[:, j % BANKS, 0:w],
                                         Q1[:, :, :].rearrange("p h t -> p (h t)")[:, bass.ds(n * P, P)],
                                         K1[:, :, :, :].rearrange("p q j g -> p (q j g)")
                                         [:, bass.ds((i // (2 * NT)) * GP + j * 512, w)],
                                         start=True, stop=True).then_inc(S("g1_scored"), 1)
                    pe.wait_ge(S("nshift_ready"), 1)
                    M.transpose(ps[:, 7, 0:P], nshift[:, :], ident[:, :]).then_inc(S("nsT_ps"), 1)

                @block.scalar
                def _(act):
                    act.wait_ge(S("nsT_ps"), 1)
                    C.copy(nsT[:, :], ps[:, 7, 0:P]).then_inc(S("nsT_sb"), 1)

                @block.vector
                def _(dve):
                    dve.sem_inc(S("g1_read"), NBK)
                    with dve.Fori(0, H1 * NT) as i:
                        gchain.loop(i, 1)
                        for j in range(NBK):
                            w = min(512, GP - j * 512)
                            dve.wait_ge(S("g1_scored"), i * NBK + j + 1)
                            V.reduce_max(gmax[:, j:j + 1], ps[:, j % BANKS, 0:w], AX.X).then_inc(S("g1_read"), 1)
                        dve.wait_ge(S("g1_read"), i * NBK + NBK + NBK)
                        gchain(V.reduce_max(nshift[:, bass.ds(i, 1)], gmax[:, 0:NBK], AX.X))
                    gchain.looped(1, H1 * NT)
                    V.tensor_scalar(nshift[:, :], nshift[:, :], -1.0, None, ALU.mult).then_inc(S("nshift_ready"), 1)
                    dve.wait_ge(S("nsT_sb"), 1)
                    gchain(V.tensor_copy(nsl[:, 0, :], nsT[:, :]))
                    gchain(V.tensor_tensor(nsR[:, :], nsT[:, :], nsl[:, 0, :], ALU.subtract))
                    gchain(V.tensor_copy(nsl[:, 1, :], nsR[:, :]))
                    V.tensor_tensor(nsl[:, 2, :], nsR[:, :], nsl[:, 1, :], ALU.subtract).then_inc(S("nsl_ready"), 1)

    next_stage()

    with ExitStack() as b8:
        ex1 = sb(b8, "ex1", [P, 2 * UNROLL, 2, TB])
        UNITS = 2 * UNROLL
        RING = 3
        NPASS = NQ * NB
        with nc.Block() as block:
            @block.gpsimd
            def _(pool):
                for w in range(NPASS):
                    quad, tb = divmod(w, NB)
                    if quad >= 2:
                        pool.wait_ge(S(f"v1_in{quad % 2}"), 16 * (quad // 2))

                    def place(k, g, n, first):
                        if not first:
                            pool.wait_ge(S("summed1"), n - UNROLL + 1)
                        PL.tensor_copy(vs1[:, k, :, 0:VW].unsqueeze(1),
                                       V1[:, quad % 2, bass.ds(g, 1), :].rearrange("p c (h v) -> p c h v", v=VW))\
                            .then_inc(S("v1_placed"), 1)

                    for k in range(UNROLL):
                        place(k, k, w * NG + k, w == 0)
                    with pool.Fori(1, TURNS) as i:
                        for k in range(UNROLL):
                            place(k, i * UNROLL + k, i * UNROLL + (w * NG + k), False)

            @block.sync
            def _(sp):
                for quad in range(2, NQ):
                    sp.wait_ge(S("scored1"), (quad - 1) * NB * 2 * NG)
                    sp.wait_ge(S("v1_placed"), (quad - 1) * NB * NG)
                    load_quad(sp, quad, S(f"k1_in{quad % 2}"), S(f"v1_in{quad % 2}"))

            @block.tensor
            def _(pe):
                for w in range(NPASS):
                    quad, tb = divmod(w, NB)
                    U0, G0 = w * 2 * NG, w * NG
                    if quad >= 2:
                        pe.wait_ge(S(f"k1_in{quad % 2}"), 16 * KIN * (quad // 2))

                    def scores(k, g, free):
                        if free is not None:
                            pe.wait_ge(S("exped1"), free)
                        for hh in range(2):
                            last = M.matmul(ps[:, 2 * (k % RING) + hh, :], K1[:, quad % 2, k % 2, bass.ds(g * P, P)],
                                            Q1[:, 4 * quad + 2 * (k % 2) + hh, tb * TB:(tb + 1) * TB], start=True, stop=True)
                        last.then_inc(S("scored1"), 1)

                    def values(t, n, start, stop):
                        pe.wait_ge(S("exped1"), 2 * n + 2)
                        pe.wait_ge(S("v1_placed"), n + 1)
                        if start and w >= 2:
                            pe.wait_ge(S("o1_read"), w - 1)
                        for j in range(4):
                            last = M.matmul(ps[32 * j:32 * j + 32, 6 + w % 2, :], vs1[:, t, j, :],
                                            ex1[:, 2 * t + j // 2, j % 2, :], start=start, stop=stop,
                                            tile_position=(0, 32 * j))
                        last.then_inc(S("summed1"), 1)

                    def turn(i, first=False, last=False):
                        for t in range(UNROLL):
                            for q in range(2):
                                k = 2 * t + q
                                free = None if first and w == 0 and k < RING else i * UNITS + (U0 + k - RING + 1)
                                scores(k, i * UNROLL + t, free)
                            if not (first and t == 0):
                                n = i * UNROLL + (G0 + t - 1)
                                values((t - 1) % UNROLL, n, first and t == 1, False)
                        if last:
                            values(UNROLL - 1, i * UNROLL + (G0 + UNROLL - 1), False, True)

                    turn(0, first=True)
                    with pe.Fori(1, TURNS - 1) as i:
                        turn(i)
                    turn(TURNS - 1, last=True)

            @block.scalar
            def _(act):
                for w in range(NPASS):
                    U0, G0 = w * 2 * NG, w * NG

                    def unit(k, i, first):
                        act.wait_ge(S("scored1"), i * UNITS + (U0 + k + 1))
                        if not first:
                            act.wait_ge(S("summed1"), i * UNROLL + (G0 + k // 2 - UNROLL + 1))
                        C.activation(ex1[:, k, :, :], ps[:, 2 * (k % RING):2 * (k % RING) + 2, :], ACT.Exp)\
                            .then_inc(S("exped1"), 1)

                    for k in range(UNITS):
                        unit(k, 0, w == 0)
                    with act.Fori(1, TURNS) as i:
                        for k in range(UNITS):
                            unit(k, i, False)

            @block.vector
            def _(dve):
                for w in range(NPASS):
                    quad, tb = divmod(w, NB)
                    dve.wait_ge(S("summed1"), (w + 1) * NG)
                    V.tensor_copy(o1[:, quad, tb * TB:(tb + 1) * TB], ps[:, 6 + w % 2, :]).then_inc(S("o1_read"), 1)

    q1s.close()
    k1s.close()

    moe = ExitStack()
    gw = sb(moe, "gw", [P, E])
    gb = sb(moe, "gb", [P, E])
    w1 = sb(moe, "w1m", [P, E, HID])
    w2 = sb(moe, "w2m", [P, E, NF, D])
    b1c = sb(moe, "b1m", [P, E, NF])
    b2e = sb(moe, "b2m", [E, D])
    sel = sb(moe, "sel", [E, E, P])
    experts = sb(moe, "experts", [P, E])
    row10 = {n: sb(moe, "row10_" + n, [P, D]) for n in ("ln_g", "ln_b")}

    with ExitStack() as b9:
        wo = sb(b9, "wo", [P, D])
        bo = sb(b9, "bo", [P, D])
        rs = sb(b9, "rs", [P, NT, H1])
        on = sb(b9, "on", [P, NT, H1, DH1])
        onT = sb(b9, "onT", [P, T])
        yo = sb(b9, "yo9", [P, NT, D])
        with nc.Block() as block:
            @block.sync
            def _(sp):
                sp.dma_start(wo[:, :], A["L1_xattn_wo"]).then_inc(S("b9_in"), 16)
                sp.dma_start(bo[:, :], A["L1_xattn_bo"].partition_broadcast(P)).then_inc(S("b9_in"), 16)
                sp.dma_start(gw[:, :], A["L1_ffn_gate_w"]).then_inc(S("moe_in"), 16)
                sp.dma_start(gb[:, :], A["L1_ffn_gate_b"].partition_broadcast(P)).then_inc(S("moe_in"), 16)
                sp.dma_start(experts[:, :], A["steps"][0:E].partition_broadcast(P)).then_inc(S("moe_in"), 16)
                sp.dma_start(b2e[:, :], A["L1_ffn_b2"]).then_inc(S("moe_in"), 16)
                sp.dma_start(sel[:, :, :], A["select"]).then_inc(S("moe_in"), 16)
                for e in range(E):
                    sp.dma_start(b1c[:, e, :], A["L1_ffn_b1"][e].rearrange("(f p) -> p f", p=P),
                                 allow_slow_non_contiguous=True).then_inc(S("moe_in"), 16)
                for n, tile in row10.items():
                    sp.dma_start(tile[:, :], A["L1_ffn_" + n].partition_broadcast(P)).then_inc(S("moe_in"), 16)
                sp.dma_start(w1[:, :, :], A["L1_ffn_w1"].rearrange("e d f -> d e f")).then_inc(S("moe_in"), 16)
                sp.dma_start(w2[:, :, :, :].rearrange("p e f d -> p (e f) d"),
                             A["L1_ffn_w2"].rearrange("e (f p) d -> p (e f) d", p=P)).then_inc(S("moe_in"), 16)
                sp.wait_ge(S("moe_in"), 16 * (5 + E + 2 + 2))

            @block.tensor
            def _(pe):
                for t in range(NT):
                    for quad in range(NQ):
                        last = M.transpose(ps[:, t, quad * P:(quad + 1) * P], o1[:, quad, t * P:(t + 1) * P], ident[:, :])
                    last.then_inc(S("o1T_ps"), 1)
                pe.wait_ge(S("on_ready"), NT)
                for t in range(NT):
                    last = M.transpose(ps[:, t // 4, (t % 4) * P:(t % 4 + 1) * P],
                                       on[:, t, :, :].rearrange("p h v -> p (h v)"), ident[:, :])
                last.then_inc(S("onT_ps"), 1)
                pe.wait_ge(S("onT"), 1)
                pe.wait_ge(S("b9_in"), 32)
                for t in range(NT):
                    last = M.matmul(ps[:, 4 + t // 4, (t % 4) * P:(t % 4 + 1) * P], onT[:, t * P:(t + 1) * P], wo[:, :],
                                    start=True, stop=True)
                last.then_inc(S("out9_ps"), 1)
                pe.wait_ge(S("xn9"), NT)
                transpose_tiles(xn, 0, S("xn9T_ps"))

            @block.scalar
            def _(act):
                act.wait_ge(S("onT_ps"), 1)
                C.copy(onT[:, :], flat(ps[:, 0:2, :])).then_inc(S("onT"), 1)
                ln_sqrt(1, S("ln_x3_var"), S("ln_x3_sd"))
                act.wait_ge(S("xn9T_ps"), 1)
                C.copy(wT[:, :], flat(ps[:, 0:2, :])).then_inc(S("wT9"), 1)

            @block.vector
            def _(dve):
                for t in range(NT):
                    dve.wait_ge(S("o1T_ps"), t + 1)
                    rows_ = ps[:, t, :].rearrange("p (h v) -> p h v", v=32)
                    dchain(V.reciprocal(rs[:, t, :], rows_[:, :, DH1]))
                    V.tensor_tensor(on[:, t, :, :], rows_[:, :, 0:DH1],
                                    rs[:, t, :].unsqueeze(2).to_broadcast([P, H1, DH1]), ALU.mult).then_inc(S("on_ready"), 1)
                w = lambda t: t[:, :, :]
                dve.wait_ge(S("b9_in"), 32)
                dve.wait_ge(S("out9_ps"), 1)
                dchain(V.tensor_tensor(w(yo), ps[:, 4:6, :].rearrange("p a (b d) -> p (a b) d", d=D), every_tile(bo), ALU.add))
                dchain(V.scalar_tensor_tensor(flat(x_sb), flat(yo), gt[:, 1:2], flat(x_sb), ALU.mult, ALU.add))
                ln_stats(x_sb, S("ln_x3_var"))
                ln_apply(xn, x_sb, S("ln_x3_sd"), 1, S("xn9"))
    next_stage()

    with ExitStack() as b10:
        lg, lw = sb(b10, "lg", [P, NT, E]), sb(b10, "lw", [P, NT, E])
        t8 = sb(b10, "t8", [P, NT, 8])
        i8 = sb(b10, "i8", [P, NT, 8], U32)
        i8f = sb(b10, "i8f", [P, NT, 2])
        keep, keep2 = sb(b10, "keep", [P, NT, E]), sb(b10, "keep2", [P, NT, E])
        pr = sb(b10, "pr", [P, NT, E])
        psum_ = sb(b10, "psm", [P, NT])
        pT = sb(b10, "pT", [E, T])
        hid = sb(b10, "hidm", [P, 2, NF, TB])
        hidp = sb(b10, "hidp", [P, 2, NF, TB])
        oT = sb(b10, "oT", [P, T])
        oo = sb(b10, "oo", [P, NT, D])
        NJ = E * NB
        with nc.Block() as block:
            @block.sync
            def _(sp):
                sp.wait_ge(S("x4_ready"), 1)
                sp.dma_start(A["out"][0].rearrange("(n p) d -> p n d", p=P), x_sb[:, :, :]).then_inc(S("stored"), 16)
                sp.wait_ge(S("stored"), 16)

            @block.tensor
            def _(pe):
                for t in range(NT):
                    last = M.matmul(ps[:, 0, t * E:(t + 1) * E], wT[:, t * P:(t + 1) * P], gw[:, :], start=True, stop=True)
                last.then_inc(S("logits_ps"), 1)

                def hidden(j):
                    e, tb = divmod(j, NB)
                    for f in range(NF):
                        if j:
                            pe.wait_ge(S("hidm"), (j - 1) * NF + f + 1)
                        elif f == 0:
                            pe.wait_ge(S("logits_read"), 1)
                        M.matmul(ps[:, f, :], w1[:, e, f * P:(f + 1) * P], wT[:, tb * TB:(tb + 1) * TB],
                                 start=True, stop=True).then_inc(S("hidm_ps"), 1)

                def share(j):
                    e, tb = divmod(j, NB)
                    if j >= 2:
                        pe.wait_ge(S("hidp"), j - 1)
                    M.matmul(ps[:, 4 + j % 2, :], sel[:, e, :], pT[:, tb * TB:(tb + 1) * TB], start=True, stop=True)\
                        .then_inc(S("share_ps"), 1)

                hidden(0)
                pe.wait_ge(S("pr_ready"), 1)
                for t in range(NT):
                    last = M.transpose(ps[0:E, 4 + t // 4, (t % 4) * P:(t % 4 + 1) * P], pr[:, t, :], ident[:, :])
                last.then_inc(S("pT_ps"), 1)
                pe.wait_ge(S("pT_ready"), 1)
                share(0)
                for j in range(NJ):
                    e, tb = divmod(j, NB)
                    if j + 1 < NJ:
                        hidden(j + 1)
                        share(j + 1)
                    pe.wait_ge(S("hidp"), j + 1)
                    for f in range(NF):
                        M.matmul(ps[:, 6 + tb, :], w2[:, e, f, :], hidp[:, j % 2, f, :], start=e == 0 and f == 0, stop=False)\
                            .then_inc(S("outm"), 1)
                for tb in range(NB):
                    last = M.matmul(ps[:, 6 + tb, :], b2e[:, :], pT[:, tb * TB:(tb + 1) * TB], start=False, stop=True)
                last.then_inc(S("oT_ps"), 1)
                pe.wait_ge(S("oT"), 1)
                for t in range(NT):
                    last = M.transpose(ps[:, 4 + t // 4, (t % 4) * P:(t % 4 + 1) * P], oT[:, t * P:(t + 1) * P], ident[:, :])
                last.then_inc(S("oo_ps"), 1)

            @block.scalar
            def _(act):
                act.wait_ge(S("lw_ready"), 1)
                C.activation(pr[:, :, :], lw[:, :, :], ACT.Exp).then_inc(S("pr_exp"), 1)
                act.wait_ge(S("pT_ps"), 1)
                C.copy(pT[:, :], flat(ps[0:E, 4:6, :])).then_inc(S("pT_ready"), 1)
                for j in range(NJ):
                    e, tb = divmod(j, NB)
                    for f in range(NF):
                        act.wait_ge(S("hidm_ps"), j * NF + f + 1)
                        if j >= 2:
                            act.wait_ge(S("hidp"), j - 1)
                        C.activation(hid[:, j % 2, f, :], ps[:, f, :], ACT.Gelu, bias=b1c[:, e, f:f + 1]).then_inc(S("hidm"), 1)
                act.wait_ge(S("oT_ps"), 1)
                C.copy(oT[:, :], flat(ps[:, 6:8, :])).then_inc(S("oT"), 1)
                ln_sqrt(1, S("ln_m_var"), S("ln_m_sd"))

            @block.vector
            def _(dve):
                w = lambda t: t[:, :, :]
                over_e = lambda t: t.unsqueeze(2).to_broadcast([P, NT, E])
                dve.wait_ge(S("logits_ps"), 1)
                dchain(V.tensor_tensor(w(lg), ps[:, 0, 0:NT * E].rearrange("p (t e) -> p t e", e=E),
                                       gb[:, :].unsqueeze(1).to_broadcast([P, NT, E]), ALU.add))
                V.tensor_scalar(w(lg), w(lg), float(1 / 0.9), None, ALU.mult).then_inc(S("logits_read"), 1)
                dve.wait_ge(S("logits_read"), 1)
                for t in range(NT):
                    V.max(t8[:, t, :], lg[:, t, :]).then_inc(S("t8"), 1)
                dve.wait_ge(S("t8"), NT)
                V.tensor_tensor(w(lw), w(lg), over_e(t8[:, :, 0]), ALU.subtract).then_inc(S("lw_ready"), 1)
                for t in range(NT):
                    V.max_index(i8[:, t, :], t8[:, t, :], lg[:, t, :]).then_inc(S("i8"), 1)
                dve.wait_ge(S("i8"), NT)
                dchain(V.tensor_copy(w(i8f), i8[:, :, 0:2]))
                each = experts[:, :].unsqueeze(1).to_broadcast([P, NT, E])
                dchain(V.tensor_tensor(w(keep), each, over_e(i8f[:, :, 0]), ALU.is_equal))
                dchain(V.tensor_tensor(w(keep2), each, over_e(i8f[:, :, 1]), ALU.is_equal))
                dchain(V.tensor_tensor(w(keep), w(keep), w(keep2), ALU.add))
                dve.wait_ge(S("pr_exp"), 1)
                dchain(V.tensor_tensor(w(pr), w(pr), w(keep), ALU.mult))
                dchain(V.reduce_sum(psum_[:, :], w(pr), AX.X))
                dchain(V.reciprocal(psum_[:, :], psum_[:, :]))
                V.tensor_tensor(w(pr), w(pr), over_e(psum_[:, :]), ALU.mult).then_inc(S("pr_ready"), 1)
                for j in range(NJ):
                    dve.wait_ge(S("share_ps"), j + 1)
                    dve.wait_ge(S("hidm"), (j + 1) * NF)
                    if j >= 2:
                        dve.wait_ge(S("outm"), (j - 1) * NF)
                    V.tensor_tensor(hidp[:, j % 2, :, :], hid[:, j % 2, :, :],
                                    ps[:, 4 + j % 2, :].unsqueeze(1).to_broadcast([P, NF, TB]), ALU.mult).then_inc(S("hidp"), 1)
                dve.wait_ge(S("oo_ps"), 1)
                dchain(V.tensor_copy(w(oo), ps[:, 4:6, :].rearrange("p a (b d) -> p (a b) d", d=D)))
                ln_stats(oo, S("ln_m_var"))
                ln_apply(xn, oo, S("ln_m_sd"), 1, S("xn10"))
                dve.wait_ge(S("xn10"), NT)
                dchain(V.tensor_tensor(w(xn), w(xn), every_tile(row10["ln_g"]), ALU.mult))
                dchain(V.tensor_tensor(w(xn), w(xn), every_tile(row10["ln_b"]), ALU.add))
                V.scalar_tensor_tensor(flat(x_sb), flat(xn), gt[:, 3:4], flat(x_sb), ALU.mult, ALU.add).then_inc(S("x4_ready"), 1)

    next_stage()
    moe.close()
    oq.close()


def constants():
    n = 2 * P
    om = 2 * np.pi * (np.arange(P) + 0.5) / n
    j = np.arange(P)
    fx = np.exp(-1j * np.outer(j, om))
    fk1 = np.exp(-1j * np.outer(P - 1 + j, om))
    fk0 = np.exp(-1j * np.outer(j - 1, om))
    fk0[0] = 0
    inv = np.exp(1j * np.outer(om, P - 1 + j)) / P
    dft = np.stack([fx.real, fx.imag, fk0.real, fk0.imag, fk1.real, fk1.imag, inv.real, -inv.real, -inv.imag], axis=1)
    return {"ident": np.eye(P, dtype=np.float32), "steps": np.arange(KTAP, dtype=np.float32),
            "select": np.ascontiguousarray(np.repeat(np.eye(E, dtype=np.float32)[:, :, None], P, axis=2)),
            "dft": np.ascontiguousarray(dft.astype(np.float32))}


def kernel(**inputs):
    import concourse.bacc as _bacc
    from concourse.bass_utils import run_bass_kernel_spmd as _run

    nc = _bacc.Bacc("TRN2", target_bir_lowering=False, num_devices=1)
    arrays, args = {}, {}
    for name, a in list(inputs.items()) + list(constants().items()):
        a = np.ascontiguousarray(a)
        if a.dtype.kind == "b":
            a = a.view(np.uint8)
        if a.ndim == 0:
            a = a.reshape(1)
        arrays[f"in_{name}"] = a
        args[name] = nc.dram_tensor(f"in_{name}", a.shape, mybir.dt.from_np(a.dtype), kind="ExternalInput").ap()
    args["out"] = nc.dram_tensor("out", (1, T, D), F32, kind="ExternalOutput").ap()
    build(nc, args)
    r = _run(nc, [arrays], core_ids=[0])
    return r.results[0]["out"]
```
